# Optimizing a Trainium2 kernel written in Bass

```python
import numpy as np
import jax
import jax.numpy as jnp

def _softmax(x, axis=-1):
    return jax.nn.softmax(x, axis=axis)

def _gelu(x):
    return jax.nn.gelu(x, approximate=True)

def _silu(x):
    return jax.nn.silu(x)

def _sigmoid(x):
    return jax.nn.sigmoid(x)

def _layernorm(x, axis=-1, eps=1e-05):
    m = jnp.mean(x, axis=axis, keepdims=True)
    v = jnp.var(x, axis=axis, keepdims=True)
    return (x - m) / jnp.sqrt(v + eps)

def _scatter_add(tgt, idx, src, axis=0):
    return tgt.at[idx].add(src)

def _segment_sum(src, seg, n):
    return jax.ops.segment_sum(src, seg, n)
kernel_name = 'mk_audio_tower_d1_tok_audfeat768_r4_3a6cb4'

def setup_inputs(seed: int=0):
    np.random.seed(seed)
    _w = jnp.asarray

    def _rec_inputs():
        import jax
        import jax.numpy as jnp
        _rk = jax.random.key(seed)
        x = -0.000222058 + 0.999998 * jax.random.normal(jax.random.fold_in(_rk, 1), (8, 750, 192), jnp.float32)
        return x
    x = _rec_inputs()

    def _L0_tok_setup():
        import jax, jax.numpy as jnp
        import numpy as np
        B, S, D, K = (8, 1024, 192, 7)
        EPS = 1e-05
        key = jax.random.key(seed)
        k0, k1, k2, k3, k4 = jax.random.split(key, 5)
        return {'x': jax.random.normal(k0, (B, S, D), jnp.float32), 'w_dw': jax.random.normal(k1, (D, 1, K), jnp.float32) * 0.2, 'b_dw': jax.random.normal(k2, (D,), jnp.float32) * 0.02, 'w_pw': jax.random.normal(k3, (D, D, 1), jnp.float32) * 0.03, 'b_pw': jax.random.normal(k4, (D,), jnp.float32) * 0.02, 'gamma': jnp.ones((D,), jnp.float32), 'beta': jnp.zeros((D,), jnp.float32)}
    _L0_tok_all = _L0_tok_setup()
    _L0_tok_in = {k: v for k, v in _L0_tok_all.items() if k in ('w_dw', 'b_dw', 'w_pw', 'b_pw', 'gamma', 'beta')}
    del _L0_tok_all

    def _L0_attn_setup():
        import jax, jax.numpy as jnp
        import numpy as np
        B, N, E, H = (2, 512, 192, 12)
        D = E // H
        G = 16
        LN_EPS = 1e-05

        def _layernorm(x, w, b):
            mu = jnp.mean(x, axis=-1, keepdims=True)
            var = jnp.mean(jnp.square(x - mu), axis=-1, keepdims=True)
            return (x - mu) * jax.lax.rsqrt(var + LN_EPS) * w + b
        key = jax.random.key(seed)
        ks = jax.random.split(key, 8)
        s = E ** (-0.5)
        x = jax.random.normal(ks[0], (B, N, E), jnp.float32)
        log_slope = -2.0 ** (-8.0 * (jnp.arange(H, dtype=jnp.float32) + 1.0) / H)
        Wq = jax.random.normal(ks[1], (E, E), jnp.float32) * s
        Wk = jax.random.normal(ks[2], (E, E), jnp.float32) * s
        Wv = jax.random.normal(ks[3], (E, E), jnp.float32) * s
        Wo = jax.random.normal(ks[4], (E, E), jnp.float32) * s
        Wg1 = jax.random.normal(ks[5], (E, G), jnp.float32) * s
        Wg2 = jax.random.normal(ks[6], (G, E), jnp.float32) * G ** (-0.5)
        ln_w = jnp.ones((E,), jnp.float32)
        ln_b = jnp.zeros((E,), jnp.float32)
        return {'x': x, 'log_slope': log_slope, 'Wq': Wq, 'Wk': Wk, 'Wv': Wv, 'Wo': Wo, 'Wg1': Wg1, 'Wg2': Wg2, 'ln_w': ln_w, 'ln_b': ln_b}
    _L0_attn_all = _L0_attn_setup()
    _L0_attn_in = {k: v for k, v in _L0_attn_all.items() if k in ('log_slope', 'Wq', 'Wk', 'Wv', 'Wo', 'Wg1', 'Wg2', 'ln_w', 'ln_b')}
    del _L0_attn_all

    def _L0_ffn_setup():
        import jax, jax.numpy as jnp
        import numpy as np
        TOP_K = 2

        def _moe(x, Wg, bg, W1, b1, W2, b2):
            B, S, D = x.shape
            E = Wg.shape[1]
            logits = x @ Wg + bg
            top_vals, top_idx = jax.lax.top_k(logits, TOP_K)
            gates_k = jax.nn.softmax(top_vals, axis=-1)
            one_hot = jax.nn.one_hot(top_idx, E, dtype=x.dtype)
            gates = jnp.sum(one_hot * gates_k[..., None], axis=-2)
            flat_x = x.reshape(-1, D)
            flat_g = gates.reshape(-1, E).T

            def body(acc, p):
                W1e, b1e, W2e, b2e, ge = p
                h = jax.nn.relu(flat_x @ W1e + b1e)
                acc = acc + (h @ W2e + b2e) * ge[:, None]
                return (acc, None)
            out, _ = jax.lax.scan(body, jnp.zeros_like(flat_x), (W1, b1, W2, b2, flat_g))
            return out.reshape(B, S, D)
        key = jax.random.key(seed)
        k = jax.random.split(key, 5)
        B, S, D, E, H = (8, 512, 192, 8, 768)
        init = lambda kk, shape: jax.random.normal(kk, shape, jnp.float32) * 0.02
        return {'x': jax.random.normal(k[0], (B, S, D), jnp.float32), 'Wg': init(k[1], (D, E)), 'bg': jnp.zeros((E,), jnp.float32), 'W1': init(k[2], (E, D, H)), 'b1': jnp.zeros((E, H), jnp.float32), 'W2': init(k[3], (E, H, D)), 'b2': jnp.zeros((E, D), jnp.float32)}
    _L0_ffn_all = _L0_ffn_setup()
    _L0_ffn_in = {k: v for k, v in _L0_ffn_all.items() if k in ('Wg', 'bg', 'W1', 'b1', 'W2', 'b2')}
    del _L0_ffn_all
    return {'x': x, 'L0_tok_w_dw': _L0_tok_in['w_dw'], 'L0_tok_b_dw': _L0_tok_in['b_dw'], 'L0_tok_w_pw': _L0_tok_in['w_pw'], 'L0_tok_b_pw': _L0_tok_in['b_pw'], 'L0_tok_gamma': _L0_tok_in['gamma'], 'L0_tok_beta': _L0_tok_in['beta'], 'L0_attn_log_slope': _L0_attn_in['log_slope'], 'L0_attn_Wq': _L0_attn_in['Wq'], 'L0_attn_Wk': _L0_attn_in['Wk'], 'L0_attn_Wv': _L0_attn_in['Wv'], 'L0_attn_Wo': _L0_attn_in['Wo'], 'L0_attn_Wg1': _L0_attn_in['Wg1'], 'L0_attn_Wg2': _L0_attn_in['Wg2'], 'L0_attn_ln_w': _L0_attn_in['ln_w'], 'L0_attn_ln_b': _L0_attn_in['ln_b'], 'L0_ffn_Wg': _L0_ffn_in['Wg'], 'L0_ffn_bg': _L0_ffn_in['bg'], 'L0_ffn_W1': _L0_ffn_in['W1'], 'L0_ffn_b1': _L0_ffn_in['b1'], 'L0_ffn_W2': _L0_ffn_in['W2'], 'L0_ffn_b2': _L0_ffn_in['b2']}

def reference(x, L0_tok_w_dw, L0_tok_b_dw, L0_tok_w_pw, L0_tok_b_pw, L0_tok_gamma, L0_tok_beta, L0_attn_log_slope, L0_attn_Wq, L0_attn_Wk, L0_attn_Wv, L0_attn_Wo, L0_attn_Wg1, L0_attn_Wg2, L0_attn_ln_w, L0_attn_ln_b, L0_ffn_Wg, L0_ffn_bg, L0_ffn_W1, L0_ffn_b1, L0_ffn_W2, L0_ffn_b2):
    import jax
    import jax.numpy as jnp

    def _L0_tok_ref(x, w_dw, b_dw, w_pw, b_pw, gamma, beta):
        import jax, jax.numpy as jnp
        import numpy as np
        B, S, D, K = (8, 1024, 192, 7)
        EPS = 1e-05
        d = w_dw.shape[0]
        h = jnp.transpose(x, (0, 2, 1))
        h = jax.lax.conv_general_dilated(h, w_dw, window_strides=(1,), padding='SAME', dimension_numbers=('NCH', 'OIH', 'NCH'), feature_group_count=d) + b_dw[None, :, None]
        h = jnp.einsum('od,bds->bos', w_pw[:, :, 0], h) + b_pw[None, :, None]
        h = jax.nn.relu(h)
        h = jax.lax.reduce_window(h, -jnp.inf, jax.lax.max, (1, 1, 2), (1, 1, 2), 'VALID')
        h = jnp.transpose(h, (0, 2, 1))
        y = jnp.real(jnp.fft.fft2(h))
        mu = jnp.mean(y, axis=-1, keepdims=True)
        var = jnp.var(y, axis=-1, keepdims=True)
        return (y - mu) * jax.lax.rsqrt(var + EPS) * gamma + beta

    def _L0_attn_ref(x, log_slope, Wq, Wk, Wv, Wo, Wg1, Wg2, ln_w, ln_b):
        import jax, jax.numpy as jnp
        import numpy as np
        B, N, E, H = (2, 512, 192, 12)
        D = E // H
        G = 16
        LN_EPS = 1e-05

        def _layernorm(x, w, b):
            mu = jnp.mean(x, axis=-1, keepdims=True)
            var = jnp.mean(jnp.square(x - mu), axis=-1, keepdims=True)
            return (x - mu) * jax.lax.rsqrt(var + LN_EPS) * w + b
        b, n, e = x.shape
        h = log_slope.shape[0]
        d = e // h
        silu = jax.nn.silu
        q = silu(x @ Wq).reshape(b, n, h, d).transpose(0, 2, 1, 3)
        k = silu(x @ Wk).reshape(b, n, h, d).transpose(0, 2, 1, 3)
        v = silu(x @ Wv).reshape(b, n, h, d).transpose(0, 2, 1, 3)
        idx = jnp.arange(n, dtype=jnp.float32)
        diff = idx[:, None] - idx[None, :]
        keep = diff >= 0
        decay = jnp.where(keep, jnp.exp(log_slope[:, None, None] * jnp.maximum(diff, 0.0)), 0.0)
        energy = jnp.einsum('bhnd,bhmd->bhnm', q, k) * decay
        out = jnp.einsum('bhnm,bhmd->bhnd', energy, v)
        out = out.transpose(0, 2, 1, 3).reshape(b, n, e)
        gate = jax.nn.sigmoid(x @ Wg1 @ Wg2)
        out = out * gate
        out = out @ Wo
        out = _layernorm(out, ln_w, ln_b)
        return out

    def _L0_ffn_ref(x, Wg, bg, W1, b1, W2, b2):
        import jax, jax.numpy as jnp
        import numpy as np
        TOP_K = 2

        def _moe(x, Wg, bg, W1, b1, W2, b2):
            B, S, D = x.shape
            E = Wg.shape[1]
            logits = x @ Wg + bg
            top_vals, top_idx = jax.lax.top_k(logits, TOP_K)
            gates_k = jax.nn.softmax(top_vals, axis=-1)
            one_hot = jax.nn.one_hot(top_idx, E, dtype=x.dtype)
            gates = jnp.sum(one_hot * gates_k[..., None], axis=-2)
            flat_x = x.reshape(-1, D)
            flat_g = gates.reshape(-1, E).T

            def body(acc, p):
                W1e, b1e, W2e, b2e, ge = p
                h = jax.nn.relu(flat_x @ W1e + b1e)
                acc = acc + (h @ W2e + b2e) * ge[:, None]
                return (acc, None)
            out, _ = jax.lax.scan(body, jnp.zeros_like(flat_x), (W1, b1, W2, b2, flat_g))
            return out.reshape(B, S, D)
        return _moe(x, Wg, bg, W1, b1, W2, b2)
    h = _L0_tok_ref(x, L0_tok_w_dw, L0_tok_b_dw, L0_tok_w_pw, L0_tok_b_pw, L0_tok_gamma, L0_tok_beta)
    h = h + _L0_attn_ref(_layernorm(h, axis=-1), L0_attn_log_slope, L0_attn_Wq, L0_attn_Wk, L0_attn_Wv, L0_attn_Wo, L0_attn_Wg1, L0_attn_Wg2, L0_attn_ln_w, L0_attn_ln_b)
    h = h + _L0_ffn_ref(_layernorm(h, axis=-1), L0_ffn_Wg, L0_ffn_bg, L0_ffn_W1, L0_ffn_b1, L0_ffn_W2, L0_ffn_b2)
    return h

_drawn_inputs = setup_inputs


def setup_inputs(seed=0):
    import zlib

    import numpy as np

    out = dict(_drawn_inputs(seed))
    spreads = {'L0_tok_gamma': (1.0, 0.2),
     'L0_tok_beta': (0.0, 0.1),
     'L0_attn_ln_w': (1.0, 0.2),
     'L0_attn_ln_b': (0.0, 0.1),
     'L0_ffn_bg': (0.0, 0.1),
     'L0_ffn_b1': (0.0, 0.444),
     'L0_ffn_b2': (0.0, 0.1)}
    factors = {}
    for name, (base, spread) in spreads.items():
        noise = np.random.default_rng([zlib.crc32(name.encode()), seed]).standard_normal(out[name].shape)
        drawn = base * np.exp(spread * noise) if base else spread * noise
        out[name] = jnp.asarray(drawn.astype(out[name].dtype))
    for name, factor in factors.items():
        out[name] = (out[name] * factor).astype(out[name].dtype)
    return out
```

```python
import numpy as np
import concourse.bass as bass
from concourse import mybir
from contextlib import ExitStack

B, S_IN, D, K = 8, 750, 192, 7
S = S_IN // 2
CH = 125
NC_ = S // CH
XT = S_IN // CH
HD = D // 2
NH, DH = 12, 16
HH = NH // 2
HG = 3
PH = 32
NG = 3
G = 16
NP, NQ = D // 2 + 1, D // 2 - 1
E, F = 8, 768
FC = F // 128
NT = B * NC_
TOK = B * S
REGION = 128 * (-(-(TOK + 127) // 128))
ROW = D + 2
MAXTILES = (2 * TOK + 127 * E) // 128
EMPTY = E * REGION
SKIP = 1.0e6
EPS = 1e-5
PAD = K // 2
POOL_CUT = (188, 187)


def channel_order():
    return np.array(list(range(NP)) + [D - c for c in range(1, NQ + 1)])


class Event:

    def __init__(self, sem, per=1):
        self.sem, self.per = sem, per

    def count(self, b, k=None):
        return b * self.per + (self.per if k is None else k + 1)


def begun(b):
    return not (isinstance(b, int) and b < 0)


class Own:

    def __init__(self, sem, per):
        self.sem, self.per = sem, per

    def begin(self, b):
        self.base, self.n = b * self.per, 0

    def after(self, steps):
        self.n += steps
        return self.base + self.n

    def end(self):
        assert self.n == self.per, (self.n, self.per)


def build(nc, a, out):
    f32, i32 = mybir.dt.float32, mybir.dt.int32
    ALU, ACT, AX = mybir.AluOpType, mybir.ActivationFunctionType, mybir.AxisListType
    ds = bass.ds
    ctx = ExitStack()
    with ctx:
        def sb(name, shape, dt=f32):
            return ctx.enter_context(nc.sbuf_tensor(name, shape, dt))

        def event(name, per=1):
            return Event(ctx.enter_context(nc.semaphore(name)), per)

        def own(name, per):
            return Own(ctx.enter_context(nc.semaphore(name)), per)

        ident = sb("ident", [128, 128])
        dft_c = sb("dft_c", [HD, 2, D])
        cos_s = sb("cos_s", [CH, NC_, S])
        sin_s = sb("sin_s", [CH, NC_, S])
        w_dw = sb("w_dw", [HD, 2, K])
        b_dw = sb("b_dw", [HD, 2])
        w_pw = sb("w_pw", [HD, 2, D])
        b_pw = sb("b_pw", [HD, 2])
        rows = sb("rows", [CH, 4, D])
        w_q = sb("w_q", [HD, 2, D])
        w_k = sb("w_k", [HD, 2, D])
        w_vk = sb("w_vk", [HD, 2, 2 * D])
        w_g1 = sb("w_g1", [HD, 2, G])
        w_g2 = sb("w_g2", [G, NH, PH])
        w_o = sb("w_o", [128, NG, D])
        w_r = sb("w_r", [HD, 2, E])
        small = sb("small", [CH, 3, NC_, E])
        slope_t = sb("slope_t", [CH, NH])
        slope_c = sb("slope_c", [HD, 2])
        to_end = sb("to_end", [CH, 1])
        pos = sb("pos", [HD, CH])
        tri = sb("tri", [CH, CH])
        head_mask = sb("head_mask", [HD, HH, PH])
        tok2 = sb("tok2", [CH, NT])
        jcol = sb("jcol", [128, MAXTILES])
        ones = sb("ones", [128, 128])
        idle = sb("idle", [1, 3])
        eps = sb("eps", [CH, NC_])
        half_neg = sb("half_neg", [CH, NC_])
        diff_keep = sb("diff_keep", [CH, 2, CH])
        decay = sb("decay", [CH, NH, CH])
        k_decay = sb("k_decay", [CH, NH, DH])
        q_decay = sb("q_decay", [HD, 2, CH])
        carry = sb("carry", [HD, 2])
        fill = sb("fill", [128, ROW])
        w2 = sb("w2", [128, E, FC, D])

        x_rows = sb("x_rows", [CH, XT, D])
        xT = sb("xT", [HD, 2, S_IN + 2 * PAD])
        area = [sb(f"area_{p}", [128, 2 * F]) for p in range(2)]
        conv, pw = [t[0:HD, 0:2 * S_IN].rearrange("p (h s) -> p h s", h=2) for t in area]
        wide = sb("wide", [128, 2 * HH * S])
        pooled = sb("pooled", [HD, 2, S])
        chan = sb("chan", [CH, NC_, D])
        sine = sb("sine", [CH, NC_, NQ])
        y = sb("y", [CH, NC_, D])
        h1 = sb("h1", [CH, NC_, D])
        xn = sb("xn", [CH, NC_, D])
        stats = sb("stats", [CH, 4, NC_, 6])
        mv = sb("mv", [CH, 4, NC_, 2])
        vp = sb("vp", [CH, 4, NC_])
        rstd = sb("rstd", [CH, 4, NC_])
        xnT = sb("xnT", [HD, 2, S])
        qT = sb("qT", [HD, 2, S])
        kT = sb("kT", [HD, 2, S])
        q_block = wide[0:HD, :].rearrange("p (u h s) -> p u h s", u=2, h=HH)
        q_dec = sb("q_dec", [HD, 2, S - CH])
        v_pad = sb("v_pad", [CH, NC_, NH, PH])
        k_tok = sb("k_tok", [CH, NC_ - 1, D])
        k_dec = sb("k_dec", [CH, NC_ - 1, D])
        g1 = sb("g1", [G, S])
        gate = sb("gate", [128, NG, S])
        deep = sb("deep", [128, NC_ * NH * CH])
        scores = deep[0:CH, :].rearrange("p (c h n) -> p c h n", c=NC_, h=NH)
        state = sb("state", [HD, NC_ - 1, 2, HH * PH])
        gated = sb("gated", [128, NG, S])
        resid = sb("resid", [CH, NT, D])
        o_ln = sb("o_ln", [CH, NC_, D])
        x2 = sb("x2", [CH, NC_, ROW])
        x2T = sb("x2T", [HD, 2, S])
        logit = sb("logit", [CH, NC_, E])
        logit2 = sb("logit2", [CH, NC_, E])
        hit = sb("hit", [CH, NC_, E])
        top = sb("top", [CH, 4, NC_])
        pick = sb("pick", [CH, 2, NC_, E])
        picked = sb("picked", [CH, NC_, E])
        row_of = sb("row_of", [CH, NC_, E])
        row_hit = sb("row_hit", [CH, 2, NC_, E])
        slots_f = sb("slots_f", [CH, 2, NC_])
        slots = sb("slots", [CH, 2, NC_], i32)
        counts = sb("counts", [CH, E])
        tile_sum = sb("tile_sum", [CH, E])
        gap = sb("gap", [CH, NT])
        n_f = sb("n_f", [128, E])
        n_i = sb("n_i", [128, 2, E], i32)
        nt_f = sb("nt_f", [128, E])
        end_f = sb("end_f", [128, E])
        cut = [0]

        def from_wide(n):
            cut[0] += n
            return wide[:, cut[0] - n:cut[0]]

        past, past_n = [from_wide(MAXTILES * E).rearrange("p (j e) -> p j e", e=E) for _ in range(2)]
        e_of = sb("e_of", [128, MAXTILES])
        first = sb("first", [128, MAXTILES])
        blk = sb("blk", [128, 3, MAXTILES])
        table = sb("table", [1, 2, MAXTILES], i32)
        fill_at = sb("fill_at", [1, E], i32)
        w1 = [t[0:HD + 1, :].rearrange("p (h f) -> p h f", h=2) for t in area]
        PAIR = 2 * NC_ * D
        at = 2 * PAIR
        b2_rows = deep[:, at:at + E * D].rearrange("p (e d) -> p e d", e=E)
        at += E * D
        xr = [deep[:, at + ROW * p:at + ROW * (p + 1)] for p in range(2)]
        pairs = [deep[0:CH, PAIR * p:PAIR * (p + 1)].rearrange("p (t e) -> p t e", t=NC_) for p in range(2)]
        xrT = [from_wide(256)[0:HD + 1].rearrange("p (h t) -> p h t", h=2) for _ in range(2)]
        hid = [from_wide(FC * 128).rearrange("p (c t) -> p c t", c=FC) for _ in range(2)]
        yo = [from_wide(D) for _ in range(2)]
        dest_f = sb("dest_f", [128, MAXTILES])
        dest = [sb(f"dest_{p}", [128, 1], i32) for p in range(2)]
        gates = sb("gates", [CH, 3, NT])

        ps = [ctx.enter_context(nc.psum_tensor(f"ps{i}", [128, 512], f32)) for i in range(8)]

        routed = nc.dram_tensor("routed", [EMPTY + 128, ROW], f32, kind="Internal").ap()
        by_pair = nc.dram_tensor("by_pair", [2 * TOK, D], f32, kind="Internal").ap()

        const_in = event("const_in")
        w2_in = event("w2_in", 16)
        b2_in = event("b2_in", 16)
        empty_in = event("empty_in", 16)
        x_in = event("x_in", 16)
        zeroed = event("zeroed")
        zeroed_d = event("zeroed_d")
        tables = event("tables")
        tables_d = event("tables_d")
        xT_ps = event("xT_ps", 4)
        xT_sb = event("xT_sb", 4)
        conv_sb = event("conv_sb", 2)
        pw_ps = event("pw_ps", 4)
        pw_sb = event("pw_sb", 4)
        pooled_sb = event("pooled_sb", 2)
        chan_ps = event("chan_ps", 2)
        chan_sb = event("chan_sb", 2)
        sine_ps = event("sine_ps")
        sine_sb = event("sine_sb")
        cosine_ps = event("cosine_ps")
        y_sb = event("y_sb")
        var_sb = event("var_sb", 2)
        rstd_sb = event("rstd_sb", 2)
        h1_sb = event("h1_sb")
        xn_sb = event("xn_sb")
        hb_sb = event("hb_sb")
        xnT_ps = event("xnT_ps", 2)
        xnT_sb = event("xnT_sb", 2)
        q_ps = event("q_ps", 2)
        q_sb = event("q_sb", 2)
        k_ps = event("k_ps", 2)
        k_sb = event("k_sb", 2)
        vk_ps = event("vk_ps", NC_)
        vk_sb = event("vk_sb", NC_)
        g1_ps = event("g1_ps")
        g1_sb = event("g1_sb")
        g2_ps = event("g2_ps", NG)
        g2_sb = event("g2_sb", NG)
        qb_in = event("qb_in", 16 * NH)
        k_dec_sb = event("k_dec_sb")
        q_dec_sb = event("q_dec_sb")
        sc_ps = event("sc_ps", 4 * NC_)
        sc_sb = event("sc_sb", 4 * NC_)
        st_ps = event("st_ps", 2)
        st_sb = event("st_sb", 2)
        av_ps = event("av_ps", NC_)
        av_sb = event("av_sb", NC_)
        o_ps = event("o_ps", 2)
        o_free = event("o_free", NC_)
        cvar_sb = event("cvar_sb", 2)
        crstd_sb = event("crstd_sb", 2)
        x2_sb = event("x2_sb")
        x2T_ps = event("x2T_ps", 2)
        x2T_sb = event("x2T_sb", 2)
        lg_ps = event("lg_ps")
        lg_sb = event("lg_sb")
        pick_sb = event("pick_sb")
        rank_ps = event("rank_ps")
        rank_sb = event("rank_sb")
        slots_sb = event("slots_sb")
        counts_sb = event("counts_sb")
        scattered = event("scattered", 16 * 2 * NC_)
        own_conv = own("own_conv", 2 * (K - 1))
        own_ln = own("own_ln", 3)
        own_c = own("own_c", 18)
        own_st = own("own_st", 1)
        own_pa = own("own_pa", 2)
        own_pc = own("own_pc", 2)
        n_ps = event("n_ps")
        own_t = own("own_t", 16)
        table_sb = event("table_sb")
        filled = event("filled")
        row_in = [event(f"row_in{p}", 16) for p in range(2)]
        w1_in = [event(f"w1_in{p}", 32) for p in range(2)]
        dest_sb = event("dest_sb")
        xrT_ps = event("xrT_ps")
        xrT_sb = event("xrT_sb")
        hid_ps = event("hid_ps", 2)
        hid_a = event("hid_a")
        hid_b = event("hid_b")
        out_ps = event("out_ps")
        out_sb = event("out_sb")
        sent = [event(f"sent{p}", 16) for p in range(2)]
        idled = event("idled")
        exp_sb = event("exp_sb")
        own_g = own("own_g", 2)
        pair_in = [event(f"pair_in{p}", 16) for p in range(2)]
        mixed = event("mixed")
        own_m = own("own_m", 1)
        out_done = event("out_done", 16)

        block = ctx.enter_context(nc.Block())

        def apart(eng):
            if eng is nc.gpsimd:
                return nc.gpsimd.tensor_tensor(idle[0:1, 0:1], idle[0:1, 1:2], idle[0:1, 1:2], ALU.add)
            return nc.vector.memset(idle[0:1, 2:3], 0.0)

        RING_A = [(xT_sb, k) for k in range(4)] + [(pw_sb, k) for k in range(4)] + \
                 [(chan_sb, 0), (chan_sb, 1), (sine_sb, 0), (y_sb, 0)]
        RING_B = [(xnT_sb, 0), (xnT_sb, 1), (q_sb, 0), (q_sb, 1), (k_sb, 0), (k_sb, 1)] + \
                 [(vk_sb, k) for k in range(NC_)] + [(g1_sb, 0)] + [(g2_sb, k) for k in range(NG)] + \
                 [(sc_sb, k) for k in range(4 * NC_)] + [(st_sb, 0), (st_sb, 1)]
        RING_C = [(av_sb, k) for k in range(NC_)] + [(o_free, 1), (o_free, 2), (x2T_sb, 0), (x2T_sb, 1),
                                                     (lg_sb, 0), (rank_sb, 0)]
        RINGS = {"A": (RING_A, [0, 1]), "B": (RING_B, [2, 3, 4]), "C": (RING_C, [5, 6, 7])}
        AT = {"xT": 0, "pw": 4, "chan": 8, "sine": 10, "cosine": 11,
              "xnT": 0, "q": 2, "k": 4, "vk": 6, "g1": 9, "g2": 10, "sc": 13, "st": 25,
              "av": 0, "o": 3, "x2T": 5, "lg": 7, "rank": 8}
        assert all(len(r) % len(banks) == 0 for r, banks in RINGS.values())

        def bank(ring, group):
            return ps[RINGS[ring][1][group % len(RINGS[ring][1])]]

        def shared(ring, group, b):
            return group >= len(RINGS[ring][1]) or begun(b - 1)

        def drained(ring, group, b):
            groups, banks = RINGS[ring]
            before = group - len(banks)
            event_, k = groups[before]
            return event_.sem, event_.count(b if before >= 0 else b - 1, k)

        def pipeline(eng, run):
            run(0, None, None)
            run(1, 0, None)
            run(2, 1, 0)
            with eng.Fori(2, B - 1) as b:
                run(b + 1, b, b - 1)
            run(None, B - 1, B - 2)
            run(None, None, B - 1)

        def tiles(eng, run):
            for j in range(4):
                run(j, j % 2, j // 2)
            with eng.Fori(2, MAXTILES // 2 - 1) as jj:
                for p in range(2):
                    run(jj * 2 + p, p, jj)
            for j in range(MAXTILES - 2, MAXTILES):
                run(j, j % 2, j // 2)

        consts = [
            (ident, a["ident"]), (dft_c, a["dft_c"]), (cos_s, a["cos_s"]), (sin_s, a["sin_s"]),
            (w_dw, a["w_dw"]), (b_dw, a["b_dw"]), (w_pw, a["w_pw"]), (b_pw, a["b_pw"]),
            (rows, a["rows"].partition_broadcast(CH)),
            (w_q, a["w_q"]), (w_k, a["w_k"]), (w_vk, a["w_vk"]), (w_g1, a["w_g1"]), (w_r, a["w_r"]),
            (small[:, 1:3], a["small"].partition_broadcast(CH)),
            (slope_t, a["slope"].partition_broadcast(CH)), (slope_c, a["slope_c"]),
            (to_end, a["to_end"]), (pos, a["pos"].partition_broadcast(HD)), (tri, a["tri"]),
            (head_mask, a["head_mask"]), (tok2, a["tok2"]),
            (jcol, a["jcol"].partition_broadcast(128)),
        ] + [(small[:, 0, i], a["bg"].partition_broadcast(CH)) for i in range(NC_)]
        def full(t):
            return t[tuple(slice(None) for _ in t.shape)]

        padded = [(w_g2[:, :, 0:DH], a["w_g2"])] + \
                 [(w_o[PH * j:PH * j + DH], a["w_o"][j]) for j in range(4)]
        N_CONST = 16 * (len(consts) + len(padded))

        @block.sync
        def _(sp):
            def load_x(b):
                if begun(b - 1):
                    sp.wait_ge(xT_ps.sem, xT_ps.count(b - 1))
                sp.dma_start(x_rows[:, :, :], a["x"][ds(b, 1)].rearrange("o (t p) d -> p (o t) d", p=CH)
                             ).then_inc(x_in.sem, 16)

            load_x(0)
            for dst, src in consts:
                sp.dma_start(full(dst), src).then_inc(const_in.sem, 16)
            sp.wait_ge(zeroed.sem, zeroed.count(0))
            for dst, src in padded:
                sp.dma_start(dst, src).then_inc(const_in.sem, 16)

            def run(a_, b, c):
                if a_ is not None and not (isinstance(a_, int) and a_ == 0):
                    load_x(a_)
                if b is not None:
                    if begun(b - 1):
                        sp.wait_ge(sc_ps.sem, sc_ps.count(b - 1))
                    for h in range(NH):
                        half, hl = divmod(h, HH)
                        if hl == 0:
                            sp.wait_ge(q_sb.sem, q_sb.count(b, half))
                        sp.dma_start(q_block[DH * hl:DH * hl + DH, half, hl, :],
                                     qT[DH * hl:DH * hl + DH, half, :]).then_inc(qb_in.sem, 16)

            pipeline(sp, run)

            sp.wait_ge(table_sb.sem, table_sb.count(0))
            sp.dma_start(b2_rows, a["b2"].partition_broadcast(128)).then_inc(b2_in.sem, 16)
            sp.wait_ge(scattered.sem, scattered.count(B - 1))
            for e in range(E):
                at = sp.value_load(fill_at[0:1, e:e + 1], min_val=e * REGION, max_val=e * REGION + TOK)
                sp.dma_start(routed[ds(at, 128), :], fill[:, :]).then_inc(filled.sem, 16)
            sp.wait_ge(filled.sem, 16 * E)
            sp.wait_ge(empty_in.sem, empty_in.count(0))

            def load(j, p, jj):
                t = j - 2
                e = sp.value_load(table[0:1, 0, ds(j, 1)], min_val=0, max_val=E - 1)
                r = sp.value_load(table[0:1, 1, ds(j, 1)], min_val=0, max_val=EMPTY)
                if begun(t):
                    sp.wait_ge(xrT_ps.sem, xrT_ps.count(t))
                if begun(t):
                    sp.wait_ge(dest_sb.sem, dest_sb.count(t))
                sp.dma_start(xr[p][:, :], routed[ds(r, 128), :]).then_inc(row_in[p].sem, 16)
                if begun(t):
                    sp.wait_ge(hid_ps.sem, hid_ps.count(t))
                sp.dma_start(w1[p][0:HD, :, :], a["w1"][ds(e, 1)].rearrange("o p h f -> (o p) h f")
                             ).then_inc(w1_in[p].sem, 16)
                sp.dma_start(w1[p][HD:HD + 1, 0, :], a["b1"][ds(e, 1), :]).then_inc(w1_in[p].sem, 16)

            tiles(sp, load)

            for p in range(2):
                sp.wait_ge(sent[p].sem, sent[p].count(MAXTILES // 2 - 1))
            for b in range(B):
                if b >= 2:
                    if begun(b - 2):
                        sp.wait_ge(mixed.sem, mixed.count(b - 2))
                sp.dma_start(pairs[b % 2], by_pair[2 * S * b:2 * S * (b + 1), :].rearrange(
                    "(t p k) d -> p t (k d)", p=CH, k=2)).then_inc(pair_in[b % 2].sem, 16)

        @block.gpsimd
        def _(pool):
            for t in (w_g2, w_o):
                last = nc.gpsimd.memset(full(t), 0.0)
            last.then_inc(zeroed.sem, 1)
            nc.gpsimd.memset(v_pad[:, :, :, :], 0.0)
            nc.gpsimd.memset(q_block[:, :, :, :], 0.0)
            nc.gpsimd.memset(half_neg[:, :], -0.5)
            nc.gpsimd.memset(eps[:, :], EPS)
            nc.gpsimd.memset(idle[:, 1:2], 0.0)
            nc.gpsimd.memset(xT[:, :, :], 0.0)
            nc.gpsimd.memset(counts[:, :], 0.0)
            nc.gpsimd.memset(ones[:, :], 1.0)
            nc.gpsimd.memset(fill[:, :], 0.0).then_inc(zeroed.sem, 1)
            pool.wait_ge(zeroed.sem, 2)
            nc.gpsimd.memset(fill[:, D:D + 1], SKIP).then_inc(zeroed.sem, 1)
            pool.wait_ge(zeroed.sem, 3)
            pool.dma_start(routed[EMPTY:EMPTY + 128, :], fill[:, :]).then_inc(empty_in.sem, 16)
            pool.dma_start(w2[:, :, :, :], a["w2"]).then_inc(w2_in.sem, 16)
            pool.wait_ge(const_in.sem, N_CONST)

            def inverse_std(own_, b, n, k, ready, done):
                pool.wait_ge(ready.sem, ready.count(b, k))
                nc.gpsimd.tensor_tensor(vp[:, n], mv[:, n, :, 1], eps[:, :], ALU.add).then_inc(own_.sem, 1)
                pool.wait_ge(own_.sem, own_.after(1))
                nc.gpsimd.tensor_tensor(rstd[:, n], vp[:, n], half_neg[:, :], ALU.pow).then_inc(done.sem, 1)

            def run(a_, b, c):
                if c is not None:
                    own_pc.begin(c)
                    inverse_std(own_pc, c, 2, 0, cvar_sb, crstd_sb)
                    inverse_std(own_pc, c, 3, 1, cvar_sb, crstd_sb)
                    own_pc.end()
                if b is not None:
                    pool.wait_ge(q_sb.sem, q_sb.count(b))
                    if begun(b - 1):
                        pool.wait_ge(av_ps.sem, av_ps.count(b - 1))
                    nc.gpsimd.tensor_tensor(
                        q_dec[:, :, :].rearrange("p h (c n) -> p h c n", n=CH),
                        qT[:, :, CH:S].rearrange("p h (c n) -> p h c n", n=CH),
                        q_decay[:, :, :].unsqueeze(2).to_broadcast([HD, 2, NC_ - 1, CH]),
                        ALU.mult).then_inc(q_dec_sb.sem, 1)
                    pool.wait_ge(vk_sb.sem, vk_sb.count(b))
                    nc.gpsimd.tensor_tensor(
                        k_dec[:, :, :], k_tok[:, :, :],
                        k_decay[:, :, :].rearrange("p h d -> p (h d)").unsqueeze(1)
                        .to_broadcast([CH, NC_ - 1, D]), ALU.mult).then_inc(k_dec_sb.sem, 1)
                if c is not None:
                    pool.wait_ge(slots_sb.sem, slots_sb.count(c))
                    apart(pool)
                    for k in range(2):
                        for i in range(NC_):
                            nc.gpsimd.indirect_dma_start(
                                routed, bass.IndirectOffsetOnAxis(ap=slots[:, k, i:i + 1], axis=0),
                                x2[:, i, :], None).then_inc(scattered.sem, 16)
                if a_ is not None:
                    own_pa.begin(a_)
                    inverse_std(own_pa, a_, 0, 0, var_sb, rstd_sb)
                    inverse_std(own_pa, a_, 1, 1, var_sb, rstd_sb)
                    own_pa.end()
                    pool.wait_ge(h1_sb.sem, h1_sb.count(a_))
                    nc.gpsimd.tensor_tensor(
                        resid[:, ds(a_ * NC_, NC_), :], h1[:, :, :],
                        rows[:, 3, :].unsqueeze(1).to_broadcast([CH, NC_, D]), ALU.add
                    ).then_inc(hb_sb.sem, 1)

            pipeline(pool, run)

            def send(j, p, jj):
                pool.wait_ge(out_sb.sem, out_sb.count(j))
                if begun(j - 1):
                    pool.wait_ge(idled.sem, idled.count(j - 1))
                apart(pool).then_inc(idled.sem, 1)
                nc.gpsimd.indirect_dma_start(
                    by_pair, bass.IndirectOffsetOnAxis(ap=dest[p][:, 0:1], axis=0), yo[p][:, :], None,
                    bounds_check=last_row, oob_is_err=False).then_inc(sent[p].sem, 16)

            pool.wait_ge(table_sb.sem, table_sb.count(0))
            for p in range(2):
                last = nc.gpsimd.memset(xrT[p][HD:HD + 1, 0, :], 1.0)
            last.then_inc(zeroed.sem, 1)
            last_row = pool.to_reg(2 * TOK - 1)
            tiles(pool, send)

        @block.scalar
        def _(act):
            act.wait_ge(const_in.sem, N_CONST)
            act.dma_start(diff_keep[:, 0], a["diff"]).then_inc(tables.sem, 16)
            act.dma_start(diff_keep[:, 1], a["keep"]).then_inc(tables.sem, 16)
            act.wait_ge(tables.sem, 32)
            for h in range(NH):
                nc.scalar.activation(decay[:, h, :], diff_keep[:, 0], ACT.Exp, scale=slope_t[:, h:h + 1])
            nc.scalar.activation(k_decay[:, :, :], slope_t[:, :].unsqueeze(2).to_broadcast([CH, NH, DH]),
                                 ACT.Exp, scale=to_end[:, 0:1])
            for half in range(2):
                nc.scalar.activation(q_decay[:, half], pos[:, :], ACT.Exp, scale=slope_c[:, half:half + 1])
            nc.scalar.activation(carry[:, :], slope_c[:, :], ACT.Exp, scale=float(CH)
                                 ).then_inc(tables.sem, 1)
            act.wait_ge(zeroed.sem, 3)

            def run(a_, b, c):
                if a_ is not None:
                    for g in range(4):
                        half, u = divmod(g, 2)
                        act.wait_ge(xT_ps.sem, xT_ps.count(a_, g))
                        if begun(a_ - 1):
                            act.wait_ge(conv_sb.sem, conv_sb.count(a_ - 1, half))
                        nc.scalar.activation(
                            xT[:, half, PAD + S * u:PAD + S * (u + 1)], bank("A", AT["xT"] + g)[0:HD, 0:S],
                            ACT.Copy).then_inc(xT_sb.sem, 1)
                if b is not None:
                    for half in range(2):
                        act.wait_ge(xnT_ps.sem, xnT_ps.count(b, half))
                        if half == 0:
                            if begun(b - 1):
                                act.wait_ge(g1_ps.sem, g1_ps.count(b - 1))
                        nc.scalar.activation(xnT[:, half], bank("B", AT["xnT"] + half)[0:HD, 0:S],
                                             ACT.Copy).then_inc(xnT_sb.sem, 1)
                    for half in range(2):
                        act.wait_ge(q_ps.sem, q_ps.count(b, half))
                        if half == 0:
                            if begun(b - 1):
                                act.wait_ge(qb_in.sem, qb_in.count(b - 1))
                            if begun(b - 1):
                                act.wait_ge(q_dec_sb.sem, q_dec_sb.count(b - 1))
                        nc.scalar.activation(qT[:, half], bank("B", AT["q"] + half)[0:HD, 0:S],
                                             ACT.Silu).then_inc(q_sb.sem, 1)
                    for half in range(2):
                        act.wait_ge(k_ps.sem, k_ps.count(b, half))
                        if half == 0:
                            if begun(b - 1):
                                act.wait_ge(sc_ps.sem, sc_ps.count(b - 1))
                        nc.scalar.activation(kT[:, half], bank("B", AT["k"] + half)[0:HD, 0:S],
                                             ACT.Silu).then_inc(k_sb.sem, 1)
                    for i in range(NC_):
                        act.wait_ge(vk_ps.sem, vk_ps.count(b, i))
                        if i == 0:
                            if begun(b - 1):
                                act.wait_ge(av_ps.sem, av_ps.count(b - 1))
                            if begun(b - 1):
                                act.wait_ge(k_dec_sb.sem, k_dec_sb.count(b - 1))
                        src = bank("B", AT["vk"] + i)
                        last = nc.scalar.activation(v_pad[:, i, :, 0:DH],
                                                    src[0:CH, 0:D].rearrange("p (h d) -> p h d", d=DH), ACT.Silu)
                        if i < NC_ - 1:
                            last = nc.scalar.activation(k_tok[:, i], src[0:CH, D:2 * D], ACT.Silu)
                        last.then_inc(vk_sb.sem, 1)
                    act.wait_ge(g1_ps.sem, g1_ps.count(b))
                    if begun(b - 1):
                        act.wait_ge(g2_ps.sem, g2_ps.count(b - 1))
                    nc.scalar.activation(g1[:, :], bank("B", AT["g1"])[0:G, 0:S], ACT.Copy
                                         ).then_inc(g1_sb.sem, 1)
                if c is not None:
                    for half in range(2):
                        act.wait_ge(x2T_ps.sem, x2T_ps.count(c, half))
                        if half == 0:
                            if begun(c - 1):
                                act.wait_ge(lg_ps.sem, lg_ps.count(c - 1))
                        nc.scalar.activation(x2T[:, half], bank("C", AT["x2T"] + half)[0:HD, 0:S],
                                             ACT.Copy).then_inc(x2T_sb.sem, 1)
                if b is not None:
                    for g in range(NG):
                        act.wait_ge(g2_ps.sem, g2_ps.count(b, g))
                        if g == 0:
                            if begun(b - 1):
                                act.wait_ge(av_sb.sem, av_sb.count(b - 1))
                        nc.scalar.activation(gate[:, g], bank("B", AT["g2"] + g)[:, 0:S], ACT.Tanh,
                                             scale=0.5).then_inc(g2_sb.sem, 1)
                if a_ is not None:
                    for g in range(4):
                        u, half = divmod(g, 2)
                        lo = 2 * POOL_CUT[0] * u
                        n = 2 * POOL_CUT[u]
                        act.wait_ge(pw_ps.sem, pw_ps.count(a_, g))
                        if g == 0:
                            if begun(a_ - 1):
                                act.wait_ge(pooled_sb.sem, pooled_sb.count(a_ - 1))
                        nc.scalar.activation(pw[:, half, lo:lo + n], bank("A", AT["pw"] + g)[0:HD, 0:n],
                                             ACT.Relu, bias=b_pw[:, half:half + 1]).then_inc(pw_sb.sem, 1)
                    for g, (lo, n) in enumerate(((0, 2), (2, 1))):
                        act.wait_ge(chan_ps.sem, chan_ps.count(a_, g))
                        if g == 0:
                            if begun(a_ - 1):
                                act.wait_ge(cosine_ps.sem, cosine_ps.count(a_ - 1))
                        nc.scalar.activation(
                            chan[:, lo:lo + n, :], bank("A", AT["chan"] + g)[0:CH, 0:n * D].rearrange(
                                "p (t d) -> p t d", d=D), ACT.Copy).then_inc(chan_sb.sem, 1)
                    act.wait_ge(sine_ps.sem, sine_ps.count(a_))
                    if begun(a_ - 1):
                        act.wait_ge(y_sb.sem, y_sb.count(a_ - 1))
                    nc.scalar.activation(
                        sine[:, :, :], bank("A", AT["sine"])[0:CH, 0:NC_ * NQ].rearrange(
                            "p (t d) -> p t d", d=NQ), ACT.Copy).then_inc(sine_sb.sem, 1)

            act.wait_ge(tables_d.sem, tables_d.count(0))
            pipeline(act, run)

            act.wait_ge(slots_sb.sem, slots_sb.count(B - 1))
            nc.scalar.activation(gates[:, 0], gap[:, :], ACT.Exp).then_inc(exp_sb.sem, 1)

            def row_tile(j, p):
                act.wait_ge(xrT_ps.sem, xrT_ps.count(j))
                if begun(j - 2):
                    act.wait_ge(hid_ps.sem, hid_ps.count(j - 2))
                nc.scalar.activation(xrT[p][0:HD], ps[p][0:HD, 0:256].rearrange("p (h t) -> p h t", h=2),
                                     ACT.Copy).then_inc(xrT_sb.sem, 1)

            def hidden(j, p):
                act.wait_ge(hid_ps.sem, hid_ps.count(j, 0))
                if begun(j - 2):
                    act.wait_ge(out_ps.sem, out_ps.count(j - 2))
                nc.scalar.activation(hid[p][:, 0:4], ps[2 + 2 * p][:, :].rearrange("p (c t) -> p c t", c=4),
                                     ACT.Relu).then_inc(hid_a.sem, 1)

            row_tile(0, 0)
            row_tile(1, 1)

            def act_tile(j, p, jj):
                hidden(j, p)
                if not (isinstance(j, int) and j >= MAXTILES - 2):
                    row_tile(j + 2, p)

            tiles(act, act_tile)
            for b in range(B):
                act.wait_ge(mixed.sem, mixed.count(b))
                act.dma_start(out[b].rearrange("(t p) d -> p t d", p=CH), resid[:, NC_ * b:NC_ * (b + 1), :]
                              ).then_inc(out_done.sem, 16)
            act.wait_ge(out_done.sem, 16 * B)

        @block.vector
        def _(dve):
            dve.wait_ge(const_in.sem, N_CONST)
            dve.wait_ge(tables.sem, 33)
            dve.wait_ge(zeroed.sem, 3)
            nc.vector.tensor_tensor(decay[:, :, :], decay[:, :, :],
                                    diff_keep[:, 1:2].to_broadcast([CH, NH, CH]), ALU.mult
                                    ).then_inc(tables_d.sem, 1)

            def layernorm_stats(own_, b, n, k, src, done):
                apart(dve)
                for i in range(NC_):
                    last = nc.vector.bn_stats(stats[:, n, i], src(i))
                last.then_inc(own_.sem, 1)
                dve.wait_ge(own_.sem, own_.after(1))
                apart(dve)
                for i in range(NC_):
                    last = nc.vector.bn_aggr(mv[:, n, i], stats[:, n, i])
                last.then_inc(done.sem, 1)

            def norms_a(b):
                own_ln.begin(b)
                layernorm_stats(own_ln, b, 0, 0, lambda i: y[:, i], var_sb)
                dve.wait_ge(var_sb.sem, var_sb.count(b, 0))
                for i in range(NC_):
                    last = nc.vector.scalar_tensor_tensor(h1t(i), y[:, i], mv[:, 0, i, 0:1], rows[:, 0], ALU.subtract, ALU.mult)
                last.then_inc(own_ln.sem, 1)
                dve.wait_ge(rstd_sb.sem, rstd_sb.count(b, 0))
                if begun(b - 1):
                    dve.wait_ge(hb_sb.sem, hb_sb.count(b - 1))
                dve.wait_ge(own_ln.sem, own_ln.after(1))
                for i in range(NC_):
                    last = nc.vector.scalar_tensor_tensor(h1[:, i], h1t(i), rstd[:, 0, i:i + 1], rows[:, 1], ALU.mult, ALU.add)
                last.then_inc(h1_sb.sem, 1)
                dve.wait_ge(h1_sb.sem, h1_sb.count(b))
                layernorm_stats(own_ln, b, 1, 1, lambda i: h1[:, i], var_sb)
                dve.wait_ge(var_sb.sem, var_sb.count(b, 1))
                dve.wait_ge(rstd_sb.sem, rstd_sb.count(b, 1))
                if begun(b - 1):
                    dve.wait_ge(xnT_ps.sem, xnT_ps.count(b - 1))
                for i in range(NC_):
                    last = nc.vector.tensor_scalar(xn[:, i], h1[:, i], mv[:, 1, i, 0:1], rstd[:, 1, i:i + 1],
                                                   ALU.subtract, ALU.mult)
                last.then_inc(xn_sb.sem, 1)
                own_ln.end()

            def h1t(i):
                return y[:, i]

            def norms_c(c):
                own_c.begin(c)
                at = c * NC_

                def o(i):
                    g, k = (0, i) if i < 2 else (1, 0)
                    return bank("C", AT["o"] + g)[0:CH, k * D:(k + 1) * D]
                dve.wait_ge(o_ps.sem, o_ps.count(c))
                layernorm_stats(own_c, c, 2, 0, o, cvar_sb)
                dve.wait_ge(cvar_sb.sem, cvar_sb.count(c, 0))
                for i in range(NC_):
                    nc.vector.scalar_tensor_tensor(o_ln[:, i], o(i), mv[:, 2, i, 0:1], rows[:, 2],
                                                   ALU.subtract, ALU.mult).then_inc(o_free.sem, 1)
                dve.wait_ge(o_free.sem, o_free.count(c))
                dve.wait_ge(crstd_sb.sem, crstd_sb.count(c, 0))
                dve.wait_ge(hb_sb.sem, hb_sb.count(c))
                for i in range(NC_):
                    last = nc.vector.scalar_tensor_tensor(
                        resid[:, ds(at + i, 1), :], o_ln[:, i:i + 1], rstd[:, 2, i:i + 1],
                        resid[:, ds(at + i, 1), :], ALU.mult, ALU.add)
                last.then_inc(own_c.sem, 1)
                dve.wait_ge(own_c.sem, own_c.after(1))
                layernorm_stats(own_c, c, 3, 1, lambda i: resid[:, ds(at + i, 1), :].rearrange("p o d -> p (o d)"), cvar_sb)
                dve.wait_ge(cvar_sb.sem, cvar_sb.count(c, 1))
                dve.wait_ge(crstd_sb.sem, crstd_sb.count(c, 1))
                if begun(c - 1):
                    dve.wait_ge(x2T_ps.sem, x2T_ps.count(c - 1))
                if begun(c - 1):
                    dve.wait_ge(scattered.sem, scattered.count(c - 1))
                for i in range(NC_):
                    last = nc.vector.tensor_scalar(x2[:, i:i + 1, 0:D], resid[:, ds(at + i, 1), :],
                                                   mv[:, 3, i, 0:1], rstd[:, 3, i:i + 1],
                                                   ALU.subtract, ALU.mult)
                last.then_inc(x2_sb.sem, 1)

            def convolve(b):
                own_conv.begin(b)
                for half in range(2):
                    dve.wait_ge(xT_sb.sem, xT_sb.count(b, 2 * half + 1))
                    if half == 0:
                        if begun(b - 1):
                            dve.wait_ge(pw_ps.sem, pw_ps.count(b - 1))
                    for k in range(K):
                        tap = xT[:, half, k:k + S_IN]
                        if k == 0:
                            ins = nc.vector.tensor_scalar(conv[:, half], tap, w_dw[:, half, 0:1],
                                                          b_dw[:, half:half + 1], ALU.mult, ALU.add)
                        else:
                            dve.wait_ge(own_conv.sem, own_conv.after(1))
                            ins = nc.vector.scalar_tensor_tensor(conv[:, half], tap, w_dw[:, half, k:k + 1],
                                                                 conv[:, half], ALU.mult, ALU.add)
                        if k < K - 1:
                            ins.then_inc(own_conv.sem, 1)
                    ins.then_inc(conv_sb.sem, 1)
                own_conv.end()

            def choose(c):
                one, two_ = pick[:, 0], pick[:, 1]
                def bc(x):
                    return x.unsqueeze(2).to_broadcast([CH, NC_, E])
                dve.wait_ge(lg_ps.sem, lg_ps.count(c))
                if begun(c - 1):
                    dve.wait_ge(rank_ps.sem, rank_ps.count(c - 1))
                if begun(c - 1):
                    dve.wait_ge(slots_sb.sem, slots_sb.count(c - 1))
                nc.vector.tensor_tensor(logit[:, :, :], bank("C", AT["lg"])[0:CH, 0:NC_ * E].rearrange(
                    "p (t e) -> p t e", e=E), small[:, 0], ALU.add).then_inc(lg_sb.sem, 1)
                dve.wait_ge(lg_sb.sem, lg_sb.count(c))
                nc.vector.tensor_reduce(top[:, 0], logit[:, :, :], AX.X, ALU.max).then_inc(own_c.sem, 1)
                dve.wait_ge(own_c.sem, own_c.after(1))
                nc.vector.tensor_tensor(hit[:, :, :], logit[:, :, :], bc(top[:, 0]), ALU.is_equal).then_inc(own_c.sem, 1)
                dve.wait_ge(own_c.sem, own_c.after(1))
                nc.vector.tensor_tensor(hit[:, :, :], hit[:, :, :], small[:, 1], ALU.mult).then_inc(own_c.sem, 1)
                dve.wait_ge(own_c.sem, own_c.after(1))
                nc.vector.tensor_reduce(top[:, 1], hit[:, :, :], AX.X, ALU.max).then_inc(own_c.sem, 1)
                dve.wait_ge(own_c.sem, own_c.after(1))
                nc.vector.tensor_tensor(one, small[:, 1], bc(top[:, 1]), ALU.is_equal).then_inc(own_c.sem, 1)
                dve.wait_ge(own_c.sem, own_c.after(1))
                nc.vector.scalar_tensor_tensor(logit2[:, :, :], one, -3.0e38, logit[:, :, :],
                                                          ALU.mult, ALU.add).then_inc(own_c.sem, 1)
                dve.wait_ge(own_c.sem, own_c.after(1))
                nc.vector.tensor_reduce(top[:, 2], logit2[:, :, :], AX.X, ALU.max).then_inc(own_c.sem, 1)
                dve.wait_ge(own_c.sem, own_c.after(1))
                nc.vector.tensor_tensor(hit[:, :, :], logit2[:, :, :], bc(top[:, 2]), ALU.is_equal).then_inc(own_c.sem, 1)
                dve.wait_ge(own_c.sem, own_c.after(1))
                nc.vector.tensor_tensor(hit[:, :, :], hit[:, :, :], small[:, 1], ALU.mult).then_inc(own_c.sem, 1)
                dve.wait_ge(own_c.sem, own_c.after(1))
                nc.vector.tensor_reduce(top[:, 3], hit[:, :, :], AX.X, ALU.max).then_inc(own_c.sem, 1)
                dve.wait_ge(own_c.sem, own_c.after(1))
                nc.vector.tensor_tensor(two_, small[:, 1], bc(top[:, 3]), ALU.is_equal).then_inc(own_c.sem, 1)
                dve.wait_ge(own_c.sem, own_c.after(1))
                nc.vector.tensor_tensor(picked[:, :, :], one, two_, ALU.add).then_inc(pick_sb.sem, 1)
                nc.vector.tensor_tensor(gap[:, ds(c * NC_, NC_)], top[:, 2], top[:, 0], ALU.subtract)
                nc.vector.tensor_copy(x2[:, :, D:D + 1], tok2[:, ds(c * NC_, NC_)].unsqueeze(2))
                nc.vector.tensor_scalar(x2[:, :, D + 1:D + 2], top[:, 1].unsqueeze(2), -1.0, float(E),
                                                   ALU.mult, ALU.add).then_inc(own_c.sem, 1)

            def place(c):
                dve.wait_ge(rank_ps.sem, rank_ps.count(c))
                nc.vector.tensor_tensor(row_of[:, :, :], bank("C", AT["rank"])[0:CH, 0:NC_ * E].rearrange(
                    "p (t e) -> p t e", e=E), small[:, 2], ALU.add).then_inc(rank_sb.sem, 1)
                nc.vector.tensor_reduce(tile_sum[:, :], picked[:, :, :].rearrange("p t e -> p e t"),
                                                   AX.X, ALU.add).then_inc(own_c.sem, 1)
                dve.wait_ge(rank_sb.sem, rank_sb.count(c))
                dve.wait_ge(own_c.sem, own_c.after(2))
                nc.vector.tensor_tensor(
                    row_hit[:, :, :, :], pick[:, :, :, :],
                    row_of[:, :, :].unsqueeze(1).to_broadcast([CH, 2, NC_, E]), ALU.mult).then_inc(own_c.sem, 1)
                nc.vector.tensor_tensor(counts[:, :], counts[:, :], tile_sum[:, :], ALU.add
                                        ).then_inc(counts_sb.sem, 1)
                dve.wait_ge(own_c.sem, own_c.after(1))
                nc.vector.tensor_reduce(slots_f[:, :, :], row_hit[:, :, :, :], AX.X, ALU.add).then_inc(own_c.sem, 1)
                dve.wait_ge(own_c.sem, own_c.after(1))
                nc.vector.tensor_copy(slots[:, :, :], slots_f[:, :, :]).then_inc(slots_sb.sem, 1)
                own_c.end()

            def run(a_, b, c):
                if c is not None:
                    norms_c(c)
                if a_ is not None:
                    convolve(a_)
                if c is not None:
                    choose(c)
                if b is not None:
                    for g in range(4 * NC_):
                        i, h0 = g // 4, HG * (g % 4)
                        dve.wait_ge(sc_ps.sem, sc_ps.count(b, g))
                        if g == 0:
                            if begun(b - 1):
                                dve.wait_ge(av_ps.sem, av_ps.count(b - 1))
                        nc.vector.tensor_tensor(
                            scores[:, i, h0:h0 + HG], bank("B", AT["sc"] + g)[0:CH, 0:HG * CH].rearrange(
                                "p (h n) -> p h n", n=CH), decay[:, h0:h0 + HG], ALU.mult
                        ).then_inc(sc_sb.sem, 1)
                if c is not None:
                    place(c)
                if a_ is not None:
                    for u in range(2):
                        lo = POOL_CUT[0] * u
                        dve.wait_ge(pw_sb.sem, pw_sb.count(a_, 2 * u + 1))
                        if u == 0:
                            if begun(a_ - 1):
                                dve.wait_ge(chan_ps.sem, chan_ps.count(a_ - 1))
                        v = pw[:, :, 2 * lo:2 * (lo + POOL_CUT[u])].rearrange("p h (s t) -> p h s t", t=2)
                        nc.vector.tensor_tensor(pooled[:, :, lo:lo + POOL_CUT[u]], v[:, :, :, 0], v[:, :, :, 1],
                                                ALU.max).then_inc(pooled_sb.sem, 1)
                if b is not None:
                    for i in range(NC_ - 1):
                        dve.wait_ge(st_ps.sem, st_ps.count(b, i))
                        p_ = bank("B", AT["st"] + i)[0:HD, 0:2 * HH * PH].rearrange("p (h s) -> p h s", h=2)
                        m_ = head_mask[:, :, :].rearrange("p h s -> p (h s)").unsqueeze(1).to_broadcast([HD, 2, HH * PH])
                        ins = nc.vector.tensor_tensor(state[:, i], p_, m_, ALU.mult)
                        if i == 0:
                            ins.then_inc(st_sb.sem, 1)
                        else:
                            own_st.begin(b)
                            ins.then_inc(own_st.sem, 1)
                            dve.wait_ge(own_st.sem, own_st.after(1))
                            own_st.end()
                            dve.wait_ge(st_sb.sem, st_sb.count(b, 0))
                            for half in range(2):
                                ins = nc.vector.scalar_tensor_tensor(
                                    state[:, i, half], state[:, i - 1, half], carry[:, half:half + 1],
                                    state[:, i, half], ALU.mult, ALU.add)
                            ins.then_inc(st_sb.sem, 1)
                    dve.wait_ge(g2_sb.sem, g2_sb.count(b))
                    for i in range(NC_):
                        dve.wait_ge(av_ps.sem, av_ps.count(b, i))
                        if i == 0:
                            if begun(b - 1):
                                dve.wait_ge(o_ps.sem, o_ps.count(b - 1))
                        nc.vector.scalar_tensor_tensor(
                            gated[:, :, CH * i:CH * (i + 1)], gate[:, :, CH * i:CH * (i + 1)], 1.0,
                            bank("C", AT["av"] + i)[:, 0:NG * CH].rearrange("p (g n) -> p g n", n=CH),
                            ALU.add, ALU.mult).then_inc(av_sb.sem, 1)
                if a_ is not None:
                    dve.wait_ge(sine_sb.sem, sine_sb.count(a_))
                    dve.wait_ge(cosine_ps.sem, cosine_ps.count(a_))
                    p_ = bank("A", AT["cosine"])[0:CH, 0:NC_ * NP].rearrange("p (t d) -> p t d", d=NP)
                    nc.vector.tensor_copy(y[:, :, 0:NP:NP - 1], p_[:, :, 0:NP:NP - 1])
                    nc.vector.tensor_tensor(y[:, :, 1:NP - 1], p_[:, :, 1:NP - 1], sine[:, :, :], ALU.subtract)
                    nc.vector.tensor_tensor(y[:, :, NP:D], p_[:, :, 1:NP - 1], sine[:, :, :], ALU.add
                                            ).then_inc(y_sb.sem, 1)
                    dve.wait_ge(y_sb.sem, y_sb.count(a_))
                    norms_a(a_)

            pipeline(dve, run)

            own_t.begin(0)

            dve.wait_ge(n_ps.sem, n_ps.count(0))
            nc.vector.tensor_copy(n_f[:, :], ps[0][:, 0:E]).then_inc(own_t.sem, 1)
            dve.wait_ge(own_t.sem, own_t.after(1))
            nc.vector.tensor_scalar(n_i[:, 0], n_f[:, :], 127.0, None, ALU.add).then_inc(own_t.sem, 1)
            dve.wait_ge(own_t.sem, own_t.after(1))
            nc.vector.tensor_scalar(n_i[:, 1], n_i[:, 0], 7, None, ALU.logical_shift_right).then_inc(own_t.sem, 1)
            dve.wait_ge(own_t.sem, own_t.after(1))
            nc.vector.tensor_copy(nt_f[:, :], n_i[:, 1]).then_inc(own_t.sem, 1)
            dve.wait_ge(own_t.sem, own_t.after(1))
            nc.vector.tensor_tensor_scan(end_f[:, :], ones[:, 0:E], nt_f[:, :], 0.0, ALU.mult, ALU.add).then_inc(own_t.sem, 1)
            dve.wait_ge(own_t.sem, own_t.after(1))
            j8 = jcol[:, :].unsqueeze(2).to_broadcast([128, MAXTILES, E])
            nc.vector.tensor_tensor(past[:, :, :], j8, end_f[:, :].unsqueeze(1).to_broadcast([128, MAXTILES, E]),
                                    ALU.is_ge).then_inc(own_t.sem, 1)
            dve.wait_ge(own_t.sem, own_t.after(1))
            nc.vector.tensor_tensor(past_n[:, :, :], past[:, :, :],
                                    nt_f[:, :].unsqueeze(1).to_broadcast([128, MAXTILES, E]), ALU.mult).then_inc(own_t.sem, 1)
            dve.wait_ge(own_t.sem, own_t.after(1))
            nc.vector.tensor_reduce(e_of[:, :], past[:, :, 0:E - 1], AX.X, ALU.add).then_inc(own_t.sem, 1)
            dve.wait_ge(own_t.sem, own_t.after(1))
            nc.vector.tensor_reduce(first[:, :], past_n[:, :, 0:E - 1], AX.X, ALU.add).then_inc(own_t.sem, 1)
            dve.wait_ge(own_t.sem, own_t.after(1))
            nc.vector.scalar_tensor_tensor(blk[:, 0], e_of[:, :], float(REGION // 128), jcol[:, :],
                                           ALU.mult, ALU.add).then_inc(own_t.sem, 1)
            dve.wait_ge(own_t.sem, own_t.after(1))
            nc.vector.tensor_tensor(blk[:, 0], blk[:, 0], first[:, :], ALU.subtract).then_inc(own_t.sem, 1)
            dve.wait_ge(own_t.sem, own_t.after(1))
            nc.vector.tensor_scalar(blk[:, 1], blk[:, 0], -1.0, float(EMPTY // 128), ALU.mult, ALU.add).then_inc(own_t.sem, 1)
            dve.wait_ge(own_t.sem, own_t.after(1))
            nc.vector.tensor_tensor(blk[:, 1], blk[:, 1], past[:, :, E - 1], ALU.mult).then_inc(own_t.sem, 1)
            dve.wait_ge(own_t.sem, own_t.after(1))
            nc.vector.tensor_tensor(blk[:, 2], blk[:, 1], blk[:, 0], ALU.add).then_inc(own_t.sem, 1)
            dve.wait_ge(own_t.sem, own_t.after(1))
            nc.vector.tensor_scalar(table[0:1, 1], blk[0:1, 2], 128.0, None, ALU.mult).then_inc(own_t.sem, 1)
            dve.wait_ge(own_t.sem, own_t.after(1))
            nc.vector.tensor_copy(table[0:1, 0], e_of[0:1, :]).then_inc(own_t.sem, 1)
            dve.wait_ge(own_t.sem, own_t.after(1))
            own_t.end()
            nc.vector.tensor_tensor(fill_at[0:1, :], n_f[0:1, :], small[0:1, 2, 0], ALU.add
                                    ).then_inc(table_sb.sem, 1)
            dve.wait_ge(table_sb.sem, table_sb.count(0))
            dve.wait_ge(exp_sb.sem, exp_sb.count(0))
            own_g.begin(0)
            nc.vector.tensor_scalar(gates[:, 2], gates[:, 0], 1.0, None, ALU.add).then_inc(own_g.sem, 1)
            dve.wait_ge(own_g.sem, own_g.after(1))
            nc.vector.reciprocal(gates[:, 1], gates[:, 2]).then_inc(own_g.sem, 1)
            dve.wait_ge(own_g.sem, own_g.after(1))
            nc.vector.tensor_tensor(gates[:, 2], gates[:, 0], gates[:, 1], ALU.mult)
            own_g.end()
            dve.wait_ge(b2_in.sem, b2_in.count(0))

            def destination(j, p, jj):
                dve.wait_ge(row_in[p].sem, row_in[p].count(jj))
                nc.vector.scalar_tensor_tensor(dest_f[:, ds(j, 1)], xr[p][:, D + 1:D + 2], e_of[:, ds(j, 1)],
                                               xr[p][:, D:D + 1], ALU.not_equal, ALU.add
                                               ).then_inc(dest_sb.sem, 1)

            destination(0, 0, 0)
            destination(1, 1, 0)

            def dve_tile(j, p, jj):
                e = dve.value_load(table[0:1, 0, ds(j, 1)], min_val=0, max_val=E - 1)
                dve.wait_ge(hid_ps.sem, hid_ps.count(j, 1))
                if begun(j - 2):
                    dve.wait_ge(out_ps.sem, out_ps.count(j - 2))
                nc.vector.tensor_scalar(hid[p][:, 4:FC], ps[3 + 2 * p][:, 0:256].rearrange(
                    "p (c t) -> p c t", c=2), 0.0, None, ALU.max).then_inc(hid_b.sem, 1)
                if not (isinstance(j, int) and j >= MAXTILES - 2):
                    destination(j + 2, p, jj + 1)
                if begun(jj - 1):
                    dve.wait_ge(sent[p].sem, sent[p].count(jj - 1))
                dve.wait_ge(dest_sb.sem, dest_sb.count(j))
                nc.vector.tensor_copy(dest[p][:, :], dest_f[:, ds(j, 1)])
                dve.wait_ge(out_ps.sem, out_ps.count(j))
                nc.vector.tensor_tensor(yo[p][:, :], ps[6 + p][:, 0:D], b2_rows[:, ds(e, 1), :].rearrange(
                    "p o d -> p (o d)"), ALU.add).then_inc(out_sb.sem, 1)

            tiles(dve, dve_tile)

            for b in range(B):
                pr = pairs[b % 2]
                dve.wait_ge(pair_in[b % 2].sem, pair_in[b % 2].count(b // 2))
                own_m.begin(b)
                for k in range(2):
                    for i in range(NC_):
                        t = NC_ * b + i
                        last = nc.vector.scalar_tensor_tensor(resid[:, t], pr[:, i, D * k:D * (k + 1)],
                                                              gates[:, 1 + k, t:t + 1], resid[:, t], ALU.mult, ALU.add)
                    if k == 0:
                        last.then_inc(own_m.sem, 1)
                        dve.wait_ge(own_m.sem, own_m.after(1))
                own_m.end()
                last.then_inc(mixed.sem, 1)

        @block.tensor
        def _(pe):
            mm, tr = nc.tensor.matmul, nc.tensor.transpose
            pe.wait_ge(const_in.sem, N_CONST)
            pe.wait_ge(zeroed.sem, 3)

            def transpose_x(b):
                pe.wait_ge(x_in.sem, x_in.count(b))
                for g in range(4):
                    half, u = divmod(g, 2)
                    if shared("A", AT["xT"] + g, b):
                        pe.wait_ge(*drained("A", AT["xT"] + g, b))
                    for t in range(XT // 2):
                        last = tr(bank("A", AT["xT"] + g)[0:HD, CH * t:CH * (t + 1)],
                                  x_rows[:, XT // 2 * u + t, HD * half:HD * (half + 1)], ident[0:CH, 0:CH])
                    last.then_inc(xT_ps.sem, 1)

            def pointwise(b):
                pe.wait_ge(conv_sb.sem, conv_sb.count(b))
                for g in range(4):
                    u, half = divmod(g, 2)
                    lo, n = 2 * POOL_CUT[0] * u, 2 * POOL_CUT[u]
                    if shared("A", AT["pw"] + g, b):
                        pe.wait_ge(*drained("A", AT["pw"] + g, b))
                    for k in range(2):
                        last = mm(bank("A", AT["pw"] + g)[0:HD, 0:n], w_pw[:, k, HD * half:HD * (half + 1)],
                                  conv[:, k, lo:lo + n], start=(k == 0), stop=(k == 1))
                    last.then_inc(pw_ps.sem, 1)

            def dft(b):
                pe.wait_ge(pooled_sb.sem, pooled_sb.count(b))
                for g, ts in enumerate(((0, 1), (2,))):
                    if shared("A", AT["chan"] + g, b):
                        pe.wait_ge(*drained("A", AT["chan"] + g, b))
                    for i, t in enumerate(ts):
                        for k in range(2):
                            last = mm(bank("A", AT["chan"] + g)[0:CH, D * i:D * (i + 1)],
                                      pooled[:, k, CH * t:CH * (t + 1)], dft_c[:, k, :],
                                      start=(k == 0), stop=(k == 1))
                    last.then_inc(chan_ps.sem, 1)
                pe.wait_ge(chan_sb.sem, chan_sb.count(b))
                for name, w, lo, n, done in (("sine", sin_s, NP, NQ, sine_ps), ("cosine", cos_s, 0, NP, cosine_ps)):
                    if shared("A", AT[name], b):
                        pe.wait_ge(*drained("A", AT[name], b))
                    for j in range(NC_):
                        for t in range(NC_):
                            last = mm(bank("A", AT[name])[0:CH, n * j:n * (j + 1)],
                                      w[:, t, CH * j:CH * (j + 1)], chan[:, t, lo:lo + n],
                                      start=(t == 0), stop=(t == NC_ - 1))
                    last.then_inc(done.sem, 1)

            def project(b):
                pe.wait_ge(xn_sb.sem, xn_sb.count(b))
                for half in range(2):
                    if shared("B", AT["xnT"] + half, b):
                        pe.wait_ge(*drained("B", AT["xnT"] + half, b))
                    for i in range(NC_):
                        last = tr(bank("B", AT["xnT"] + half)[0:HD, CH * i:CH * (i + 1)],
                                  xn[:, i, HD * half:HD * (half + 1)], ident[0:CH, 0:CH])
                    last.then_inc(xnT_ps.sem, 1)
                pe.wait_ge(xnT_sb.sem, xnT_sb.count(b))
                for name, w, done in (("q", w_q, q_ps), ("k", w_k, k_ps)):
                    for half in range(2):
                        if shared("B", AT[name] + half, b):
                            pe.wait_ge(*drained("B", AT[name] + half, b))
                        for k in range(2):
                            last = mm(bank("B", AT[name] + half)[0:HD, 0:S], w[:, k, HD * half:HD * (half + 1)],
                                      xnT[:, k, :], start=(k == 0), stop=(k == 1))
                        last.then_inc(done.sem, 1)
                for i in range(NC_):
                    n = 2 * D if i < NC_ - 1 else D
                    if shared("B", AT["vk"] + i, b):
                        pe.wait_ge(*drained("B", AT["vk"] + i, b))
                    for k in range(2):
                        last = mm(bank("B", AT["vk"] + i)[0:CH, 0:n], xnT[:, k, CH * i:CH * (i + 1)],
                                  w_vk[:, k, 0:n], start=(k == 0), stop=(k == 1))
                    last.then_inc(vk_ps.sem, 1)
                if shared("B", AT["g1"], b):
                    pe.wait_ge(*drained("B", AT["g1"], b))
                for k in range(2):
                    last = mm(bank("B", AT["g1"])[0:G, 0:S], w_g1[:, k, :], xnT[:, k, :],
                              start=(k == 0), stop=(k == 1))
                last.then_inc(g1_ps.sem, 1)

            def project_gate(b):
                pe.wait_ge(g1_sb.sem, g1_sb.count(b))
                for g in range(NG):
                    if shared("B", AT["g2"] + g, b):
                        pe.wait_ge(*drained("B", AT["g2"] + g, b))
                    mm(bank("B", AT["g2"] + g)[:, 0:S], w_g2[:, 4 * g:4 * (g + 1), :].rearrange("p h d -> p (h d)"),
                       g1[:, :], start=True, stop=True).then_inc(g2_ps.sem, 1)

            def score(b):
                pe.wait_ge(k_sb.sem, k_sb.count(b))
                pe.wait_ge(qb_in.sem, qb_in.count(b))
                for g in range(4 * NC_):
                    i, q = divmod(g, 4)
                    half, h0 = divmod(HG * q, HH)
                    if shared("B", AT["sc"] + g, b):
                        pe.wait_ge(*drained("B", AT["sc"] + g, b))
                    mm(bank("B", AT["sc"] + g)[0:CH, 0:HG * CH], kT[:, half, CH * i:CH * (i + 1)],
                       q_block[:, half, h0:h0 + HG, CH * i:CH * (i + 1)], start=True, stop=True
                       ).then_inc(sc_ps.sem, 1)

            def attend(b):
                pe.wait_ge(vk_sb.sem, vk_sb.count(b))
                pe.wait_ge(k_dec_sb.sem, k_dec_sb.count(b))
                for i in range(NC_ - 1):
                    if shared("B", AT["st"] + i, b):
                        pe.wait_ge(*drained("B", AT["st"] + i, b))
                    for half in range(2):
                        last = mm(bank("B", AT["st"] + i)[0:HD, HH * PH * half:HH * PH * (half + 1)],
                                  k_dec[:, i, HD * half:HD * (half + 1)],
                                  v_pad[:, i, HH * half:HH * (half + 1), :].rearrange("p h d -> p (h d)"),
                                  start=True, stop=True)
                    last.then_inc(st_ps.sem, 1)
                pe.wait_ge(q_dec_sb.sem, q_dec_sb.count(b))
                for i in range(NC_):
                    o = bank("C", AT["av"] + i)
                    pe.wait_ge(sc_sb.sem, sc_sb.count(b, 4 * i + 3))
                    if shared("C", AT["av"] + i, b):
                        pe.wait_ge(*drained("C", AT["av"] + i, b))
                    if i:
                        pe.wait_ge(st_sb.sem, st_sb.count(b, i - 1))
                    for g in range(NG):
                        cols = slice(CH * g, CH * (g + 1))
                        if i:
                            for p0, n, half, s0 in (((0, 128, 0, 0),), ((0, 64, 0, 128), (64, 64, 1, 0)),
                                                    ((0, 128, 1, 64),))[g]:
                                mm(o[p0:p0 + n, cols], state[:, i - 1, half, s0:s0 + n],
                                   q_dec[:, half, CH * (i - 1):CH * i], start=True, stop=False,
                                   skip_group_check=True)
                        for j in range(4):
                            last = mm(o[PH * j:PH * (j + 1), cols], v_pad[:, i, 4 * g + j, :],
                                      scores[:, i, 4 * g + j, :], start=(i == 0), stop=True, skip_group_check=True)
                    last.then_inc(av_ps.sem, 1)

            def output(c):
                pe.wait_ge(av_sb.sem, av_sb.count(c))
                for g, ts in enumerate(((0, 1), (2,))):
                    if shared("C", AT["o"] + g, c):
                        pe.wait_ge(*drained("C", AT["o"] + g, c))
                    for i, t in enumerate(ts):
                        for k in range(NG):
                            last = mm(bank("C", AT["o"] + g)[0:CH, D * i:D * (i + 1)],
                                      gated[:, k, CH * t:CH * (t + 1)], w_o[:, k, :],
                                      start=(k == 0), stop=(k == NG - 1))
                    last.then_inc(o_ps.sem, 1)

            def route(c):
                pe.wait_ge(x2_sb.sem, x2_sb.count(c))
                for half in range(2):
                    if shared("C", AT["x2T"] + half, c):
                        pe.wait_ge(*drained("C", AT["x2T"] + half, c))
                    for i in range(NC_):
                        last = tr(bank("C", AT["x2T"] + half)[0:HD, CH * i:CH * (i + 1)],
                                  x2[:, i, HD * half:HD * (half + 1)], ident[0:CH, 0:CH])
                    last.then_inc(x2T_ps.sem, 1)
                pe.wait_ge(x2T_sb.sem, x2T_sb.count(c))
                if shared("C", AT["lg"], c):
                    pe.wait_ge(*drained("C", AT["lg"], c))
                for i in range(NC_):
                    for k in range(2):
                        last = mm(bank("C", AT["lg"])[0:CH, E * i:E * (i + 1)], x2T[:, k, CH * i:CH * (i + 1)],
                                  w_r[:, k, :], start=(k == 0), stop=(k == 1))
                last.then_inc(lg_ps.sem, 1)

            def rank(c):
                pe.wait_ge(pick_sb.sem, pick_sb.count(c))
                if begun(c - 1):
                    pe.wait_ge(counts_sb.sem, counts_sb.count(c - 1))
                if shared("C", AT["rank"], c):
                    pe.wait_ge(*drained("C", AT["rank"], c))
                o = bank("C", AT["rank"])
                flat = picked[:, :, :].rearrange("p t e -> p (t e)")
                mm(o[0:CH, 0:NC_ * E], tri[:, :], flat, start=True, stop=False, skip_group_check=True)
                mm(o[0:CH, 0:NC_ * E], ones[0:CH, 0:CH], counts[:, :].unsqueeze(1).to_broadcast([CH, NC_, E]),
                   start=False, stop=False, skip_group_check=True)
                mm(o[0:CH, 2 * E:3 * E], ones[0:CH, 0:CH], flat[:, 0:E], start=False, stop=False, skip_group_check=True)
                mm(o[0:CH, E:3 * E], ones[0:CH, 0:CH], flat[:, 0:2 * E], start=False, stop=True, skip_group_check=True
                   ).then_inc(rank_ps.sem, 1)

            def run(a_, b, c):
                if c is not None:
                    output(c)
                if a_ is not None:
                    transpose_x(a_)
                if b is not None:
                    project(b)
                if c is not None:
                    route(c)
                if b is not None:
                    project_gate(b)
                    score(b)
                if c is not None:
                    rank(c)
                if a_ is not None:
                    pointwise(a_)
                if b is not None:
                    attend(b)
                if a_ is not None:
                    dft(a_)

            pipeline(pe, run)

            pe.wait_ge(counts_sb.sem, counts_sb.count(B - 1))
            mm(ps[0][:, 0:E], ones[0:CH, :], counts[:, :], start=True, stop=True).then_inc(n_ps.sem, 1)
            pe.wait_ge(table_sb.sem, table_sb.count(0))
            pe.wait_ge(w2_in.sem, w2_in.count(0))
            pe.wait_ge(zeroed.sem, 4)

            def up(j, p, jj):
                pe.wait_ge(w1_in[p].sem, w1_in[p].count(jj))
                pe.wait_ge(xrT_sb.sem, xrT_sb.count(j))
                if begun(j - 2):
                    pe.wait_ge(hid_a.sem, hid_a.count(j - 2))
                if begun(j - 2):
                    pe.wait_ge(hid_b.sem, hid_b.count(j - 2))
                for m in range(FC):
                    dst = ps[2 + 2 * p][:, 128 * m:128 * (m + 1)] if m < 4 else \
                        ps[3 + 2 * p][:, 128 * (m - 4):128 * (m - 3)]
                    for k in range(2):
                        n = HD + 1 - k
                        last = mm(dst, w1[p][0:n, k, 128 * m:128 * (m + 1)], xrT[p][0:n, k, :],
                                  start=(k == 0), stop=(k == 1))
                    if m in (3, FC - 1):
                        last.then_inc(hid_ps.sem, 1)

            def down(j, p):
                e = pe.value_load(table[0:1, 0, ds(j, 1)], min_val=0, max_val=E - 1)
                pe.wait_ge(hid_a.sem, hid_a.count(j))
                pe.wait_ge(hid_b.sem, hid_b.count(j))
                if begun(j - 2):
                    pe.wait_ge(out_sb.sem, out_sb.count(j - 2))
                for m in range(FC):
                    last = mm(ps[6 + p][:, 0:D], hid[p][:, m, :], w2[:, ds(e, 1), m, :].rearrange("p o d -> p (o d)"),
                              start=(m == 0), stop=(m == FC - 1))
                last.then_inc(out_ps.sem, 1)

            def tile_step(j, p, jj):
                if not (isinstance(j, int) and j + 1 >= MAXTILES):
                    up(j + 1, 1 - p, jj + p)
                if not (isinstance(j, int) and j + 2 >= MAXTILES):
                    pe.wait_ge(row_in[p].sem, row_in[p].count(jj + 1))
                    xrT_in(j + 2, p)
                down(j, p)

            def xrT_in(j, p):
                if begun(j - 2):
                    pe.wait_ge(xrT_sb.sem, xrT_sb.count(j - 2))
                for half in range(2):
                    last = tr(ps[p][0:HD, 128 * half:128 * (half + 1)], xr[p][:, HD * half:HD * (half + 1)],
                              ident[:, :])
                last.then_inc(xrT_ps.sem, 1)

            pe.wait_ge(row_in[0].sem, row_in[0].count(0))
            xrT_in(0, 0)
            pe.wait_ge(row_in[1].sem, row_in[1].count(0))
            xrT_in(1, 1)
            up(0, 0, 0)
            tiles(pe, tile_step)


def tables():
    f = np.float32
    order = channel_order()
    k = np.arange(D)
    turn = 2 * np.pi * ((k[:, None] * k[None, :]) % D) / D
    dft_c = np.concatenate([np.cos(turn)[:, 0:NP], np.sin(turn)[:, 1:NQ + 1]], 1)
    s = np.arange(S)
    turn = 2 * np.pi * ((s[:, None] * s[None, :]) % S) / S
    seq = lambda m: m.reshape(NC_, CH, S).transpose(1, 0, 2).astype(f)
    n = np.arange(CH)
    diff = n[None, :] - n[:, None]
    ch = np.arange(HD)
    tile = np.arange(NT)
    return dict(
        ident=np.eye(128, dtype=f), dft_c=halves(dft_c.astype(f)),
        cos_s=seq(np.cos(turn)), sin_s=seq(np.sin(turn)),
        small=np.stack([np.tile(E - np.arange(E), (NC_, 1)), np.tile(REGION * np.arange(E), (NC_, 1))]).astype(f),
        to_end=(CH - n)[:, None].astype(f), pos=n.astype(f), tri=(n[:, None] < n[None, :]).astype(f),
        head_mask=np.repeat((0.5 * (ch[:, None] // DH == np.arange(HH)[None, :])).astype(f)[:, :, None], PH, 2),
        tok2=(2 * (tile[None, :] * CH + n[:, None])).astype(f), jcol=np.arange(MAXTILES).astype(f),
        diff=np.maximum(diff, 0).astype(f), keep=(0.5 * (diff >= 0)).astype(f)), order


def halves(w):
    return np.ascontiguousarray(w.reshape(2, HD, *w.shape[1:]).swapaxes(0, 1))


def kernel(x, L0_tok_w_dw, L0_tok_b_dw, L0_tok_w_pw, L0_tok_b_pw, L0_tok_gamma, L0_tok_beta, L0_attn_log_slope,
           L0_attn_Wq, L0_attn_Wk, L0_attn_Wv, L0_attn_Wo, L0_attn_Wg1, L0_attn_Wg2, L0_attn_ln_w, L0_attn_ln_b,
           L0_ffn_Wg, L0_ffn_bg, L0_ffn_W1, L0_ffn_b1, L0_ffn_W2, L0_ffn_b2):
    import concourse.bacc as bacc
    from concourse.bass_utils import run_bass_kernel_spmd as run

    arrays, o = tables()
    g = np.asarray
    arrays |= dict(
        x=g(x), w_dw=halves(g(L0_tok_w_dw)[:, 0, :]), b_dw=halves(g(L0_tok_b_dw)),
        w_pw=halves(g(L0_tok_w_pw)[:, :, 0].T), b_pw=halves(g(L0_tok_b_pw)),
        rows=np.stack([g(v)[o] for v in (L0_tok_gamma, L0_tok_beta, L0_attn_ln_w, L0_attn_ln_b)]),
        w_q=halves(g(L0_attn_Wq)[o]), w_k=halves(g(L0_attn_Wk)[o]),
        w_vk=halves(np.concatenate([g(L0_attn_Wv), g(L0_attn_Wk)], 1)[o]),
        w_g1=halves(g(L0_attn_Wg1)[o]), w_g2=g(L0_attn_Wg2).reshape(G, NH, DH),
        w_o=g(L0_attn_Wo)[:, o].reshape(NG, 4, DH, D).transpose(1, 2, 0, 3),
        slope=g(L0_attn_log_slope), slope_c=halves(np.repeat(g(L0_attn_log_slope), DH)),
        w_r=halves(g(L0_ffn_Wg)[o]), bg=g(L0_ffn_bg),
        w1=g(L0_ffn_W1)[:, o].reshape(E, 2, HD, F).transpose(0, 2, 1, 3), b1=g(L0_ffn_b1),
        w2=g(L0_ffn_W2)[:, :, o].reshape(E, FC, 128, D).transpose(2, 0, 1, 3), b2=g(L0_ffn_b2)[:, o])
    nc = bacc.Bacc("TRN2", target_bir_lowering=False, num_devices=1)
    arrays = {f"in_{k}": np.ascontiguousarray(v) for k, v in arrays.items()}
    aps = {k[3:]: nc.dram_tensor(k, v.shape, mybir.dt.from_np(v.dtype), kind="ExternalInput").ap()
           for k, v in arrays.items()}
    out = nc.dram_tensor("out_rows", (B, S, D), mybir.dt.float32, kind="ExternalOutput").ap()
    build(nc, aps, out)
    got = run(nc, [arrays], core_ids=[0]).results[0]["out_rows"]
    return np.ascontiguousarray(got[:, :, np.argsort(o)])
```

```python
import numpy as np
import concourse.bass as bass
from concourse import mybir
from contextlib import ExitStack

B, S_IN, D, K = 8, 750, 192, 7
S = S_IN // 2
CH = 125
NC_ = S // CH
XT = S_IN // CH
HD = D // 2
NH, DH = 12, 16
HH = NH // 2
HG = 3
PH = 32
NG = 3
G = 16
NP, NQ = D // 2 + 1, D // 2 - 1
E, F = 8, 768
FC = F // 128
NT = B * NC_
TOK = B * S
REGION = 128 * (-(-(TOK + 127) // 128))
ROW = D + 2
MAXTILES = (2 * TOK + 127 * E) // 128
EMPTY = E * REGION
SKIP = 1.0e6
EPS = 1e-5
PAD = K // 2
POOL_CUT = (188, 187)


def channel_order():
    return np.array(list(range(NP)) + [D - c for c in range(1, NQ + 1)])


class Event:

    def __init__(self, sem, per=1):
        self.sem, self.per = sem, per

    def count(self, b, k=None):
        return b * self.per + (self.per if k is None else k + 1)


def first(b):
    return isinstance(b, int) and b == 0


def begun(b):
    return not (isinstance(b, int) and b < 0)


class Own:

    def __init__(self, sem, per):
        self.sem, self.per = sem, per

    def begin(self, b):
        self.base, self.n = b * self.per, 0

    def after(self, steps):
        self.n += steps
        return self.base + self.n

    def end(self):
        assert self.n == self.per, (self.n, self.per)


def build(nc, a, out):
    f32, i32 = mybir.dt.float32, mybir.dt.int32
    ALU, ACT, AX = mybir.AluOpType, mybir.ActivationFunctionType, mybir.AxisListType
    ds = bass.ds
    ctx = ExitStack()
    with ctx:
        def sb(name, shape, dt=f32):
            return ctx.enter_context(nc.sbuf_tensor(name, shape, dt))

        def event(name, per=1):
            return Event(ctx.enter_context(nc.semaphore(name)), per)

        def own(name, per):
            return Own(ctx.enter_context(nc.semaphore(name)), per)

        ident = sb("ident", [128, 128])
        dft_c = sb("dft_c", [HD, 2, D])
        cos_s = sb("cos_s", [CH, NC_, S])
        sin_s = sb("sin_s", [CH, NC_, S])
        w_dw = sb("w_dw", [HD, 2, K])
        b_dw = sb("b_dw", [HD, 2])
        w_pw = sb("w_pw", [HD, 2, D])
        b_pw = sb("b_pw", [HD, 2])
        rows = sb("rows", [CH, 4, D])
        w_q = sb("w_q", [HD, 2, D])
        w_k = sb("w_k", [HD, 2, D])
        w_vk = sb("w_vk", [HD, 2, 2 * D])
        w_g1 = sb("w_g1", [G, 2, HD])
        w_g = sb("w_g", [HD, 2, NH * PH])
        w_g2 = sb("w_g2", [G, NH, PH])
        w_o = sb("w_o", [128, NG, D])
        w_r = sb("w_r", [HD, 2, E])
        small = sb("small", [CH, 3, NC_, E])
        slope_t = sb("slope_t", [CH, NH])
        slope_c = sb("slope_c", [HD, 2])
        to_end = sb("to_end", [CH, 1])
        pos = sb("pos", [HD, CH])
        tri = sb("tri", [CH, CH])
        head_mask = sb("head_mask", [HD, HH, PH])
        tok2 = sb("tok2", [CH, NT])
        jcol = sb("jcol", [128, MAXTILES])
        ones = sb("ones", [128, 128])
        idle = sb("idle", [1, 3])
        eps = sb("eps", [CH, NC_])
        half_neg = sb("half_neg", [CH, NC_])
        diff_keep = sb("diff_keep", [CH, 2, CH])
        decay = sb("decay", [CH, NH, CH])
        k_decay = sb("k_decay", [CH, NH, DH])
        q_decay = sb("q_decay", [HD, 2, CH])
        carry = sb("carry", [HD, 2])
        fill = sb("fill", [128, ROW])
        w2 = sb("w2", [128, E, FC, D])

        x_rows = sb("x_rows", [CH, XT, D])
        xT = sb("xT", [HD, 2, S_IN + 2 * PAD])
        area = [sb(f"area_{p}", [128, 2 * F]) for p in range(2)]
        conv, pw = [t[0:HD, 0:2 * S_IN].rearrange("p (h s) -> p h s", h=2) for t in area]
        wide = sb("wide", [128, 2 * HH * S])
        pooled = sb("pooled", [HD, 2, S])
        chan = sb("chan", [CH, NC_, D])
        sine = sb("sine", [CH, NC_, NQ])
        y = sb("y", [CH, NC_, D])
        h1 = sb("h1", [CH, NC_, D])
        xn = sb("xn", [CH, NC_, D])
        stats = sb("stats", [CH, 4, NC_, 6])
        mv = sb("mv", [CH, 4, NC_, 2])
        vp = sb("vp", [CH, 4, NC_])
        rstd = sb("rstd", [CH, 4, NC_])
        xnT = sb("xnT", [HD, 2, S])
        qT = sb("qT", [HD, 2, S])
        kT = sb("kT", [HD, 2, S])
        q_block = wide[0:HD, :].rearrange("p (u h s) -> p u h s", u=2, h=HH)
        q_dec = sb("q_dec", [HD, 2, S - CH])
        v_pad = sb("v_pad", [CH, NC_, NH, PH])
        k_tok = sb("k_tok", [CH, NC_ - 1, D])
        k_dec = sb("k_dec", [CH, NC_ - 1, D])
        gate = sb("gate", [128, NG, S])
        deep = sb("deep", [128, NC_ * NH * CH])
        scores = deep[0:CH, :].rearrange("p (c h n) -> p c h n", c=NC_, h=NH)
        state = sb("state", [HD, NC_ - 1, 2, HH * PH])
        gated = sb("gated", [128, NG, S])
        resid = sb("resid", [CH, NT, D])
        o_ln = sb("o_ln", [CH, NC_, D])
        x2 = sb("x2", [CH, NC_, ROW])
        x2T = sb("x2T", [HD, 2, S])
        logit = sb("logit", [CH, NC_, E])
        logit2 = sb("logit2", [CH, NC_, E])
        hit = sb("hit", [CH, NC_, E])
        top = sb("top", [CH, 4, NC_])
        pick = sb("pick", [CH, 2, NC_, E])
        picked = sb("picked", [CH, NC_, E])
        row_of = sb("row_of", [CH, NC_, E])
        row_hit = sb("row_hit", [CH, 2, NC_, E])
        slots_f = sb("slots_f", [CH, 2, NC_])
        slots = sb("slots", [CH, 2, NC_], i32)
        counts = sb("counts", [CH, E])
        tile_sum = sb("tile_sum", [CH, E])
        gap = sb("gap", [CH, NT])
        n_f = sb("n_f", [128, E])
        n_i = sb("n_i", [128, 2, E], i32)
        nt_f = sb("nt_f", [128, E])
        end_f = sb("end_f", [128, E])
        cut = [0]

        def from_wide(n):
            cut[0] += n
            return wide[:, cut[0] - n:cut[0]]

        past, past_n = [from_wide(MAXTILES * E).rearrange("p (j e) -> p j e", e=E) for _ in range(2)]
        e_of = sb("e_of", [128, MAXTILES])
        tiles_before = sb("tiles_before", [128, MAXTILES])
        blk = sb("blk", [128, 3, MAXTILES])
        table = sb("table", [1, 2, MAXTILES], i32)
        fill_at = sb("fill_at", [1, E], i32)
        w1 = [t[0:HD + 1, :].rearrange("p (h f) -> p h f", h=2) for t in area]
        PAIR = 2 * NC_ * D
        at = 2 * PAIR
        b2_rows = deep[:, at:at + E * D].rearrange("p (e d) -> p e d", e=E)
        at += E * D
        xr = [deep[:, at + ROW * p:at + ROW * (p + 1)] for p in range(2)]
        pairs = [deep[0:CH, PAIR * p:PAIR * (p + 1)].rearrange("p (t e) -> p t e", t=NC_) for p in range(2)]
        xrT = [from_wide(256)[0:HD + 1].rearrange("p (h t) -> p h t", h=2) for _ in range(2)]
        hid = [from_wide(FC * 128).rearrange("p (c t) -> p c t", c=FC) for _ in range(2)]
        yo = [from_wide(D) for _ in range(2)]
        dest_f = sb("dest_f", [128, MAXTILES])
        dest = [sb(f"dest_{p}", [128, 1], i32) for p in range(2)]
        gates = sb("gates", [CH, 3, NT])

        ps = [ctx.enter_context(nc.psum_tensor(f"ps{i}", [128, 512], f32)) for i in range(8)]

        routed = nc.dram_tensor("routed", [EMPTY + 128, ROW], f32, kind="Internal").ap()
        by_pair = nc.dram_tensor("by_pair", [2 * TOK, D], f32, kind="Internal").ap()

        ident_in = event("ident_in", 16)
        in_a = event("in_a", 16 * 8)
        in_b = event("in_b", 16 * 6)
        in_c = event("in_c", 16 * 9)
        in_d = event("in_d", 16 * 6)
        wg_ps = event("wg_ps")
        wg_sb = event("wg_sb")
        w2_in = event("w2_in", 16)
        b2_in = event("b2_in", 16)
        empty_in = event("empty_in", 16)
        x_in = event("x_in", 16)
        zeroed = event("zeroed")
        zeroed_d = event("zeroed_d")
        tables = event("tables")
        tables_d = event("tables_d")
        xT_ps = event("xT_ps", 4)
        xT_sb = event("xT_sb", 4)
        conv_sb = event("conv_sb", 2)
        pw_ps = event("pw_ps", 4)
        pw_sb = event("pw_sb", 4)
        pooled_sb = event("pooled_sb", 2)
        chan_ps = event("chan_ps", 2)
        chan_sb = event("chan_sb", 2)
        sine_ps = event("sine_ps")
        sine_sb = event("sine_sb")
        cosine_ps = event("cosine_ps")
        y_sb = event("y_sb")
        var_sb = event("var_sb", 2)
        rstd_sb = event("rstd_sb", 2)
        h1_sb = event("h1_sb")
        xn_sb = event("xn_sb")
        hb_sb = event("hb_sb")
        xnT_ps = event("xnT_ps", 2)
        xnT_sb = event("xnT_sb", 2)
        q_ps = event("q_ps", 2)
        q_sb = event("q_sb", 2)
        k_ps = event("k_ps", 2)
        k_sb = event("k_sb", 2)
        vk_ps = event("vk_ps", NC_)
        vk_sb = event("vk_sb", NC_)
        g_ps = event("g_ps", NG)
        g_sb = event("g_sb", NG)
        qb_in = event("qb_in", 16 * NH)
        k_dec_sb = event("k_dec_sb")
        q_dec_sb = event("q_dec_sb")
        sc_ps = event("sc_ps", 4 * NC_)
        sc_sb = event("sc_sb", 4 * NC_)
        st_ps = event("st_ps", 2)
        st_sb = event("st_sb", 2)
        av_ps = event("av_ps", NC_)
        av_sb = event("av_sb", NC_)
        o_ps = event("o_ps", 2)
        o_free = event("o_free", NC_)
        cvar_sb = event("cvar_sb", 2)
        crstd_sb = event("crstd_sb", 2)
        x2_sb = event("x2_sb")
        x2T_ps = event("x2T_ps", 2)
        x2T_sb = event("x2T_sb", 2)
        lg_ps = event("lg_ps")
        lg_sb = event("lg_sb")
        pick_sb = event("pick_sb")
        rank_ps = event("rank_ps")
        rank_sb = event("rank_sb")
        slots_sb = event("slots_sb")
        counts_sb = event("counts_sb")
        scattered = event("scattered", 16 * 2 * NC_)
        own_conv = own("own_conv", 2 * (K - 1))
        own_ln = own("own_ln", 3)
        own_c = own("own_c", 18)
        own_st = own("own_st", 1)
        own_pa = own("own_pa", 2)
        own_pc = own("own_pc", 2)
        n_ps = event("n_ps")
        own_t = own("own_t", 16)
        table_sb = event("table_sb")
        filled = event("filled")
        row_in = [event(f"row_in{p}", 16) for p in range(2)]
        w1_in = [event(f"w1_in{p}", 32) for p in range(2)]
        dest_sb = event("dest_sb")
        xrT_ps = event("xrT_ps")
        xrT_sb = event("xrT_sb")
        hid_ps = event("hid_ps", 2)
        hid_a = event("hid_a")
        hid_b = event("hid_b")
        out_ps = event("out_ps")
        out_sb = event("out_sb")
        sent = [event(f"sent{p}", 16) for p in range(2)]
        idled = event("idled")
        exp_sb = event("exp_sb")
        own_g = own("own_g", 2)
        pair_in = [event(f"pair_in{p}", 16) for p in range(2)]
        mixed = event("mixed")
        own_m = own("own_m", 1)
        out_done = event("out_done", 16)

        block = ctx.enter_context(nc.Block())

        def apart(eng):
            if eng is nc.gpsimd:
                return nc.gpsimd.tensor_tensor(idle[0:1, 0:1], idle[0:1, 1:2], idle[0:1, 1:2], ALU.add)
            return nc.vector.memset(idle[0:1, 2:3], 0.0)

        RING_A = [(xT_sb, k) for k in range(4)] + [(pw_sb, k) for k in range(4)] + \
                 [(chan_sb, 0), (chan_sb, 1), (sine_sb, 0), (y_sb, 0)]
        RING_B = [(xnT_sb, 0), (xnT_sb, 1), (q_sb, 0), (q_sb, 1), (k_sb, 0), (k_sb, 1)] + \
                 [(vk_sb, k) for k in range(NC_)] + [(g_sb, k) for k in range(NG)] + \
                 [(sc_sb, k) for k in range(4 * NC_)] + [(st_sb, 0), (st_sb, 1)] + \
                 [(sc_sb, 4 * NC_ - 1)]
        RING_C = [(av_sb, k) for k in range(NC_)] + [(o_free, 1), (o_free, 2), (x2T_sb, 0), (x2T_sb, 1),
                                                     (lg_sb, 0), (rank_sb, 0)]
        RINGS = {"A": (RING_A, [0, 1]), "B": (RING_B, [2, 3, 4]), "C": (RING_C, [5, 6, 7])}
        AT = {"xT": 0, "pw": 4, "chan": 8, "sine": 10, "cosine": 11,
              "xnT": 0, "q": 2, "k": 4, "vk": 6, "g": 9, "sc": 12, "st": 24,
              "av": 0, "o": 3, "x2T": 5, "lg": 7, "rank": 8}
        assert all(len(r) % len(banks) == 0 for r, banks in RINGS.values())

        def bank(ring, group):
            return ps[RINGS[ring][1][group % len(RINGS[ring][1])]]

        def shared(ring, group, b):
            return group >= len(RINGS[ring][1]) or begun(b - 1)

        def drained(ring, group, b):
            groups, banks = RINGS[ring]
            before = group - len(banks)
            event_, k = groups[before]
            return event_.sem, event_.count(b if before >= 0 else b - 1, k)

        def pipeline(eng, run):
            run(0, None, None, None)
            run(1, 0, None, None)
            run(2, 1, 0, None)
            run(3, 2, 1, 0)
            with eng.Fori(2, B - 2) as b:
                run(b + 2, b + 1, b, b - 1)
            run(None, B - 1, B - 2, B - 3)
            run(None, None, B - 1, B - 2)
            run(None, None, None, B - 1)

        def tiles(eng, run):
            for j in range(4):
                run(j, j % 2, j // 2)
            with eng.Fori(2, MAXTILES // 2 - 1) as jj:
                for p in range(2):
                    run(jj * 2 + p, p, jj)
            for j in range(MAXTILES - 2, MAXTILES):
                run(j, j % 2, j // 2)

        def full(t):
            return t[tuple(slice(None) for _ in t.shape)]

        consts_a = [
            (w_dw, a["w_dw"]), (b_dw, a["b_dw"]), (w_pw, a["w_pw"]), (b_pw, a["b_pw"]),
            (dft_c, a["dft_c"]), (sin_s, a["sin_s"]), (cos_s, a["cos_s"]),
            (rows, a["rows"].partition_broadcast(CH))]
        consts_b = [
            (w_q, a["w_q"]), (w_k, a["w_k"]), (w_vk, a["w_vk"]), (w_g1, a["w_g1"]),
            (head_mask, a["head_mask"])]
        consts_b_padded = [(w_g2[:, :, 0:DH], a["w_g2"])]
        consts_d = [
            (slope_t, a["slope"].partition_broadcast(CH)), (slope_c, a["slope_c"]), (to_end, a["to_end"]),
            (pos, a["pos"].partition_broadcast(HD)), (diff_keep[:, 0], a["diff"]), (diff_keep[:, 1], a["keep"])]
        consts_c = [
            (w_r, a["w_r"]), (small, a["small"].partition_broadcast(CH)), (tri, a["tri"]), (tok2, a["tok2"]),
            (jcol, a["jcol"].partition_broadcast(128))] + [(w_o[PH * j:PH * j + DH], a["w_o"][j]) for j in range(4)]

        @block.sync
        def _(sp):
            def load_x(b):
                if begun(b - 1):
                    sp.wait_ge(xT_ps.sem, xT_ps.count(b - 1))
                sp.dma_start(x_rows[:, :, :], a["x"][ds(b, 1)].rearrange("o (t p) d -> p (o t) d", p=CH)
                             ).then_inc(x_in.sem, 16)

            load_x(0)
            for dst, src in consts_a:
                sp.dma_start(full(dst), src).then_inc(in_a.sem, 16)
            for dst, src in consts_b:
                sp.dma_start(full(dst), src).then_inc(in_b.sem, 16)
            sp.wait_ge(zeroed.sem, zeroed.count(0))
            for dst, src in consts_b_padded:
                sp.dma_start(dst, src).then_inc(in_b.sem, 16)
            for dst, src in consts_c:
                sp.dma_start(dst if isinstance(dst, bass.AP) else full(dst), src).then_inc(in_c.sem, 16)

            def run(x_, a_, b, c):
                if x_ is not None and not (isinstance(x_, int) and x_ == 0):
                    load_x(x_)
                if b is not None:
                    if begun(b - 1):
                        sp.wait_ge(sc_ps.sem, sc_ps.count(b - 1))
                    for h in range(NH):
                        half, hl = divmod(h, HH)
                        if hl == 0:
                            sp.wait_ge(q_sb.sem, q_sb.count(b, half))
                        sp.dma_start(q_block[DH * hl:DH * hl + DH, half, hl, :],
                                     qT[DH * hl:DH * hl + DH, half, :]).then_inc(qb_in.sem, 16)

            pipeline(sp, run)

            sp.wait_ge(table_sb.sem, table_sb.count(0))
            sp.dma_start(b2_rows, a["b2"].partition_broadcast(128)).then_inc(b2_in.sem, 16)
            sp.wait_ge(scattered.sem, scattered.count(B - 1))
            for e in range(E):
                at = sp.value_load(fill_at[0:1, e:e + 1], min_val=e * REGION, max_val=e * REGION + TOK)
                sp.dma_start(routed[ds(at, 128), :], fill[:, :]).then_inc(filled.sem, 16)
            sp.wait_ge(filled.sem, 16 * E)
            sp.wait_ge(empty_in.sem, empty_in.count(0))

            def load(j, p, jj):
                t = j - 2
                e = sp.value_load(table[0:1, 0, ds(j, 1)], min_val=0, max_val=E - 1)
                r = sp.value_load(table[0:1, 1, ds(j, 1)], min_val=0, max_val=EMPTY)
                if begun(t):
                    sp.wait_ge(xrT_ps.sem, xrT_ps.count(t))
                if begun(t):
                    sp.wait_ge(dest_sb.sem, dest_sb.count(t))
                sp.dma_start(xr[p][:, :], routed[ds(r, 128), :]).then_inc(row_in[p].sem, 16)
                if begun(t):
                    sp.wait_ge(hid_ps.sem, hid_ps.count(t))
                sp.dma_start(w1[p][0:HD, :, :], a["w1"][ds(e, 1)].rearrange("o p h f -> (o p) h f")
                             ).then_inc(w1_in[p].sem, 16)
                sp.dma_start(w1[p][HD:HD + 1, 0, :], a["b1"][ds(e, 1), :]).then_inc(w1_in[p].sem, 16)

            tiles(sp, load)

            for p in range(2):
                sp.wait_ge(sent[p].sem, sent[p].count(MAXTILES // 2 - 1))
            for b in range(B):
                if b >= 2:
                    if begun(b - 2):
                        sp.wait_ge(mixed.sem, mixed.count(b - 2))
                sp.dma_start(pairs[b % 2], by_pair[2 * S * b:2 * S * (b + 1), :].rearrange(
                    "(t p k) d -> p t (k d)", p=CH, k=2)).then_inc(pair_in[b % 2].sem, 16)

        @block.gpsimd
        def _(pool):
            for side in (slice(0, PAD), slice(PAD + S_IN, S_IN + 2 * PAD)):
                nc.gpsimd.memset(xT[:, :, side], 0.0)
            for t in (w_g2, w_o):
                last = nc.gpsimd.memset(full(t), 0.0)
            last.then_inc(zeroed.sem, 1)
            nc.gpsimd.memset(half_neg[:, :], -0.5)
            nc.gpsimd.memset(eps[:, :], EPS)
            nc.gpsimd.memset(idle[:, 1:2], 0.0)
            nc.gpsimd.memset(q_block[:, :, :, :], 0.0)
            nc.gpsimd.memset(v_pad[:, :, :, :], 0.0)
            nc.gpsimd.memset(counts[:, :], 0.0)
            nc.gpsimd.memset(ones[:, :], 1.0)
            nc.gpsimd.memset(fill[:, :], 0.0).then_inc(zeroed.sem, 1)
            pool.wait_ge(zeroed.sem, 2)
            nc.gpsimd.memset(fill[:, D:D + 1], SKIP).then_inc(zeroed.sem, 1)
            pool.wait_ge(zeroed.sem, 3)
            pool.dma_start(routed[EMPTY:EMPTY + 128, :], fill[:, :]).then_inc(empty_in.sem, 16)
            pool.dma_start(w2[:, :, :, :], a["w2"]).then_inc(w2_in.sem, 16)
            pool.wait_ge(in_a.sem, in_a.count(0))
            pool.wait_ge(tables.sem, 1)

            def inverse_std(own_, b, n, k, ready, done):
                pool.wait_ge(ready.sem, ready.count(b, k))
                nc.gpsimd.tensor_tensor(vp[:, n], mv[:, n, :, 1], eps[:, :], ALU.add).then_inc(own_.sem, 1)
                pool.wait_ge(own_.sem, own_.after(1))
                nc.gpsimd.tensor_tensor(rstd[:, n], vp[:, n], half_neg[:, :], ALU.pow).then_inc(done.sem, 1)

            def run(x_, a_, b, c):
                if c is not None:
                    own_pc.begin(c)
                    inverse_std(own_pc, c, 2, 0, cvar_sb, crstd_sb)
                    inverse_std(own_pc, c, 3, 1, cvar_sb, crstd_sb)
                    own_pc.end()
                if b is not None:
                    pool.wait_ge(q_sb.sem, q_sb.count(b))
                    if begun(b - 1):
                        pool.wait_ge(av_ps.sem, av_ps.count(b - 1))
                    nc.gpsimd.tensor_tensor(
                        q_dec[:, :, :].rearrange("p h (c n) -> p h c n", n=CH),
                        qT[:, :, CH:S].rearrange("p h (c n) -> p h c n", n=CH),
                        q_decay[:, :, :].unsqueeze(2).to_broadcast([HD, 2, NC_ - 1, CH]),
                        ALU.mult).then_inc(q_dec_sb.sem, 1)
                    pool.wait_ge(vk_sb.sem, vk_sb.count(b))
                    nc.gpsimd.tensor_tensor(
                        k_dec[:, :, :], k_tok[:, :, :],
                        k_decay[:, :, :].rearrange("p h d -> p (h d)").unsqueeze(1)
                        .to_broadcast([CH, NC_ - 1, D]), ALU.mult).then_inc(k_dec_sb.sem, 1)
                if c is not None:
                    pool.wait_ge(slots_sb.sem, slots_sb.count(c))
                    apart(pool)
                    for k in range(2):
                        for i in range(NC_):
                            nc.gpsimd.indirect_dma_start(
                                routed, bass.IndirectOffsetOnAxis(ap=slots[:, k, i:i + 1], axis=0),
                                x2[:, i, :], None).then_inc(scattered.sem, 16)
                if a_ is not None:
                    own_pa.begin(a_)
                    inverse_std(own_pa, a_, 0, 0, var_sb, rstd_sb)
                    inverse_std(own_pa, a_, 1, 1, var_sb, rstd_sb)
                    own_pa.end()
                    pool.wait_ge(h1_sb.sem, h1_sb.count(a_))
                    nc.gpsimd.tensor_tensor(
                        resid[:, ds(a_ * NC_, NC_), :], h1[:, :, :],
                        rows[:, 3, :].unsqueeze(1).to_broadcast([CH, NC_, D]), ALU.add
                    ).then_inc(hb_sb.sem, 1)

            pipeline(pool, run)

            def send(j, p, jj):
                pool.wait_ge(out_sb.sem, out_sb.count(j))
                if begun(j - 1):
                    pool.wait_ge(idled.sem, idled.count(j - 1))
                apart(pool).then_inc(idled.sem, 1)
                nc.gpsimd.indirect_dma_start(
                    by_pair, bass.IndirectOffsetOnAxis(ap=dest[p][:, 0:1], axis=0), yo[p][:, :], None,
                    bounds_check=last_row, oob_is_err=False).then_inc(sent[p].sem, 16)

            pool.wait_ge(table_sb.sem, table_sb.count(0))
            for p in range(2):
                last = nc.gpsimd.memset(xrT[p][HD:HD + 1, 0, :], 1.0)
            last.then_inc(zeroed.sem, 1)
            last_row = pool.to_reg(2 * TOK - 1)
            tiles(pool, send)

        @block.scalar
        def _(act):
            act.dma_start(ident[:, :], a["ident"]).then_inc(ident_in.sem, 16)
            for dst, src in consts_d:
                act.dma_start(dst if isinstance(dst, bass.AP) else full(dst), src).then_inc(in_d.sem, 16)

            def decay_tables():
                act.wait_ge(in_d.sem, in_d.count(0))
                for h in range(NH):
                    nc.scalar.activation(decay[:, h, :], diff_keep[:, 0], ACT.Exp, scale=slope_t[:, h:h + 1])
                nc.scalar.activation(k_decay[:, :, :], slope_t[:, :].unsqueeze(2).to_broadcast([CH, NH, DH]),
                                     ACT.Exp, scale=to_end[:, 0:1])
                for half in range(2):
                    nc.scalar.activation(q_decay[:, half], pos[:, :], ACT.Exp, scale=slope_c[:, half:half + 1])
                nc.scalar.activation(carry[:, :], slope_c[:, :], ACT.Exp, scale=float(CH)
                                     ).then_inc(tables.sem, 1)

            def gate_weights():
                act.wait_ge(wg_ps.sem, wg_ps.count(0))
                for half in range(2):
                    last = nc.scalar.activation(w_g[:, half], ps[2 + half][0:HD, 0:NH * PH], ACT.Copy)
                last.then_inc(wg_sb.sem, 1)

            def run(x_, a_, b, c):
                if first(a_):
                    decay_tables()
                    act.wait_ge(in_a.sem, in_a.count(0))
                if first(b):
                    gate_weights()
                    act.wait_ge(zeroed.sem, 3)
                if b is not None:
                    for half in range(2):
                        act.wait_ge(xnT_ps.sem, xnT_ps.count(b, half))
                        if half == 0:
                            if begun(b - 1):
                                act.wait_ge(g_ps.sem, g_ps.count(b - 1))
                        nc.scalar.activation(xnT[:, half], bank("B", AT["xnT"] + half)[0:HD, 0:S],
                                             ACT.Copy).then_inc(xnT_sb.sem, 1)
                    for half in range(2):
                        act.wait_ge(q_ps.sem, q_ps.count(b, half))
                        if half == 0:
                            if begun(b - 1):
                                act.wait_ge(qb_in.sem, qb_in.count(b - 1))
                            if begun(b - 1):
                                act.wait_ge(q_dec_sb.sem, q_dec_sb.count(b - 1))
                        nc.scalar.activation(qT[:, half], bank("B", AT["q"] + half)[0:HD, 0:S],
                                             ACT.Silu).then_inc(q_sb.sem, 1)
                    for half in range(2):
                        act.wait_ge(k_ps.sem, k_ps.count(b, half))
                        if half == 0:
                            if begun(b - 1):
                                act.wait_ge(sc_ps.sem, sc_ps.count(b - 1))
                        nc.scalar.activation(kT[:, half], bank("B", AT["k"] + half)[0:HD, 0:S],
                                             ACT.Silu).then_inc(k_sb.sem, 1)
                    for i in range(NC_):
                        act.wait_ge(vk_ps.sem, vk_ps.count(b, i))
                        if i == 0:
                            if begun(b - 1):
                                act.wait_ge(av_ps.sem, av_ps.count(b - 1))
                            if begun(b - 1):
                                act.wait_ge(k_dec_sb.sem, k_dec_sb.count(b - 1))
                        src = bank("B", AT["vk"] + i)
                        last = nc.scalar.activation(v_pad[:, i, :, 0:DH],
                                                    src[0:CH, 0:D].rearrange("p (h d) -> p h d", d=DH), ACT.Silu)
                        if i < NC_ - 1:
                            last = nc.scalar.activation(k_tok[:, i], src[0:CH, D:2 * D], ACT.Silu)
                        last.then_inc(vk_sb.sem, 1)
                if c is not None:
                    for half in range(2):
                        act.wait_ge(x2T_ps.sem, x2T_ps.count(c, half))
                        if half == 0:
                            if begun(c - 1):
                                act.wait_ge(lg_ps.sem, lg_ps.count(c - 1))
                        nc.scalar.activation(x2T[:, half], bank("C", AT["x2T"] + half)[0:HD, 0:S],
                                             ACT.Copy).then_inc(x2T_sb.sem, 1)
                if b is not None:
                    for g in range(NG):
                        act.wait_ge(g_ps.sem, g_ps.count(b, g))
                        if g == 0:
                            if begun(b - 1):
                                act.wait_ge(av_sb.sem, av_sb.count(b - 1))
                        nc.scalar.activation(gate[:, g], bank("B", AT["g"] + g)[:, 0:S], ACT.Tanh,
                                             scale=0.5).then_inc(g_sb.sem, 1)
                if a_ is not None:
                    for g in range(4):
                        u, half = divmod(g, 2)
                        lo = 2 * POOL_CUT[0] * u
                        n = 2 * POOL_CUT[u]
                        act.wait_ge(pw_ps.sem, pw_ps.count(a_, g))
                        if g == 0:
                            if begun(a_ - 1):
                                act.wait_ge(pooled_sb.sem, pooled_sb.count(a_ - 1))
                        nc.scalar.activation(pw[:, half, lo:lo + n], bank("A", AT["pw"] + g)[0:HD, 0:n],
                                             ACT.Relu, bias=b_pw[:, half:half + 1]).then_inc(pw_sb.sem, 1)
                    for g, (lo, n) in enumerate(((0, 2), (2, 1))):
                        act.wait_ge(chan_ps.sem, chan_ps.count(a_, g))
                        if g == 0:
                            if begun(a_ - 1):
                                act.wait_ge(cosine_ps.sem, cosine_ps.count(a_ - 1))
                        nc.scalar.activation(
                            chan[:, lo:lo + n, :], bank("A", AT["chan"] + g)[0:CH, 0:n * D].rearrange(
                                "p (t d) -> p t d", d=D), ACT.Copy).then_inc(chan_sb.sem, 1)
                    act.wait_ge(sine_ps.sem, sine_ps.count(a_))
                    if begun(a_ - 1):
                        act.wait_ge(y_sb.sem, y_sb.count(a_ - 1))
                    nc.scalar.activation(
                        sine[:, :, :], bank("A", AT["sine"])[0:CH, 0:NC_ * NQ].rearrange(
                            "p (t d) -> p t d", d=NQ), ACT.Copy).then_inc(sine_sb.sem, 1)
                if x_ is not None:
                    for g in range(4):
                        half, u = divmod(g, 2)
                        act.wait_ge(xT_ps.sem, xT_ps.count(x_, g))
                        if begun(x_ - 1):
                            act.wait_ge(conv_sb.sem, conv_sb.count(x_ - 1, half))
                        nc.scalar.activation(
                            xT[:, half, PAD + S * u:PAD + S * (u + 1)], bank("A", AT["xT"] + g)[0:HD, 0:S],
                            ACT.Copy).then_inc(xT_sb.sem, 1)

            pipeline(act, run)

            act.wait_ge(slots_sb.sem, slots_sb.count(B - 1))
            nc.scalar.activation(gates[:, 0], gap[:, :], ACT.Exp).then_inc(exp_sb.sem, 1)

            def row_tile(j, p):
                act.wait_ge(xrT_ps.sem, xrT_ps.count(j))
                if begun(j - 2):
                    act.wait_ge(hid_ps.sem, hid_ps.count(j - 2))
                nc.scalar.activation(xrT[p][0:HD], ps[p][0:HD, 0:256].rearrange("p (h t) -> p h t", h=2),
                                     ACT.Copy).then_inc(xrT_sb.sem, 1)

            def hidden(j, p):
                act.wait_ge(hid_ps.sem, hid_ps.count(j, 0))
                if begun(j - 2):
                    act.wait_ge(out_ps.sem, out_ps.count(j - 2))
                nc.scalar.activation(hid[p][:, 0:4], ps[2 + 2 * p][:, :].rearrange("p (c t) -> p c t", c=4),
                                     ACT.Relu).then_inc(hid_a.sem, 1)

            row_tile(0, 0)
            row_tile(1, 1)

            def act_tile(j, p, jj):
                hidden(j, p)
                if not (isinstance(j, int) and j >= MAXTILES - 2):
                    row_tile(j + 2, p)

            tiles(act, act_tile)
            for b in range(B):
                act.wait_ge(mixed.sem, mixed.count(b))
                act.dma_start(out[b].rearrange("(t p) d -> p t d", p=CH), resid[:, NC_ * b:NC_ * (b + 1), :]
                              ).then_inc(out_done.sem, 16)
            act.wait_ge(out_done.sem, 16 * B)

        @block.vector
        def _(dve):
            def causal_decay():
                dve.wait_ge(in_d.sem, in_d.count(0))
                dve.wait_ge(tables.sem, tables.count(0))
                nc.vector.tensor_tensor(decay[:, :, :], decay[:, :, :],
                                        diff_keep[:, 1:2].to_broadcast([CH, NH, CH]), ALU.mult
                                        ).then_inc(tables_d.sem, 1)
                dve.wait_ge(tables_d.sem, tables_d.count(0))

            def layernorm_stats(own_, b, n, k, src, done):
                apart(dve)
                for i in range(NC_):
                    last = nc.vector.bn_stats(stats[:, n, i], src(i))
                last.then_inc(own_.sem, 1)
                dve.wait_ge(own_.sem, own_.after(1))
                apart(dve)
                for i in range(NC_):
                    last = nc.vector.bn_aggr(mv[:, n, i], stats[:, n, i])
                last.then_inc(done.sem, 1)

            def norms_a(b):
                own_ln.begin(b)
                layernorm_stats(own_ln, b, 0, 0, lambda i: y[:, i], var_sb)
                dve.wait_ge(var_sb.sem, var_sb.count(b, 0))
                for i in range(NC_):
                    last = nc.vector.scalar_tensor_tensor(y[:, i], y[:, i], mv[:, 0, i, 0:1], rows[:, 0],
                                                          ALU.subtract, ALU.mult)
                last.then_inc(own_ln.sem, 1)
                after_centre = own_ln.after(1)
                yield
                dve.wait_ge(rstd_sb.sem, rstd_sb.count(b, 0))
                if begun(b - 1):
                    dve.wait_ge(hb_sb.sem, hb_sb.count(b - 1))
                dve.wait_ge(own_ln.sem, after_centre)
                for i in range(NC_):
                    last = nc.vector.scalar_tensor_tensor(h1[:, i], y[:, i], rstd[:, 0, i:i + 1], rows[:, 1],
                                                          ALU.mult, ALU.add)
                last.then_inc(h1_sb.sem, 1)
                dve.wait_ge(h1_sb.sem, h1_sb.count(b))
                layernorm_stats(own_ln, b, 1, 1, lambda i: h1[:, i], var_sb)
                yield
                dve.wait_ge(var_sb.sem, var_sb.count(b, 1))
                dve.wait_ge(rstd_sb.sem, rstd_sb.count(b, 1))
                if begun(b - 1):
                    dve.wait_ge(xnT_ps.sem, xnT_ps.count(b - 1))
                for i in range(NC_):
                    last = nc.vector.tensor_scalar(xn[:, i], h1[:, i], mv[:, 1, i, 0:1], rstd[:, 1, i:i + 1],
                                                   ALU.subtract, ALU.mult)
                last.then_inc(xn_sb.sem, 1)
                own_ln.end()

            def norms_c(c):
                own_c.begin(c)
                at = c * NC_

                def o(i):
                    g, k = (0, i) if i < 2 else (1, 0)
                    return bank("C", AT["o"] + g)[0:CH, k * D:(k + 1) * D]
                dve.wait_ge(o_ps.sem, o_ps.count(c))
                layernorm_stats(own_c, c, 2, 0, o, cvar_sb)
                dve.wait_ge(cvar_sb.sem, cvar_sb.count(c, 0))
                for i in range(NC_):
                    nc.vector.scalar_tensor_tensor(o_ln[:, i], o(i), mv[:, 2, i, 0:1], rows[:, 2],
                                                   ALU.subtract, ALU.mult).then_inc(o_free.sem, 1)
                yield
                dve.wait_ge(o_free.sem, o_free.count(c))
                dve.wait_ge(crstd_sb.sem, crstd_sb.count(c, 0))
                dve.wait_ge(hb_sb.sem, hb_sb.count(c))
                for i in range(NC_):
                    last = nc.vector.scalar_tensor_tensor(
                        resid[:, ds(at + i, 1), :], o_ln[:, i:i + 1], rstd[:, 2, i:i + 1],
                        resid[:, ds(at + i, 1), :], ALU.mult, ALU.add)
                last.then_inc(own_c.sem, 1)
                dve.wait_ge(own_c.sem, own_c.after(1))
                layernorm_stats(own_c, c, 3, 1, lambda i: resid[:, ds(at + i, 1), :].rearrange("p o d -> p (o d)"), cvar_sb)
                yield
                dve.wait_ge(cvar_sb.sem, cvar_sb.count(c, 1))
                dve.wait_ge(crstd_sb.sem, crstd_sb.count(c, 1))
                if begun(c - 1):
                    dve.wait_ge(x2T_ps.sem, x2T_ps.count(c - 1))
                if begun(c - 1):
                    dve.wait_ge(scattered.sem, scattered.count(c - 1))
                for i in range(NC_):
                    last = nc.vector.tensor_scalar(x2[:, i:i + 1, 0:D], resid[:, ds(at + i, 1), :],
                                                   mv[:, 3, i, 0:1], rstd[:, 3, i:i + 1],
                                                   ALU.subtract, ALU.mult)
                last.then_inc(x2_sb.sem, 1)

            def convolve(b):
                own_conv.begin(b)
                for half in range(2):
                    dve.wait_ge(xT_sb.sem, xT_sb.count(b, 2 * half + 1))
                    if half == 0:
                        if begun(b - 1):
                            dve.wait_ge(pw_ps.sem, pw_ps.count(b - 1))
                    for k in range(K):
                        tap = xT[:, half, k:k + S_IN]
                        if k == 0:
                            ins = nc.vector.tensor_scalar(conv[:, half], tap, w_dw[:, half, 0:1],
                                                          b_dw[:, half:half + 1], ALU.mult, ALU.add)
                        else:
                            dve.wait_ge(own_conv.sem, own_conv.after(1))
                            ins = nc.vector.scalar_tensor_tensor(conv[:, half], tap, w_dw[:, half, k:k + 1],
                                                                 conv[:, half], ALU.mult, ALU.add)
                        ins.then_inc(own_conv.sem if k < K - 1 else conv_sb.sem, 1)
                        if (half, k) != (1, K - 1):
                            yield
                own_conv.end()

            def choose(c):
                one, two_ = pick[:, 0], pick[:, 1]
                def bc(x):
                    return x.unsqueeze(2).to_broadcast([CH, NC_, E])
                dve.wait_ge(lg_ps.sem, lg_ps.count(c))
                if begun(c - 1):
                    dve.wait_ge(rank_ps.sem, rank_ps.count(c - 1))
                if begun(c - 1):
                    dve.wait_ge(slots_sb.sem, slots_sb.count(c - 1))
                nc.vector.tensor_tensor(logit[:, :, :], bank("C", AT["lg"])[0:CH, 0:NC_ * E].rearrange(
                    "p (t e) -> p t e", e=E), small[:, 0], ALU.add).then_inc(lg_sb.sem, 1)
                yield
                dve.wait_ge(lg_sb.sem, lg_sb.count(c))
                nc.vector.tensor_reduce(top[:, 0], logit[:, :, :], AX.X, ALU.max).then_inc(own_c.sem, 1)
                done = own_c.after(1)
                yield
                dve.wait_ge(own_c.sem, done)
                nc.vector.tensor_tensor(hit[:, :, :], logit[:, :, :], bc(top[:, 0]), ALU.is_equal).then_inc(own_c.sem, 1)
                done = own_c.after(1)
                yield
                dve.wait_ge(own_c.sem, done)
                nc.vector.tensor_tensor(hit[:, :, :], hit[:, :, :], small[:, 1], ALU.mult).then_inc(own_c.sem, 1)
                done = own_c.after(1)
                yield
                dve.wait_ge(own_c.sem, done)
                nc.vector.tensor_reduce(top[:, 1], hit[:, :, :], AX.X, ALU.max).then_inc(own_c.sem, 1)
                done = own_c.after(1)
                yield
                dve.wait_ge(own_c.sem, done)
                nc.vector.tensor_tensor(one, small[:, 1], bc(top[:, 1]), ALU.is_equal).then_inc(own_c.sem, 1)
                done = own_c.after(1)
                yield
                dve.wait_ge(own_c.sem, done)
                nc.vector.scalar_tensor_tensor(logit2[:, :, :], one, -3.0e38, logit[:, :, :],
                                                          ALU.mult, ALU.add).then_inc(own_c.sem, 1)
                done = own_c.after(1)
                yield
                dve.wait_ge(own_c.sem, done)
                nc.vector.tensor_reduce(top[:, 2], logit2[:, :, :], AX.X, ALU.max).then_inc(own_c.sem, 1)
                done = own_c.after(1)
                yield
                dve.wait_ge(own_c.sem, done)
                nc.vector.tensor_tensor(hit[:, :, :], logit2[:, :, :], bc(top[:, 2]), ALU.is_equal).then_inc(own_c.sem, 1)
                done = own_c.after(1)
                yield
                dve.wait_ge(own_c.sem, done)
                nc.vector.tensor_tensor(hit[:, :, :], hit[:, :, :], small[:, 1], ALU.mult).then_inc(own_c.sem, 1)
                done = own_c.after(1)
                yield
                dve.wait_ge(own_c.sem, done)
                nc.vector.tensor_reduce(top[:, 3], hit[:, :, :], AX.X, ALU.max).then_inc(own_c.sem, 1)
                done = own_c.after(1)
                yield
                dve.wait_ge(own_c.sem, done)
                nc.vector.tensor_tensor(two_, small[:, 1], bc(top[:, 3]), ALU.is_equal).then_inc(own_c.sem, 1)
                done = own_c.after(1)
                yield
                dve.wait_ge(own_c.sem, done)
                nc.vector.tensor_tensor(picked[:, :, :], one, two_, ALU.add).then_inc(pick_sb.sem, 1)
                nc.vector.tensor_tensor(gap[:, ds(c * NC_, NC_)], top[:, 2], top[:, 0], ALU.subtract)
                nc.vector.tensor_copy(x2[:, :, D:D + 1], tok2[:, ds(c * NC_, NC_)].unsqueeze(2))
                nc.vector.tensor_scalar(x2[:, :, D + 1:D + 2], top[:, 1].unsqueeze(2), -1.0, float(E),
                                                   ALU.mult, ALU.add).then_inc(own_c.sem, 1)

            def place(c):
                dve.wait_ge(rank_ps.sem, rank_ps.count(c))
                nc.vector.tensor_tensor(row_of[:, :, :], bank("C", AT["rank"])[0:CH, 0:NC_ * E].rearrange(
                    "p (t e) -> p t e", e=E), small[:, 2], ALU.add).then_inc(rank_sb.sem, 1)
                nc.vector.tensor_reduce(tile_sum[:, :], picked[:, :, :].rearrange("p t e -> p e t"),
                                                   AX.X, ALU.add).then_inc(own_c.sem, 1)
                dve.wait_ge(rank_sb.sem, rank_sb.count(c))
                dve.wait_ge(own_c.sem, own_c.after(2))
                nc.vector.tensor_tensor(
                    row_hit[:, :, :, :], pick[:, :, :, :],
                    row_of[:, :, :].unsqueeze(1).to_broadcast([CH, 2, NC_, E]), ALU.mult).then_inc(own_c.sem, 1)
                nc.vector.tensor_tensor(counts[:, :], counts[:, :], tile_sum[:, :], ALU.add
                                        ).then_inc(counts_sb.sem, 1)
                dve.wait_ge(own_c.sem, own_c.after(1))
                nc.vector.tensor_reduce(slots_f[:, :, :], row_hit[:, :, :, :], AX.X, ALU.add).then_inc(own_c.sem, 1)
                dve.wait_ge(own_c.sem, own_c.after(1))
                nc.vector.tensor_copy(slots[:, :, :], slots_f[:, :, :]).then_inc(slots_sb.sem, 1)
                own_c.end()

            def apply_decay(b, g):
                i, h0 = g // 4, HG * (g % 4)
                dve.wait_ge(sc_ps.sem, sc_ps.count(b, g))
                if g == 0:
                    if begun(b - 1):
                        dve.wait_ge(av_ps.sem, av_ps.count(b - 1))
                nc.vector.tensor_tensor(
                    scores[:, i, h0:h0 + HG], bank("B", AT["sc"] + g)[0:CH, 0:HG * CH].rearrange(
                        "p (h n) -> p h n", n=CH), decay[:, h0:h0 + HG], ALU.mult
                ).then_inc(sc_sb.sem, 1)

            def pool_pairs(a_):
                for u in range(2):
                    lo = POOL_CUT[0] * u
                    dve.wait_ge(pw_sb.sem, pw_sb.count(a_, 2 * u + 1))
                    if u == 0:
                        if begun(a_ - 1):
                            dve.wait_ge(chan_ps.sem, chan_ps.count(a_ - 1))
                    v = pw[:, :, 2 * lo:2 * (lo + POOL_CUT[u])].rearrange("p h (s t) -> p h s t", t=2)
                    nc.vector.tensor_tensor(pooled[:, :, lo:lo + POOL_CUT[u]], v[:, :, :, 0], v[:, :, :, 1],
                                            ALU.max).then_inc(pooled_sb.sem, 1)

            def keep_state(b, i):
                dve.wait_ge(st_ps.sem, st_ps.count(b, i))
                ins = nc.vector.tensor_tensor(
                    state[:, i], bank("B", AT["st"] + i)[0:HD, 0:2 * HH * PH].rearrange("p (h s) -> p h s", h=2),
                    head_mask[:, :, :].rearrange("p h s -> p (h s)").unsqueeze(1).to_broadcast([HD, 2, HH * PH]),
                    ALU.mult)
                if i == 0:
                    ins.then_inc(st_sb.sem, 1)
                else:
                    own_st.begin(b)
                    ins.then_inc(own_st.sem, 1)
                    dve.wait_ge(own_st.sem, own_st.after(1))
                    own_st.end()
                    dve.wait_ge(st_sb.sem, st_sb.count(b, 0))
                    for half in range(2):
                        ins = nc.vector.scalar_tensor_tensor(
                            state[:, i, half], state[:, i - 1, half], carry[:, half:half + 1],
                            state[:, i, half], ALU.mult, ALU.add)
                    ins.then_inc(st_sb.sem, 1)

            def apply_gate(b, i):
                dve.wait_ge(av_ps.sem, av_ps.count(b, i))
                if i == 0:
                    dve.wait_ge(g_sb.sem, g_sb.count(b))
                    if begun(b - 1):
                        dve.wait_ge(o_ps.sem, o_ps.count(b - 1))
                nc.vector.scalar_tensor_tensor(
                    gated[:, :, CH * i:CH * (i + 1)], gate[:, :, CH * i:CH * (i + 1)], 1.0,
                    bank("C", AT["av"] + i)[:, 0:NG * CH].rearrange("p (g n) -> p g n", n=CH),
                    ALU.add, ALU.mult).then_inc(av_sb.sem, 1)

            def spectrum(a_):
                dve.wait_ge(sine_sb.sem, sine_sb.count(a_))
                dve.wait_ge(cosine_ps.sem, cosine_ps.count(a_))
                p_ = bank("A", AT["cosine"])[0:CH, 0:NC_ * NP].rearrange("p (t d) -> p t d", d=NP)
                nc.vector.tensor_copy(y[:, :, 0:NP:NP - 1], p_[:, :, 0:NP:NP - 1])
                nc.vector.tensor_tensor(y[:, :, 1:NP - 1], p_[:, :, 1:NP - 1], sine[:, :, :], ALU.subtract)
                nc.vector.tensor_tensor(y[:, :, NP:D], p_[:, :, 1:NP - 1], sine[:, :, :], ALU.add
                                        ).then_inc(y_sb.sem, 1)
                dve.wait_ge(y_sb.sem, y_sb.count(a_))

            def run(x_, a_, b, c):
                if first(a_):
                    dve.wait_ge(in_a.sem, in_a.count(0))
                    dve.wait_ge(zeroed.sem, 1)
                if first(b):
                    dve.wait_ge(in_b.sem, in_b.count(0))
                    causal_decay()
                if first(c):
                    dve.wait_ge(in_c.sem, in_c.count(0))
                    dve.wait_ge(zeroed.sem, 3)
                norming = norms_c(c) if c is not None else iter(())
                tapping = convolve(a_) if a_ is not None else iter(())
                next(norming, None)
                for _ in range(2):
                    next(tapping, None)
                next(norming, None)
                for _ in range(2):
                    next(tapping, None)
                next(norming, None)
                for _ in tapping:
                    pass
                choosing = choose(c) if c is not None else iter(())
                if b is not None:
                    for g in range(4 * NC_):
                        apply_decay(b, g)
                        next(choosing, None)
                for _ in choosing:
                    pass
                if c is not None:
                    place(c)
                if a_ is not None:
                    pool_pairs(a_)
                if b is not None:
                    keep_state(b, 0)
                    apply_gate(b, 0)
                    keep_state(b, 1)
                    apply_gate(b, 1)
                norming = norms_a(a_) if a_ is not None else iter(())
                if a_ is not None:
                    spectrum(a_)
                next(norming, None)
                if b is not None:
                    apply_gate(b, 2)
                for _ in norming:
                    pass

            pipeline(dve, run)

            own_t.begin(0)

            dve.wait_ge(n_ps.sem, n_ps.count(0))
            nc.vector.tensor_copy(n_f[:, :], ps[0][:, 0:E]).then_inc(own_t.sem, 1)
            dve.wait_ge(own_t.sem, own_t.after(1))
            nc.vector.tensor_scalar(n_i[:, 0], n_f[:, :], 127.0, None, ALU.add).then_inc(own_t.sem, 1)
            dve.wait_ge(own_t.sem, own_t.after(1))
            nc.vector.tensor_scalar(n_i[:, 1], n_i[:, 0], 7, None, ALU.logical_shift_right).then_inc(own_t.sem, 1)
            dve.wait_ge(own_t.sem, own_t.after(1))
            nc.vector.tensor_copy(nt_f[:, :], n_i[:, 1]).then_inc(own_t.sem, 1)
            dve.wait_ge(own_t.sem, own_t.after(1))
            nc.vector.tensor_tensor_scan(end_f[:, :], ones[:, 0:E], nt_f[:, :], 0.0, ALU.mult, ALU.add).then_inc(own_t.sem, 1)
            dve.wait_ge(own_t.sem, own_t.after(1))
            j8 = jcol[:, :].unsqueeze(2).to_broadcast([128, MAXTILES, E])
            nc.vector.tensor_tensor(past[:, :, :], j8, end_f[:, :].unsqueeze(1).to_broadcast([128, MAXTILES, E]),
                                    ALU.is_ge).then_inc(own_t.sem, 1)
            dve.wait_ge(own_t.sem, own_t.after(1))
            nc.vector.tensor_tensor(past_n[:, :, :], past[:, :, :],
                                    nt_f[:, :].unsqueeze(1).to_broadcast([128, MAXTILES, E]), ALU.mult).then_inc(own_t.sem, 1)
            dve.wait_ge(own_t.sem, own_t.after(1))
            nc.vector.tensor_reduce(e_of[:, :], past[:, :, 0:E - 1], AX.X, ALU.add).then_inc(own_t.sem, 1)
            dve.wait_ge(own_t.sem, own_t.after(1))
            nc.vector.tensor_reduce(tiles_before[:, :], past_n[:, :, 0:E - 1], AX.X, ALU.add).then_inc(own_t.sem, 1)
            dve.wait_ge(own_t.sem, own_t.after(1))
            nc.vector.scalar_tensor_tensor(blk[:, 0], e_of[:, :], float(REGION // 128), jcol[:, :],
                                           ALU.mult, ALU.add).then_inc(own_t.sem, 1)
            dve.wait_ge(own_t.sem, own_t.after(1))
            nc.vector.tensor_tensor(blk[:, 0], blk[:, 0], tiles_before[:, :], ALU.subtract).then_inc(own_t.sem, 1)
            dve.wait_ge(own_t.sem, own_t.after(1))
            nc.vector.tensor_scalar(blk[:, 1], blk[:, 0], -1.0, float(EMPTY // 128), ALU.mult, ALU.add).then_inc(own_t.sem, 1)
            dve.wait_ge(own_t.sem, own_t.after(1))
            nc.vector.tensor_tensor(blk[:, 1], blk[:, 1], past[:, :, E - 1], ALU.mult).then_inc(own_t.sem, 1)
            dve.wait_ge(own_t.sem, own_t.after(1))
            nc.vector.tensor_tensor(blk[:, 2], blk[:, 1], blk[:, 0], ALU.add).then_inc(own_t.sem, 1)
            dve.wait_ge(own_t.sem, own_t.after(1))
            nc.vector.tensor_scalar(table[0:1, 1], blk[0:1, 2], 128.0, None, ALU.mult).then_inc(own_t.sem, 1)
            dve.wait_ge(own_t.sem, own_t.after(1))
            nc.vector.tensor_copy(table[0:1, 0], e_of[0:1, :]).then_inc(own_t.sem, 1)
            dve.wait_ge(own_t.sem, own_t.after(1))
            own_t.end()
            nc.vector.tensor_tensor(fill_at[0:1, :], n_f[0:1, :], small[0:1, 2, 0], ALU.add
                                    ).then_inc(table_sb.sem, 1)
            dve.wait_ge(table_sb.sem, table_sb.count(0))
            dve.wait_ge(exp_sb.sem, exp_sb.count(0))
            own_g.begin(0)
            nc.vector.tensor_scalar(gates[:, 2], gates[:, 0], 1.0, None, ALU.add).then_inc(own_g.sem, 1)
            dve.wait_ge(own_g.sem, own_g.after(1))
            nc.vector.reciprocal(gates[:, 1], gates[:, 2]).then_inc(own_g.sem, 1)
            dve.wait_ge(own_g.sem, own_g.after(1))
            nc.vector.tensor_tensor(gates[:, 2], gates[:, 0], gates[:, 1], ALU.mult)
            own_g.end()
            dve.wait_ge(b2_in.sem, b2_in.count(0))

            def destination(j, p, jj):
                dve.wait_ge(row_in[p].sem, row_in[p].count(jj))
                nc.vector.scalar_tensor_tensor(dest_f[:, ds(j, 1)], xr[p][:, D + 1:D + 2], e_of[:, ds(j, 1)],
                                               xr[p][:, D:D + 1], ALU.not_equal, ALU.add
                                               ).then_inc(dest_sb.sem, 1)

            destination(0, 0, 0)
            destination(1, 1, 0)

            def dve_tile(j, p, jj):
                e = dve.value_load(table[0:1, 0, ds(j, 1)], min_val=0, max_val=E - 1)
                dve.wait_ge(hid_ps.sem, hid_ps.count(j, 1))
                if begun(j - 2):
                    dve.wait_ge(out_ps.sem, out_ps.count(j - 2))
                nc.vector.tensor_scalar(hid[p][:, 4:FC], ps[3 + 2 * p][:, 0:256].rearrange(
                    "p (c t) -> p c t", c=2), 0.0, None, ALU.max).then_inc(hid_b.sem, 1)
                if not (isinstance(j, int) and j >= MAXTILES - 2):
                    destination(j + 2, p, jj + 1)
                if begun(jj - 1):
                    dve.wait_ge(sent[p].sem, sent[p].count(jj - 1))
                dve.wait_ge(dest_sb.sem, dest_sb.count(j))
                nc.vector.tensor_copy(dest[p][:, :], dest_f[:, ds(j, 1)])
                dve.wait_ge(out_ps.sem, out_ps.count(j))
                nc.vector.tensor_tensor(yo[p][:, :], ps[6 + p][:, 0:D], b2_rows[:, ds(e, 1), :].rearrange(
                    "p o d -> p (o d)"), ALU.add).then_inc(out_sb.sem, 1)

            tiles(dve, dve_tile)

            for b in range(B):
                pr = pairs[b % 2]
                dve.wait_ge(pair_in[b % 2].sem, pair_in[b % 2].count(b // 2))
                own_m.begin(b)
                for k in range(2):
                    for i in range(NC_):
                        t = NC_ * b + i
                        last = nc.vector.scalar_tensor_tensor(resid[:, t], pr[:, i, D * k:D * (k + 1)],
                                                              gates[:, 1 + k, t:t + 1], resid[:, t], ALU.mult, ALU.add)
                    if k == 0:
                        last.then_inc(own_m.sem, 1)
                        dve.wait_ge(own_m.sem, own_m.after(1))
                own_m.end()
                last.then_inc(mixed.sem, 1)

        @block.tensor
        def _(pe):
            mm, tr = nc.tensor.matmul, nc.tensor.transpose

            def gate_weights():
                for half in range(2):
                    last = mm(ps[2 + half][0:HD, 0:NH * PH], w_g1[:, half, :],
                              w_g2[:, :, :].rearrange("p h d -> p (h d)"), start=True, stop=True)
                last.then_inc(wg_ps.sem, 1)
                pe.wait_ge(wg_sb.sem, wg_sb.count(0))

            def transpose_x(b):
                pe.wait_ge(x_in.sem, x_in.count(b))
                for g in range(4):
                    half, u = divmod(g, 2)
                    if shared("A", AT["xT"] + g, b):
                        pe.wait_ge(*drained("A", AT["xT"] + g, b))
                    for t in range(XT // 2):
                        last = tr(bank("A", AT["xT"] + g)[0:HD, CH * t:CH * (t + 1)],
                                  x_rows[:, XT // 2 * u + t, HD * half:HD * (half + 1)], ident[0:CH, 0:CH])
                    last.then_inc(xT_ps.sem, 1)

            def pointwise(b):
                pe.wait_ge(conv_sb.sem, conv_sb.count(b))
                for g in range(4):
                    u, half = divmod(g, 2)
                    lo, n = 2 * POOL_CUT[0] * u, 2 * POOL_CUT[u]
                    if shared("A", AT["pw"] + g, b):
                        pe.wait_ge(*drained("A", AT["pw"] + g, b))
                    for k in range(2):
                        last = mm(bank("A", AT["pw"] + g)[0:HD, 0:n], w_pw[:, k, HD * half:HD * (half + 1)],
                                  conv[:, k, lo:lo + n], start=(k == 0), stop=(k == 1))
                    last.then_inc(pw_ps.sem, 1)

            def dft_channels(b):
                pe.wait_ge(pooled_sb.sem, pooled_sb.count(b))
                for g, ts in enumerate(((0, 1), (2,))):
                    if shared("A", AT["chan"] + g, b):
                        pe.wait_ge(*drained("A", AT["chan"] + g, b))
                    for i, t in enumerate(ts):
                        for k in range(2):
                            last = mm(bank("A", AT["chan"] + g)[0:CH, D * i:D * (i + 1)],
                                      pooled[:, k, CH * t:CH * (t + 1)], dft_c[:, k, :],
                                      start=(k == 0), stop=(k == 1))
                    last.then_inc(chan_ps.sem, 1)

            def dft_positions(b):
                pe.wait_ge(chan_sb.sem, chan_sb.count(b))
                for name, w, lo, n, done in (("sine", sin_s, NP, NQ, sine_ps), ("cosine", cos_s, 0, NP, cosine_ps)):
                    if shared("A", AT[name], b):
                        pe.wait_ge(*drained("A", AT[name], b))
                    for j in range(NC_):
                        for t in range(NC_):
                            last = mm(bank("A", AT[name])[0:CH, n * j:n * (j + 1)],
                                      w[:, t, CH * j:CH * (j + 1)], chan[:, t, lo:lo + n],
                                      start=(t == 0), stop=(t == NC_ - 1))
                    last.then_inc(done.sem, 1)

            def project(b):
                pe.wait_ge(xn_sb.sem, xn_sb.count(b))
                for half in range(2):
                    if shared("B", AT["xnT"] + half, b):
                        pe.wait_ge(*drained("B", AT["xnT"] + half, b))
                    for i in range(NC_):
                        last = tr(bank("B", AT["xnT"] + half)[0:HD, CH * i:CH * (i + 1)],
                                  xn[:, i, HD * half:HD * (half + 1)], ident[0:CH, 0:CH])
                    last.then_inc(xnT_ps.sem, 1)
                pe.wait_ge(xnT_sb.sem, xnT_sb.count(b))
                for name, w, done in (("q", w_q, q_ps), ("k", w_k, k_ps)):
                    for half in range(2):
                        if shared("B", AT[name] + half, b):
                            pe.wait_ge(*drained("B", AT[name] + half, b))
                        for k in range(2):
                            last = mm(bank("B", AT[name] + half)[0:HD, 0:S], w[:, k, HD * half:HD * (half + 1)],
                                      xnT[:, k, :], start=(k == 0), stop=(k == 1))
                        last.then_inc(done.sem, 1)
                for i in range(NC_):
                    n = 2 * D if i < NC_ - 1 else D
                    if shared("B", AT["vk"] + i, b):
                        pe.wait_ge(*drained("B", AT["vk"] + i, b))
                    for k in range(2):
                        last = mm(bank("B", AT["vk"] + i)[0:CH, 0:n], xnT[:, k, CH * i:CH * (i + 1)],
                                  w_vk[:, k, 0:n], start=(k == 0), stop=(k == 1))
                    last.then_inc(vk_ps.sem, 1)

            def project_gate(b):
                for g in range(NG):
                    if shared("B", AT["g"] + g, b):
                        pe.wait_ge(*drained("B", AT["g"] + g, b))
                    for k in range(2):
                        last = mm(bank("B", AT["g"] + g)[:, 0:S], w_g[:, k, 4 * PH * g:4 * PH * (g + 1)],
                                  xnT[:, k, :], start=(k == 0), stop=(k == 1))
                    last.then_inc(g_ps.sem, 1)

            def score(b):
                pe.wait_ge(k_sb.sem, k_sb.count(b))
                pe.wait_ge(qb_in.sem, qb_in.count(b))
                for g in range(4 * NC_):
                    i, q = divmod(g, 4)
                    half, h0 = divmod(HG * q, HH)
                    if shared("B", AT["sc"] + g, b):
                        pe.wait_ge(*drained("B", AT["sc"] + g, b))
                    mm(bank("B", AT["sc"] + g)[0:CH, 0:HG * CH], kT[:, half, CH * i:CH * (i + 1)],
                       q_block[:, half, h0:h0 + HG, CH * i:CH * (i + 1)], start=True, stop=True
                       ).then_inc(sc_ps.sem, 1)

            def chunk_states(b):
                pe.wait_ge(vk_sb.sem, vk_sb.count(b))
                pe.wait_ge(k_dec_sb.sem, k_dec_sb.count(b))
                for i in range(NC_ - 1):
                    if shared("B", AT["st"] + i, b):
                        pe.wait_ge(*drained("B", AT["st"] + i, b))
                    for half in range(2):
                        last = mm(bank("B", AT["st"] + i)[0:HD, HH * PH * half:HH * PH * (half + 1)],
                                  k_dec[:, i, HD * half:HD * (half + 1)],
                                  v_pad[:, i, HH * half:HH * (half + 1), :].rearrange("p h d -> p (h d)"),
                                  start=True, stop=True)
                    last.then_inc(st_ps.sem, 1)

            def attend(b, i):
                o = bank("C", AT["av"] + i)
                pe.wait_ge(sc_sb.sem, sc_sb.count(b, 4 * i + 3))
                if shared("C", AT["av"] + i, b):
                    pe.wait_ge(*drained("C", AT["av"] + i, b))
                if i:
                    pe.wait_ge(q_dec_sb.sem, q_dec_sb.count(b))
                    pe.wait_ge(st_sb.sem, st_sb.count(b, i - 1))
                for g in range(NG):
                    cols = slice(CH * g, CH * (g + 1))
                    if i:
                        for p0, n, half, s0 in (((0, 128, 0, 0),), ((0, 64, 0, 128), (64, 64, 1, 0)),
                                                ((0, 128, 1, 64),))[g]:
                            mm(o[p0:p0 + n, cols], state[:, i - 1, half, s0:s0 + n],
                               q_dec[:, half, CH * (i - 1):CH * i], start=True, stop=False,
                               skip_group_check=True)
                    for j in range(4):
                        last = mm(o[PH * j:PH * (j + 1), cols], v_pad[:, i, 4 * g + j, :],
                                  scores[:, i, 4 * g + j, :], start=(i == 0), stop=True, skip_group_check=True)
                last.then_inc(av_ps.sem, 1)

            def output(c):
                pe.wait_ge(av_sb.sem, av_sb.count(c))
                for g, ts in enumerate(((0, 1), (2,))):
                    if shared("C", AT["o"] + g, c):
                        pe.wait_ge(*drained("C", AT["o"] + g, c))
                    for i, t in enumerate(ts):
                        for k in range(NG):
                            last = mm(bank("C", AT["o"] + g)[0:CH, D * i:D * (i + 1)],
                                      gated[:, k, CH * t:CH * (t + 1)], w_o[:, k, :],
                                      start=(k == 0), stop=(k == NG - 1))
                    last.then_inc(o_ps.sem, 1)

            def transpose_x2(c):
                pe.wait_ge(x2_sb.sem, x2_sb.count(c))
                for half in range(2):
                    if shared("C", AT["x2T"] + half, c):
                        pe.wait_ge(*drained("C", AT["x2T"] + half, c))
                    for i in range(NC_):
                        last = tr(bank("C", AT["x2T"] + half)[0:HD, CH * i:CH * (i + 1)],
                                  x2[:, i, HD * half:HD * (half + 1)], ident[0:CH, 0:CH])
                    last.then_inc(x2T_ps.sem, 1)

            def router(c):
                pe.wait_ge(x2T_sb.sem, x2T_sb.count(c))
                if shared("C", AT["lg"], c):
                    pe.wait_ge(*drained("C", AT["lg"], c))
                for i in range(NC_):
                    for k in range(2):
                        last = mm(bank("C", AT["lg"])[0:CH, E * i:E * (i + 1)], x2T[:, k, CH * i:CH * (i + 1)],
                                  w_r[:, k, :], start=(k == 0), stop=(k == 1))
                last.then_inc(lg_ps.sem, 1)

            def rank(c):
                pe.wait_ge(pick_sb.sem, pick_sb.count(c))
                if begun(c - 1):
                    pe.wait_ge(counts_sb.sem, counts_sb.count(c - 1))
                if shared("C", AT["rank"], c):
                    pe.wait_ge(*drained("C", AT["rank"], c))
                o = bank("C", AT["rank"])
                flat = picked[:, :, :].rearrange("p t e -> p (t e)")
                mm(o[0:CH, 0:NC_ * E], tri[:, :], flat, start=True, stop=False, skip_group_check=True)
                mm(o[0:CH, 0:NC_ * E], ones[0:CH, 0:CH], counts[:, :].unsqueeze(1).to_broadcast([CH, NC_, E]),
                   start=False, stop=False, skip_group_check=True)
                mm(o[0:CH, 2 * E:3 * E], ones[0:CH, 0:CH], flat[:, 0:E], start=False, stop=False, skip_group_check=True)
                mm(o[0:CH, E:3 * E], ones[0:CH, 0:CH], flat[:, 0:2 * E], start=False, stop=True, skip_group_check=True
                   ).then_inc(rank_ps.sem, 1)

            def run(x_, a_, b, c):
                if first(x_):
                    pe.wait_ge(ident_in.sem, ident_in.count(0))
                if first(a_):
                    pe.wait_ge(in_a.sem, in_a.count(0))
                if first(b):
                    pe.wait_ge(in_b.sem, in_b.count(0))
                    gate_weights()
                if first(c):
                    pe.wait_ge(in_c.sem, in_c.count(0))
                if c is not None:
                    output(c)
                if b is not None:
                    project(b)
                if c is not None:
                    transpose_x2(c)
                if b is not None:
                    project_gate(b)
                if c is not None:
                    router(c)
                if b is not None:
                    score(b)
                if c is not None:
                    rank(c)
                if a_ is not None:
                    pointwise(a_)
                if b is not None:
                    chunk_states(b)
                    attend(b, 0)
                if a_ is not None:
                    dft_channels(a_)
                if b is not None:
                    attend(b, 1)
                if a_ is not None:
                    dft_positions(a_)
                if b is not None:
                    attend(b, 2)
                if x_ is not None:
                    transpose_x(x_)

            pipeline(pe, run)

            pe.wait_ge(counts_sb.sem, counts_sb.count(B - 1))
            mm(ps[0][:, 0:E], ones[0:CH, :], counts[:, :], start=True, stop=True).then_inc(n_ps.sem, 1)
            pe.wait_ge(table_sb.sem, table_sb.count(0))
            pe.wait_ge(w2_in.sem, w2_in.count(0))
            pe.wait_ge(zeroed.sem, 4)

            def up(j, p, jj):
                pe.wait_ge(w1_in[p].sem, w1_in[p].count(jj))
                pe.wait_ge(xrT_sb.sem, xrT_sb.count(j))
                if begun(j - 2):
                    pe.wait_ge(hid_a.sem, hid_a.count(j - 2))
                if begun(j - 2):
                    pe.wait_ge(hid_b.sem, hid_b.count(j - 2))
                for m in range(FC):
                    dst = ps[2 + 2 * p][:, 128 * m:128 * (m + 1)] if m < 4 else \
                        ps[3 + 2 * p][:, 128 * (m - 4):128 * (m - 3)]
                    for k in range(2):
                        n = HD + 1 - k
                        last = mm(dst, w1[p][0:n, k, 128 * m:128 * (m + 1)], xrT[p][0:n, k, :],
                                  start=(k == 0), stop=(k == 1))
                    if m in (3, FC - 1):
                        last.then_inc(hid_ps.sem, 1)

            def down(j, p):
                e = pe.value_load(table[0:1, 0, ds(j, 1)], min_val=0, max_val=E - 1)
                pe.wait_ge(hid_a.sem, hid_a.count(j))
                pe.wait_ge(hid_b.sem, hid_b.count(j))
                if begun(j - 2):
                    pe.wait_ge(out_sb.sem, out_sb.count(j - 2))
                for m in range(FC):
                    last = mm(ps[6 + p][:, 0:D], hid[p][:, m, :], w2[:, ds(e, 1), m, :].rearrange("p o d -> p (o d)"),
                              start=(m == 0), stop=(m == FC - 1))
                last.then_inc(out_ps.sem, 1)

            def tile_step(j, p, jj):
                if not (isinstance(j, int) and j + 1 >= MAXTILES):
                    up(j + 1, 1 - p, jj + p)
                if not (isinstance(j, int) and j + 2 >= MAXTILES):
                    pe.wait_ge(row_in[p].sem, row_in[p].count(jj + 1))
                    xrT_in(j + 2, p)
                down(j, p)

            def xrT_in(j, p):
                if begun(j - 2):
                    pe.wait_ge(xrT_sb.sem, xrT_sb.count(j - 2))
                for half in range(2):
                    last = tr(ps[p][0:HD, 128 * half:128 * (half + 1)], xr[p][:, HD * half:HD * (half + 1)],
                              ident[:, :])
                last.then_inc(xrT_ps.sem, 1)

            pe.wait_ge(row_in[0].sem, row_in[0].count(0))
            xrT_in(0, 0)
            pe.wait_ge(row_in[1].sem, row_in[1].count(0))
            xrT_in(1, 1)
            up(0, 0, 0)
            tiles(pe, tile_step)


def tables():
    f = np.float32
    order = channel_order()
    k = np.arange(D)
    turn = 2 * np.pi * ((k[:, None] * k[None, :]) % D) / D
    dft_c = np.concatenate([np.cos(turn)[:, 0:NP], np.sin(turn)[:, 1:NQ + 1]], 1)
    s = np.arange(S)
    turn = 2 * np.pi * ((s[:, None] * s[None, :]) % S) / S
    seq = lambda m: m.reshape(NC_, CH, S).transpose(1, 0, 2).astype(f)
    n = np.arange(CH)
    diff = n[None, :] - n[:, None]
    ch = np.arange(HD)
    tile = np.arange(NT)
    return dict(
        ident=np.eye(128, dtype=f), dft_c=halves(dft_c.astype(f)),
        cos_s=seq(np.cos(turn)), sin_s=seq(np.sin(turn)),
        code=np.tile(E - np.arange(E), (NC_, 1)).astype(f), region=np.tile(REGION * np.arange(E), (NC_, 1)).astype(f),
        to_end=(CH - n)[:, None].astype(f), pos=n.astype(f), tri=(n[:, None] < n[None, :]).astype(f),
        head_mask=np.repeat((0.5 * (ch[:, None] // DH == np.arange(HH)[None, :])).astype(f)[:, :, None], PH, 2),
        tok2=(2 * (tile[None, :] * CH + n[:, None])).astype(f), jcol=np.arange(MAXTILES).astype(f),
        diff=np.maximum(diff, 0).astype(f), keep=(0.5 * (diff >= 0)).astype(f)), order


def halves(w):
    return np.ascontiguousarray(w.reshape(2, HD, *w.shape[1:]).swapaxes(0, 1))


def kernel(x, L0_tok_w_dw, L0_tok_b_dw, L0_tok_w_pw, L0_tok_b_pw, L0_tok_gamma, L0_tok_beta, L0_attn_log_slope,
           L0_attn_Wq, L0_attn_Wk, L0_attn_Wv, L0_attn_Wo, L0_attn_Wg1, L0_attn_Wg2, L0_attn_ln_w, L0_attn_ln_b,
           L0_ffn_Wg, L0_ffn_bg, L0_ffn_W1, L0_ffn_b1, L0_ffn_W2, L0_ffn_b2):
    import concourse.bacc as bacc
    from concourse.bass_utils import run_bass_kernel_spmd as run

    arrays, o = tables()
    g = np.asarray
    arrays |= dict(
        x=g(x), w_dw=halves(g(L0_tok_w_dw)[:, 0, :]), b_dw=halves(g(L0_tok_b_dw)),
        w_pw=halves(g(L0_tok_w_pw)[:, :, 0].T), b_pw=halves(g(L0_tok_b_pw)),
        rows=np.stack([g(v)[o] for v in (L0_tok_gamma, L0_tok_beta, L0_attn_ln_w, L0_attn_ln_b)]),
        w_q=halves(g(L0_attn_Wq)[o]), w_k=halves(g(L0_attn_Wk)[o]),
        w_vk=halves(np.concatenate([g(L0_attn_Wv), g(L0_attn_Wk)], 1)[o]),
        w_g1=g(L0_attn_Wg1)[o].T.reshape(G, 2, HD), w_g2=g(L0_attn_Wg2).reshape(G, NH, DH),
        w_o=g(L0_attn_Wo)[:, o].reshape(NG, 4, DH, D).transpose(1, 2, 0, 3),
        slope=g(L0_attn_log_slope), slope_c=halves(np.repeat(g(L0_attn_log_slope), DH)),
        w_r=halves(g(L0_ffn_Wg)[o]),
        small=np.stack([np.tile(g(L0_ffn_bg), (NC_, 1)), arrays.pop("code"), arrays.pop("region")]),
        w1=g(L0_ffn_W1)[:, o].reshape(E, 2, HD, F).transpose(0, 2, 1, 3), b1=g(L0_ffn_b1),
        w2=g(L0_ffn_W2)[:, :, o].reshape(E, FC, 128, D).transpose(2, 0, 1, 3), b2=g(L0_ffn_b2)[:, o])
    nc = bacc.Bacc("TRN2", target_bir_lowering=False, num_devices=1)
    arrays = {f"in_{k}": np.ascontiguousarray(v) for k, v in arrays.items()}
    aps = {k[3:]: nc.dram_tensor(k, v.shape, mybir.dt.from_np(v.dtype), kind="ExternalInput").ap()
           for k, v in arrays.items()}
    out = nc.dram_tensor("out_rows", (B, S, D), mybir.dt.float32, kind="ExternalOutput").ap()
    build(nc, aps, out)
    got = run(nc, [arrays], core_ids=[0]).results[0]["out_rows"]
    return np.ascontiguousarray(got[:, :, np.argsort(o)])
```

```python
import numpy as np
import concourse.bass as bass
from concourse import mybir
from contextlib import ExitStack

B, S_IN, D, K = 8, 750, 192, 7
S = S_IN // 2
CH = 125
NC_ = S // CH
XT = S_IN // CH
HD = D // 2
NH, DH = 12, 16
HH = NH // 2
HG = 3
HP = HH // 2
VP = 3 * DH
G = 16
NP, NQ = D // 2 + 1, D // 2 - 1
E, F = 8, 768
FC = F // 128
NT = B * NC_
TOK = B * S
REGION = 128 * (-(-(TOK + 127) // 128))
ROW = D + 2
MAXTILES = (2 * TOK + 127 * E) // 128
EMPTY = E * REGION
SKIP = 1.0e6
EPS = 1e-5
PAD = K // 2
AHEAD = 6
POOL_CUT = (188, 187)


def channel_order():
    return np.array(list(range(NP)) + [D - c for c in range(1, NQ + 1)])


class Event:

    def __init__(self, sem, per=1):
        self.sem, self.per = sem, per

    def count(self, b, k=None):
        return b * self.per + (self.per if k is None else k + 1)


def first(b):
    return isinstance(b, int) and b == 0


def begun(b):
    return not (isinstance(b, int) and b < 0)


class Own:

    def __init__(self, sem, per):
        self.sem, self.per = sem, per

    def begin(self, b):
        self.base, self.n = b * self.per, 0

    def after(self, steps):
        self.n += steps
        return self.base + self.n

    def end(self):
        assert self.n == self.per, (self.n, self.per)


def build(nc, a, out):
    f32, i32 = mybir.dt.float32, mybir.dt.int32
    ALU, ACT, AX = mybir.AluOpType, mybir.ActivationFunctionType, mybir.AxisListType
    ds = bass.ds
    ctx = ExitStack()
    with ctx:
        def sb(name, shape, dt=f32):
            return ctx.enter_context(nc.sbuf_tensor(name, shape, dt))

        def event(name, per=1):
            return Event(ctx.enter_context(nc.semaphore(name)), per)

        def own(name, per):
            return Own(ctx.enter_context(nc.semaphore(name)), per)

        ident = sb("ident", [128, 128])
        dft_c = sb("dft_c", [HD, 2, D])
        cos_s = sb("cos_s", [CH, NC_, S])
        sin_s = sb("sin_s", [CH, NC_, S])
        w_dw = sb("w_dw", [HD, 2, K])
        b_dw = sb("b_dw", [HD, 2])
        w_pw = sb("w_pw", [HD, 2, D])
        b_pw = sb("b_pw", [HD, 2])
        rows = sb("rows", [CH, 4, D])
        w_q = sb("w_q", [HD, 2, D])
        w_k = sb("w_k", [HD, 2, D])
        w_v = sb("w_v", [HD, 2, D])
        w_g1 = sb("w_g1", [G, 2, HD])
        w_g2 = sb("w_g2", [G, D])
        w_g = sb("w_g", [HD, 2, D])
        w_o = sb("w_o", [HD, 2, D])
        w_r = sb("w_r", [HD, 2, E])
        small = sb("small", [CH, 3, NC_, E])
        slope_t = sb("slope_t", [CH, NH])
        slope_c = sb("slope_c", [HD, 2])
        to_end = sb("to_end", [CH, 1])
        pos = sb("pos", [HD, CH])
        tri = sb("tri", [CH, CH])
        head_mask = sb("head_mask", [HD, HH, DH])
        tok2 = sb("tok2", [CH, NT])
        jcol = sb("jcol", [128, MAXTILES])
        ones = sb("ones", [128, 128])
        idle = sb("idle", [1, 4])
        eps = sb("eps", [CH, NC_])
        half_neg = sb("half_neg", [CH, NC_])
        diff_keep = sb("diff_keep", [CH, 2, CH])
        decay = sb("decay", [CH, NH, CH])
        k_decay = sb("k_decay", [CH, NH, DH])
        q_decay = sb("q_decay", [HD, 2, CH])
        carry = sb("carry", [HD, 2])
        fill = sb("fill", [128, ROW])
        w2 = sb("w2", [128, E, FC, D])

        x_rows = sb("x_rows", [CH, XT, D])
        xT = sb("xT", [HD, 2, S_IN + 2 * PAD])
        area = [sb(f"area_{p}", [128, 2 * F]) for p in range(2)]
        conv, pw = [t[0:HD, 0:2 * S_IN].rearrange("p (h s) -> p h s", h=2) for t in area]
        wide = sb("wide", [128, 2 * HH * S])
        pooled = sb("pooled", [HD, 2, S])
        chan = sb("chan", [CH, NC_, D])
        sine = sb("sine", [CH, NC_, NQ])
        y = sb("y", [CH, NC_, D])
        h1 = sb("h1", [CH, NC_, D])
        xn = sb("xn", [CH, NC_, D])
        stats = sb("stats", [CH, 4, NC_, 6])
        mv = sb("mv", [CH, 4, NC_, 2])
        vp = sb("vp", [CH, 4, NC_])
        rstd = sb("rstd", [CH, 4, NC_])
        xnT = sb("xnT", [HD, 2, S])
        qT = sb("qT", [HD, 2, S])
        kT = sb("kT", [HD, 2, S])
        q_block = wide[0:HD, :].rearrange("p (u h s) -> p u h s", u=2, h=HH)
        q_dec = sb("q_dec", [HD, 2, S - CH])
        v_pad = sb("v_pad", [CH, NC_, NH // 2, 2 * VP])
        k_tok = sb("k_tok", [CH, NC_ - 1, D])
        k_dec = sb("k_dec", [CH, NC_ - 1, D])
        gate = sb("gate", [HD, 2, S])
        deep = sb("deep", [128, NC_ * NH * CH])
        scores = deep[0:CH, :].rearrange("p (c h n) -> p c h n", c=NC_, h=NH)
        state = sb("state", [HD, NC_ - 1, 2, HD])
        gated = sb("gated", [HD, 2, S])
        resid = sb("resid", [CH, NT, D])
        o_ln = sb("o_ln", [CH, NC_, D])
        x2 = sb("x2", [CH, NC_, ROW])
        x2T = sb("x2T", [HD, 2, S])
        logit = sb("logit", [CH, NC_, E])
        logit2 = sb("logit2", [CH, NC_, E])
        hit = sb("hit", [CH, NC_, E])
        top = sb("top", [CH, 4, NC_])
        pick = sb("pick", [CH, 2, NC_, E])
        picked = sb("picked", [CH, NC_, E])
        row_of = sb("row_of", [CH, NC_, E])
        row_hit = sb("row_hit", [CH, 2, NC_, E])
        slots_f = sb("slots_f", [CH, 2, NC_])
        slots = sb("slots", [CH, 2, NC_], i32)
        counts = sb("counts", [CH, E])
        tile_sum = sb("tile_sum", [CH, E])
        gap = sb("gap", [CH, NT])
        n_f = sb("n_f", [128, E])
        n_i = sb("n_i", [128, 2, E], i32)
        nt_f = sb("nt_f", [128, E])
        end_f = sb("end_f", [128, E])
        cut = [0]

        def from_wide(n):
            cut[0] += n
            return wide[:, cut[0] - n:cut[0]]

        past, past_n = [from_wide(MAXTILES * E).rearrange("p (j e) -> p j e", e=E) for _ in range(2)]
        e_of = sb("e_of", [128, MAXTILES])
        tiles_before = sb("tiles_before", [128, MAXTILES])
        blk = sb("blk", [128, 3, MAXTILES])
        table = sb("table", [1, 2, MAXTILES], i32)
        fill_at = sb("fill_at", [1, E], i32)
        w1 = [t[0:HD + 1, :].rearrange("p (h f) -> p h f", h=2) for t in area]
        PAIR = 2 * NC_ * D
        at = 2 * PAIR
        b2_rows = deep[:, at:at + E * D].rearrange("p (e d) -> p e d", e=E)
        at += E * D
        xr = [deep[:, at + ROW * p:at + ROW * (p + 1)] for p in range(2)]
        pairs = [t[0:CH, PAIR * p:PAIR * (p + 1)].rearrange("p (t e) -> p t e", t=NC_)
                 for t, n in ((deep, 3), (wide, 3), (area[0], 1), (area[1], 1)) for p in range(n)]
        xrT = [from_wide(256)[0:HD + 1].rearrange("p (h t) -> p h t", h=2) for _ in range(2)]
        hid = [from_wide(FC * 128).rearrange("p (c t) -> p c t", c=FC) for _ in range(2)]
        yo = [from_wide(D) for _ in range(2)]
        dest_f = sb("dest_f", [128, MAXTILES])
        dest = [sb(f"dest_{p}", [128, 1], i32) for p in range(2)]
        gates = sb("gates", [CH, 3, NT])

        ps = [ctx.enter_context(nc.psum_tensor(f"ps{i}", [128, 512], f32)) for i in range(8)]

        routed = nc.dram_tensor("routed", [EMPTY + 128, ROW], f32, kind="Internal").ap()
        by_pair = nc.dram_tensor("by_pair", [2 * TOK, D], f32, kind="Internal").ap()

        ident_in = event("ident_in", 16)
        in_w = event("in_w", 16 * 2)
        in_a = event("in_a", 16 * 6)
        in_b = event("in_b", 16 * 6)
        in_c = event("in_c", 16 * 6)
        in_d = event("in_d", 16 * 6)
        wg_ps = event("wg_ps")
        wg_sb = event("wg_sb")
        w2_in = event("w2_in", 16)
        b2_in = event("b2_in", 16)
        empty_in = event("empty_in", 16)
        x_in = event("x_in", 16)
        zeroed = event("zeroed")
        zeroed_d = event("zeroed_d")
        tables = event("tables")
        tables_d = event("tables_d")
        xT_ps = event("xT_ps", 4)
        xT_sb = event("xT_sb", 4)
        conv_sb = event("conv_sb", 2)
        pw_ps = event("pw_ps", 4)
        pw_sb = event("pw_sb", 4)
        pooled_sb = event("pooled_sb", 2)
        chan_ps = event("chan_ps", 2)
        chan_sb = event("chan_sb", 2)
        sine_ps = event("sine_ps")
        sine_sb = event("sine_sb")
        cosine_ps = event("cosine_ps")
        y_sb = event("y_sb")
        var_sb = event("var_sb", 2)
        rstd_sb = event("rstd_sb", 2)
        h1_sb = event("h1_sb")
        xn_sb = event("xn_sb")
        hb_sb = event("hb_sb")
        xnT_ps = event("xnT_ps", 2)
        xnT_sb = event("xnT_sb", 2)
        q_ps = event("q_ps", 2)
        q_sb = event("q_sb", 2)
        k_ps = event("k_ps", 2)
        k_sb = event("k_sb", 2)
        v_ps = event("v_ps", NC_)
        v_sb = event("v_sb", NC_)
        kt_ps = event("kt_ps")
        kt_sb = event("kt_sb")
        g_ps = event("g_ps", 2)
        g_sb = event("g_sb", 2)
        qb_in = event("qb_in", 16 * NH)
        k_dec_sb = event("k_dec_sb")
        q_dec_sb = event("q_dec_sb")
        sc_ps = event("sc_ps", 4 * NC_)
        sc_sb = event("sc_sb", 4 * NC_)
        st_ps = event("st_ps", 2)
        st_sb = event("st_sb", 2)
        av_ps = event("av_ps", NC_)
        av_sb = event("av_sb", NC_)
        o_ps = event("o_ps", 2)
        o_free = event("o_free", NC_)
        cvar_sb = event("cvar_sb", 2)
        crstd_sb = event("crstd_sb", 2)
        x2_sb = event("x2_sb")
        x2T_ps = event("x2T_ps", 2)
        x2T_sb = event("x2T_sb", 2)
        lg_ps = event("lg_ps")
        lg_sb = event("lg_sb")
        pick_sb = event("pick_sb")
        rank_ps = event("rank_ps")
        rank_sb = event("rank_sb")
        slots_sb = event("slots_sb")
        counts_sb = event("counts_sb")
        scattered = event("scattered", 16 * 2 * NC_)
        tap_done = event("tap_done", 2 * (K - 1))
        own_ln = own("own_ln", 3)
        own_c = own("own_c", 18)
        own_st = own("own_st", 1)
        own_pa = own("own_pa", 2)
        own_pc = own("own_pc", 2)
        n_ps = event("n_ps")
        own_t = own("own_t", 15)
        table_sb = event("table_sb")
        fill_at_sb = event("fill_at_sb")
        filled = event("filled")
        row_in = [event(f"row_in{p}", 16) for p in range(2)]
        w1_in = [event(f"w1_in{p}", 32) for p in range(2)]
        dest_sb = event("dest_sb")
        xrT_ps = event("xrT_ps")
        xrT_sb = event("xrT_sb")
        hid_ps = event("hid_ps", 2)
        hid_a = event("hid_a")
        hid_b = event("hid_b")
        out_ps = event("out_ps")
        out_sb = event("out_sb")
        sent = [event(f"sent{p}", 16) for p in range(2)]
        idled = event("idled")
        exp_sb = event("exp_sb")
        gates_sb = event("gates_sb")
        own_g = own("own_g", 2)
        pair_in = [event(f"pair_in{b}", 16) for b in range(B)]
        mixed = event("mixed")
        scaled = event("scaled")
        own_m = own("own_m", 1)
        out_done = event("out_done", 16)

        block = ctx.enter_context(nc.Block())

        def apart(eng):
            if eng is nc.gpsimd:
                return nc.gpsimd.tensor_tensor(idle[0:1, 0:1], idle[0:1, 1:2], idle[0:1, 1:2], ALU.add)
            return nc.vector.memset(idle[0:1, 2:3], 0.0)

        RING_A = [(xT_sb, k, 1) for k in range(2)] + [(pw_sb, k, 0) for k in range(4)] + \
                 [(chan_sb, k, 0) for k in range(2)] + [(sine_sb, 0, 0), (y_sb, 0, 0)] + \
                 [(xT_sb, k, 1) for k in range(2, 4)]
        RING_B = [(xnT_sb, k, 0) for k in range(2)] + [(q_sb, k, 0) for k in range(2)] + \
                 [(k_sb, k, 0) for k in range(2)] + [(v_sb, k, 0) for k in range(NC_)] + \
                 [(g_sb, k, 0) for k in range(2)] + [(kt_sb, 0, 0)] + \
                 [(sc_sb, k, 0) for k in range(9)] + [(st_sb, k, 0) for k in range(2)] + \
                 [(sc_sb, k, 0) for k in range(9, 4 * NC_)] + \
                 [(sc_sb, 9, 0)]
        RING_C = [(av_sb, k, 0) for k in range(NC_)] + [(o_free, 1, 0), (o_free, 2, 0)] + \
                 [(x2T_sb, k, 0) for k in range(2)] + [(lg_sb, 0, 0), (rank_sb, 0, 0)]
        RINGS = {"A": (RING_A, [0, 1]), "B": (RING_B, [2, 3, 4]), "C": (RING_C, [5, 6, 7])}
        AT = {"pw": (2, 3, 4, 5), "chan": (6, 7), "xT": (0, 1, 10, 11), "sine": (8,), "cosine": (9,),
              "xnT": (0, 1), "q": (2, 3), "k": (4, 5), "v": (6, 7, 8), "g": (9, 10), "kt": (11,),
              "sc": (*range(12, 21), 23, 24, 25), "st": (21, 22),
              "av": (0, 1, 2), "o": (3, 4), "x2T": (5, 6), "lg": (7,), "rank": (8,)}
        assert all(len(r) % len(banks) == 0 for r, banks in RINGS.values())

        def bank(ring, name, k=0):
            return ps[RINGS[ring][1][AT[name][k] % len(RINGS[ring][1])]]

        def before(ring, name, k, b):
            groups, banks = RINGS[ring]
            at = AT[name][k]
            turn = b - groups[at][2]
            for back in range(1, len(groups)):
                n = at - back * len(banks)
                event_, number, ahead = groups[n % len(groups)]
                batch = turn + n // len(groups) + ahead
                if not isinstance(batch, int) or 0 <= batch < B:
                    return event_, batch, number
            return None

        def shared(ring, name, k, b):
            return before(ring, name, k, b) is not None

        def drained(ring, name, k, b):
            event_, batch, number = before(ring, name, k, b)
            return event_.sem, event_.count(batch, number)

        def pipeline(eng, run):
            run(0, None, None, None)
            run(1, 0, None, None)
            run(2, 1, 0, None)
            run(3, 2, 1, 0)
            with eng.Fori(2, B - 2) as b:
                run(b + 2, b + 1, b, b - 1)
            run(None, B - 1, B - 2, B - 3)
            run(None, None, B - 1, B - 2)
            run(None, None, None, B - 1)

        def tiles(eng, run):
            for j in range(4):
                run(j, j % 2, j // 2)
            with eng.Fori(2, MAXTILES // 2 - 1) as jj:
                for p in range(2):
                    run(jj * 2 + p, p, jj)
            for j in range(MAXTILES - 2, MAXTILES):
                run(j, j % 2, j // 2)

        def full(t):
            return t[tuple(slice(None) for _ in t.shape)]

        consts_w = [(w_dw, a["w_dw"]), (b_dw, a["b_dw"])]
        consts_a = [
            (w_pw, a["w_pw"]), (b_pw, a["b_pw"]),
            (dft_c, a["dft_c"]), (sin_s, a["sin_s"]), (cos_s, a["cos_s"]),
            (rows, a["rows"].partition_broadcast(CH))]
        consts_b = [
            (w_q, a["w_q"]), (w_k, a["w_k"]), (w_v, a["w_v"]), (w_g1, a["w_g1"]), (w_g2, a["w_g2"]),
            (head_mask, a["head_mask"])]
        consts_d = [
            (slope_t, a["slope"].partition_broadcast(CH)), (slope_c, a["slope_c"]), (to_end, a["to_end"]),
            (pos, a["pos"].partition_broadcast(HD)), (diff_keep[:, 0], a["diff"]), (diff_keep[:, 1], a["keep"])]
        consts_c = [
            (w_r, a["w_r"]), (small, a["small"].partition_broadcast(CH)), (tri, a["tri"]), (tok2, a["tok2"]),
            (jcol, a["jcol"].partition_broadcast(128)), (w_o, a["w_o"])]

        def fill_regions(eng, experts):
            for e in experts:
                at = eng.value_load(fill_at[0:1, e:e + 1], min_val=e * REGION, max_val=e * REGION + TOK)
                eng.dma_start(routed[ds(at, 128), :], fill[:, :]).then_inc(filled.sem, 16)

        @block.sync
        def _(sp):
            def load_x(b):
                if begun(b - 1):
                    sp.wait_ge(xT_ps.sem, xT_ps.count(b - 1))
                sp.dma_start(x_rows[:, :, :], a["x"][ds(b, 1)].rearrange("o (t p) d -> p (o t) d", p=CH)
                             ).then_inc(x_in.sem, 16)

            load_x(0)
            for dst, src in consts_w:
                sp.dma_start(full(dst), src).then_inc(in_w.sem, 16)
            for dst, src in consts_a:
                sp.dma_start(full(dst), src).then_inc(in_a.sem, 16)
            for dst, src in consts_d:
                sp.dma_start(dst if isinstance(dst, bass.AP) else full(dst), src).then_inc(in_d.sem, 16)

            def run(x_, a_, b, c):
                if x_ is not None and not (isinstance(x_, int) and x_ == 0):
                    load_x(x_)
                if first(a_):
                    for dst, src in consts_b:
                        sp.dma_start(full(dst), src).then_inc(in_b.sem, 16)
                    for dst, src in consts_c:
                        sp.dma_start(full(dst), src).then_inc(in_c.sem, 16)
                if b is not None:
                    if begun(b - 1):
                        sp.wait_ge(sc_ps.sem, sc_ps.count(b - 1))
                    for h in range(NH):
                        half, hl = divmod(h, HH)
                        if hl == 0:
                            sp.wait_ge(q_sb.sem, q_sb.count(b, half))
                        sp.dma_start(q_block[DH * hl:DH * hl + DH, half, hl, :],
                                     qT[DH * hl:DH * hl + DH, half, :]).then_inc(qb_in.sem, 16)

            pipeline(sp, run)

            sp.wait_ge(av_ps.sem, av_ps.count(B - 1))
            sp.dma_start(b2_rows, a["b2"].partition_broadcast(128)).then_inc(b2_in.sem, 16)
            sp.wait_ge(fill_at_sb.sem, fill_at_sb.count(0))
            fill_regions(sp, range(0, E // 2))

            def load_w1(e, p):
                sp.dma_start(w1[p][0:HD, :, :], a["w1"][ds(e, 1)].rearrange("o p h f -> (o p) h f")
                             ).then_inc(w1_in[p].sem, 16)
                sp.dma_start(w1[p][HD:HD + 1, 0, :], a["b1"][ds(e, 1), :]).then_inc(w1_in[p].sem, 16)

            sp.wait_ge(table_sb.sem, table_sb.count(0))
            for j in range(2):
                load_w1(sp.value_load(table[0:1, 0, j:j + 1], min_val=0, max_val=E - 1), j)
            sp.wait_ge(scattered.sem, scattered.count(B - 1))
            sp.wait_ge(filled.sem, 16 * E)
            sp.wait_ge(empty_in.sem, empty_in.count(0))

            def load(j, p, jj):
                t = j - 2
                r = sp.value_load(table[0:1, 1, ds(j, 1)], min_val=0, max_val=EMPTY)
                if begun(t):
                    sp.wait_ge(xrT_ps.sem, xrT_ps.count(t))
                if begun(t):
                    sp.wait_ge(dest_sb.sem, dest_sb.count(t))
                sp.dma_start(xr[p][:, :], routed[ds(r, 128), :]).then_inc(row_in[p].sem, 16)
                if begun(t):
                    sp.wait_ge(hid_ps.sem, hid_ps.count(t))
                    load_w1(sp.value_load(table[0:1, 0, ds(j, 1)], min_val=0, max_val=E - 1), p)

            tiles(sp, load)

            for p in range(2):
                sp.wait_ge(sent[p].sem, sent[p].count(MAXTILES // 2 - 1))
            for b in range(B):
                sp.dma_start(pairs[b], by_pair[2 * S * b:2 * S * (b + 1), :].rearrange(
                    "(t p k) d -> p t (k d)", p=CH, k=2)).then_inc(pair_in[b].sem, 16)
            for b in range(B):
                sp.wait_ge(mixed.sem, mixed.count(b))
                sp.dma_start(out[b].rearrange("(t p) d -> p t d", p=CH), resid[:, NC_ * b:NC_ * (b + 1), :]
                             ).then_inc(out_done.sem, 16)
            sp.wait_ge(out_done.sem, 16 * B)

        @block.gpsimd
        def _(pool):
            nc.gpsimd.memset(idle[:, 1:2], 0.0)
            for side in (slice(0, PAD), slice(PAD + S_IN, S_IN + 2 * PAD)):
                last = nc.gpsimd.memset(xT[:, :, side], 0.0)
            last.then_inc(zeroed.sem, 1)
            nc.gpsimd.memset(half_neg[:, :], -0.5)
            nc.gpsimd.memset(eps[:, :], EPS)
            nc.gpsimd.memset(q_block[:, :, :, :], 0.0)
            nc.gpsimd.memset(v_pad[:, :, :, :], 0.0)
            nc.gpsimd.memset(counts[:, :], 0.0)
            nc.gpsimd.memset(ones[:, :], 1.0)
            nc.gpsimd.memset(fill[:, :], 0.0).then_inc(zeroed.sem, 1)
            pool.wait_ge(zeroed.sem, 2)
            nc.gpsimd.memset(fill[:, D:D + 1], SKIP).then_inc(zeroed.sem, 1)
            pool.wait_ge(zeroed.sem, 3)
            pool.dma_start(routed[EMPTY:EMPTY + 128, :], fill[:, :]).then_inc(empty_in.sem, 16)
            pool.wait_ge(in_a.sem, in_a.count(0))
            pool.wait_ge(tables.sem, 1)

            def inverse_std(own_, b, n, k, ready, done):
                pool.wait_ge(ready.sem, ready.count(b, k))
                nc.gpsimd.tensor_tensor(vp[:, n], mv[:, n, :, 1], eps[:, :], ALU.add).then_inc(own_.sem, 1)
                pool.wait_ge(own_.sem, own_.after(1))
                nc.gpsimd.tensor_tensor(rstd[:, n], vp[:, n], half_neg[:, :], ALU.pow).then_inc(done.sem, 1)

            def run(x_, a_, b, c):
                if c is not None:
                    own_pc.begin(c)
                    inverse_std(own_pc, c, 2, 0, cvar_sb, crstd_sb)
                    inverse_std(own_pc, c, 3, 1, cvar_sb, crstd_sb)
                    own_pc.end()
                if b is not None:
                    pool.wait_ge(q_sb.sem, q_sb.count(b))
                    if begun(b - 1):
                        pool.wait_ge(av_ps.sem, av_ps.count(b - 1))
                    nc.gpsimd.tensor_tensor(
                        q_dec[:, :, :].rearrange("p h (c n) -> p h c n", n=CH),
                        qT[:, :, CH:S].rearrange("p h (c n) -> p h c n", n=CH),
                        q_decay[:, :, :].unsqueeze(2).to_broadcast([HD, 2, NC_ - 1, CH]),
                        ALU.mult).then_inc(q_dec_sb.sem, 1)
                    pool.wait_ge(kt_sb.sem, kt_sb.count(b))
                    nc.gpsimd.tensor_tensor(
                        k_dec[:, :, :], k_tok[:, :, :],
                        k_decay[:, :, :].rearrange("p h d -> p (h d)").unsqueeze(1)
                        .to_broadcast([CH, NC_ - 1, D]), ALU.mult).then_inc(k_dec_sb.sem, 1)
                if first(b):
                    pool.dma_start(w2[:, :, :, :], a["w2"]).then_inc(w2_in.sem, 16)
                if c is not None:
                    pool.wait_ge(slots_sb.sem, slots_sb.count(c))
                    apart(pool)
                    for k in range(2):
                        for i in range(NC_):
                            nc.gpsimd.indirect_dma_start(
                                routed, bass.IndirectOffsetOnAxis(ap=slots[:, k, i:i + 1], axis=0),
                                x2[:, i, :], None).then_inc(scattered.sem, 16)
                if a_ is not None:
                    own_pa.begin(a_)
                    inverse_std(own_pa, a_, 0, 0, var_sb, rstd_sb)
                    inverse_std(own_pa, a_, 1, 1, var_sb, rstd_sb)
                    own_pa.end()
                    pool.wait_ge(h1_sb.sem, h1_sb.count(a_))
                    nc.gpsimd.tensor_tensor(
                        resid[:, ds(a_ * NC_, NC_), :], h1[:, :, :],
                        rows[:, 3, :].unsqueeze(1).to_broadcast([CH, NC_, D]), ALU.add
                    ).then_inc(hb_sb.sem, 1)

            pipeline(pool, run)

            def send(j, p, jj):
                pool.wait_ge(out_sb.sem, out_sb.count(j))
                if begun(j - 1):
                    pool.wait_ge(idled.sem, idled.count(j - 1))
                apart(pool).then_inc(idled.sem, 1)
                nc.gpsimd.indirect_dma_start(
                    by_pair, bass.IndirectOffsetOnAxis(ap=dest[p][:, 0:1], axis=0), yo[p][:, :], None,
                    bounds_check=last_row, oob_is_err=False).then_inc(sent[p].sem, 16)

            pool.wait_ge(table_sb.sem, table_sb.count(0))
            for p in range(2):
                last = nc.gpsimd.memset(xrT[p][HD:HD + 1, 0, :], 1.0)
            last.then_inc(zeroed.sem, 1)
            last_row = pool.to_reg(2 * TOK - 1)
            tiles(pool, send)

        @block.scalar
        def _(act):
            act.dma_start(ident[:, :], a["ident"]).then_inc(ident_in.sem, 16)
            act.wait_ge(zeroed.sem, 1)
            nc.scalar.activation(idle[0:1, 3:4], idle[0:1, 1:2], ACT.Exp)

            def decay_tables():
                act.wait_ge(in_d.sem, in_d.count(0))
                for h in range(NH):
                    nc.scalar.activation(decay[:, h, :], diff_keep[:, 0], ACT.Exp, scale=slope_t[:, h:h + 1])
                nc.scalar.activation(k_decay[:, :, :], slope_t[:, :].unsqueeze(2).to_broadcast([CH, NH, DH]),
                                     ACT.Exp, scale=to_end[:, 0:1])
                for half in range(2):
                    nc.scalar.activation(q_decay[:, half], pos[:, :], ACT.Exp, scale=slope_c[:, half:half + 1])
                nc.scalar.activation(carry[:, :], slope_c[:, :], ACT.Exp, scale=float(CH)
                                     ).then_inc(tables.sem, 1)

            def keep_xT(b, half):
                for u in range(2):
                    act.wait_ge(xT_ps.sem, xT_ps.count(b, 2 * half + u))
                    if u == 0:
                        if begun(b - 1):
                            act.wait_ge(conv_sb.sem, conv_sb.count(b - 1, half))
                    nc.scalar.activation(
                        xT[:, half, PAD + S * u:PAD + S * (u + 1)], bank("A", "xT", 2 * half + u)[0:HD, 0:S],
                        ACT.Copy).then_inc(xT_sb.sem, 1)

            def gate_weights():
                act.wait_ge(wg_ps.sem, wg_ps.count(0))
                for half in range(2):
                    last = nc.scalar.activation(w_g[:, half], ps[2 + half][0:HD, 0:D], ACT.Copy)
                last.then_inc(wg_sb.sem, 1)

            def run(x_, a_, b, c):
                if first(a_):
                    decay_tables()
                    act.wait_ge(in_a.sem, in_a.count(0))
                if first(b):
                    gate_weights()
                    act.wait_ge(zeroed.sem, 3)
                if b is not None:
                    for half in range(2):
                        act.wait_ge(xnT_ps.sem, xnT_ps.count(b, half))
                        if half == 0:
                            if begun(b - 1):
                                act.wait_ge(g_ps.sem, g_ps.count(b - 1))
                        nc.scalar.activation(xnT[:, half], bank("B", "xnT", half)[0:HD, 0:S],
                                             ACT.Copy).then_inc(xnT_sb.sem, 1)
                    for half in range(2):
                        act.wait_ge(q_ps.sem, q_ps.count(b, half))
                        if half == 0:
                            if begun(b - 1):
                                act.wait_ge(qb_in.sem, qb_in.count(b - 1))
                            if begun(b - 1):
                                act.wait_ge(q_dec_sb.sem, q_dec_sb.count(b - 1))
                        nc.scalar.activation(qT[:, half], bank("B", "q", half)[0:HD, 0:S],
                                             ACT.Silu).then_inc(q_sb.sem, 1)
                    for half in range(2):
                        act.wait_ge(k_ps.sem, k_ps.count(b, half))
                        if half == 0:
                            if begun(b - 1):
                                act.wait_ge(sc_ps.sem, sc_ps.count(b - 1))
                        nc.scalar.activation(kT[:, half], bank("B", "k", half)[0:HD, 0:S],
                                             ACT.Silu).then_inc(k_sb.sem, 1)
                    for i in range(NC_):
                        act.wait_ge(v_ps.sem, v_ps.count(b, i))
                        if i == 0:
                            if begun(b - 1):
                                act.wait_ge(av_ps.sem, av_ps.count(b - 1))
                        nc.scalar.activation(
                            v_pad[:, i].rearrange("p q (j d) -> p q j d", j=2)[:, :, :, 0:DH],
                            bank("B", "v", i)[0:CH, 0:D].rearrange("p (q j d) -> p q j d", j=2, d=DH), ACT.Silu
                        ).then_inc(v_sb.sem, 1)
                    for half in range(2):
                        act.wait_ge(g_ps.sem, g_ps.count(b, half))
                        if half == 0:
                            if begun(b - 1):
                                act.wait_ge(av_sb.sem, av_sb.count(b - 1))
                        nc.scalar.activation(gate[:, half], bank("B", "g", half)[0:HD, 0:S], ACT.Tanh,
                                             scale=0.5).then_inc(g_sb.sem, 1)
                    act.wait_ge(kt_ps.sem, kt_ps.count(b))
                    if begun(b - 1):
                        act.wait_ge(k_dec_sb.sem, k_dec_sb.count(b - 1))
                    nc.scalar.activation(
                        k_tok[:, :, :], bank("B", "kt")[0:CH, 0:(NC_ - 1) * D].rearrange("p (t d) -> p t d", d=D),
                        ACT.Copy).then_inc(kt_sb.sem, 1)
                if c is not None:
                    for half in range(2):
                        act.wait_ge(x2T_ps.sem, x2T_ps.count(c, half))
                        if half == 0:
                            if begun(c - 1):
                                act.wait_ge(lg_ps.sem, lg_ps.count(c - 1))
                        nc.scalar.activation(x2T[:, half], bank("C", "x2T", half)[0:HD, 0:S],
                                             ACT.Copy).then_inc(x2T_sb.sem, 1)
                if x_ is not None:
                    keep_xT(x_, 0)
                if a_ is not None:
                    for g in range(4):
                        u, half = divmod(g, 2)
                        lo = 2 * POOL_CUT[0] * u
                        n = 2 * POOL_CUT[u]
                        act.wait_ge(pw_ps.sem, pw_ps.count(a_, g))
                        if g == 0:
                            if begun(a_ - 1):
                                act.wait_ge(pooled_sb.sem, pooled_sb.count(a_ - 1))
                        nc.scalar.activation(pw[:, half, lo:lo + n], bank("A", "pw", g)[0:HD, 0:n],
                                             ACT.Relu, bias=b_pw[:, half:half + 1]).then_inc(pw_sb.sem, 1)
                    for g, (lo, n) in enumerate(((0, 2), (2, 1))):
                        act.wait_ge(chan_ps.sem, chan_ps.count(a_, g))
                        if g == 0:
                            if begun(a_ - 1):
                                act.wait_ge(cosine_ps.sem, cosine_ps.count(a_ - 1))
                        nc.scalar.activation(
                            chan[:, lo:lo + n, :], bank("A", "chan", g)[0:CH, 0:n * D].rearrange(
                                "p (t d) -> p t d", d=D), ACT.Copy).then_inc(chan_sb.sem, 1)
                    act.wait_ge(sine_ps.sem, sine_ps.count(a_))
                    if begun(a_ - 1):
                        act.wait_ge(y_sb.sem, y_sb.count(a_ - 1))
                    nc.scalar.activation(
                        sine[:, :, :], bank("A", "sine")[0:CH, 0:NC_ * NQ].rearrange(
                            "p (t d) -> p t d", d=NQ), ACT.Copy).then_inc(sine_sb.sem, 1)
                if x_ is not None:
                    keep_xT(x_, 1)

            pipeline(act, run)

            act.wait_ge(fill_at_sb.sem, fill_at_sb.count(0))
            fill_regions(act, range(E // 2, E))
            act.wait_ge(slots_sb.sem, slots_sb.count(B - 1))
            nc.scalar.activation(gates[:, 0], gap[:, :], ACT.Exp).then_inc(exp_sb.sem, 1)

            def row_tile(j, p):
                act.wait_ge(xrT_ps.sem, xrT_ps.count(j))
                if begun(j - 2):
                    act.wait_ge(hid_ps.sem, hid_ps.count(j - 2))
                nc.scalar.activation(xrT[p][0:HD], ps[p][0:HD, 0:256].rearrange("p (h t) -> p h t", h=2),
                                     ACT.Copy).then_inc(xrT_sb.sem, 1)

            def hidden(j, p):
                act.wait_ge(hid_ps.sem, hid_ps.count(j, 0))
                if begun(j - 2):
                    act.wait_ge(out_ps.sem, out_ps.count(j - 2))
                nc.scalar.activation(hid[p][:, 0:4], ps[2 + 2 * p][:, :].rearrange("p (c t) -> p c t", c=4),
                                     ACT.Relu).then_inc(hid_a.sem, 1)

            row_tile(0, 0)
            row_tile(1, 1)

            def act_tile(j, p, jj):
                hidden(j, p)
                if not (isinstance(j, int) and j >= MAXTILES - 2):
                    row_tile(j + 2, p)

            tiles(act, act_tile)
            act.wait_ge(gates_sb.sem, gates_sb.count(0))
            for b in range(B):
                act.wait_ge(pair_in[b].sem, pair_in[b].count(0))
                for i in range(NC_):
                    t = NC_ * b + i
                    last = nc.scalar.activation(pairs[b][:, i, 0:D], pairs[b][:, i, 0:D], ACT.Copy,
                                                scale=gates[:, 1, t:t + 1])
                last.then_inc(scaled.sem, 1)

        @block.vector
        def _(dve):
            def causal_decay():
                dve.wait_ge(in_d.sem, in_d.count(0))
                dve.wait_ge(tables.sem, tables.count(0))
                nc.vector.tensor_tensor(decay[:, :, :], decay[:, :, :],
                                        diff_keep[:, 1:2].to_broadcast([CH, NH, CH]), ALU.mult
                                        ).then_inc(tables_d.sem, 1)
                dve.wait_ge(tables_d.sem, tables_d.count(0))

            def layernorm_stats(own_, b, n, k, src, done):
                apart(dve)
                for i in range(NC_):
                    last = nc.vector.bn_stats(stats[:, n, i], src(i))
                last.then_inc(own_.sem, 1)
                dve.wait_ge(own_.sem, own_.after(1))
                apart(dve)
                for i in range(NC_):
                    last = nc.vector.bn_aggr(mv[:, n, i], stats[:, n, i])
                last.then_inc(done.sem, 1)

            def norms_a(b):
                own_ln.begin(b)
                layernorm_stats(own_ln, b, 0, 0, lambda i: y[:, i], var_sb)
                dve.wait_ge(var_sb.sem, var_sb.count(b, 0))
                for i in range(NC_):
                    last = nc.vector.scalar_tensor_tensor(y[:, i], y[:, i], mv[:, 0, i, 0:1], rows[:, 0],
                                                          ALU.subtract, ALU.mult)
                last.then_inc(own_ln.sem, 1)
                yield
                dve.wait_ge(rstd_sb.sem, rstd_sb.count(b, 0))
                if begun(b - 1):
                    dve.wait_ge(hb_sb.sem, hb_sb.count(b - 1))
                dve.wait_ge(own_ln.sem, own_ln.after(1))
                for i in range(NC_):
                    last = nc.vector.scalar_tensor_tensor(h1[:, i], y[:, i], rstd[:, 0, i:i + 1], rows[:, 1],
                                                          ALU.mult, ALU.add)
                last.then_inc(h1_sb.sem, 1)
                dve.wait_ge(h1_sb.sem, h1_sb.count(b))
                layernorm_stats(own_ln, b, 1, 1, lambda i: h1[:, i], var_sb)
                yield
                dve.wait_ge(var_sb.sem, var_sb.count(b, 1))
                dve.wait_ge(rstd_sb.sem, rstd_sb.count(b, 1))
                if begun(b - 1):
                    dve.wait_ge(xnT_ps.sem, xnT_ps.count(b - 1))
                for i in range(NC_):
                    last = nc.vector.tensor_scalar(xn[:, i], h1[:, i], mv[:, 1, i, 0:1], rstd[:, 1, i:i + 1],
                                                   ALU.subtract, ALU.mult)
                last.then_inc(xn_sb.sem, 1)
                own_ln.end()

            def norms_c(c):
                own_c.begin(c)
                at = c * NC_

                def o(i):
                    g, k = (0, i) if i < 2 else (1, 0)
                    return bank("C", "o", g)[0:CH, k * D:(k + 1) * D]
                dve.wait_ge(o_ps.sem, o_ps.count(c))
                layernorm_stats(own_c, c, 2, 0, o, cvar_sb)
                dve.wait_ge(cvar_sb.sem, cvar_sb.count(c, 0))
                for i in range(NC_):
                    nc.vector.scalar_tensor_tensor(o_ln[:, i], o(i), mv[:, 2, i, 0:1], rows[:, 2],
                                                   ALU.subtract, ALU.mult).then_inc(o_free.sem, 1)
                yield
                dve.wait_ge(o_free.sem, o_free.count(c))
                dve.wait_ge(crstd_sb.sem, crstd_sb.count(c, 0))
                dve.wait_ge(hb_sb.sem, hb_sb.count(c))
                for i in range(NC_):
                    last = nc.vector.scalar_tensor_tensor(
                        resid[:, ds(at + i, 1), :], o_ln[:, i:i + 1], rstd[:, 2, i:i + 1],
                        resid[:, ds(at + i, 1), :], ALU.mult, ALU.add)
                last.then_inc(own_c.sem, 1)
                dve.wait_ge(own_c.sem, own_c.after(1))
                layernorm_stats(own_c, c, 3, 1,
                                lambda i: resid[:, ds(at + i, 1), :].rearrange("p o d -> p (o d)"), cvar_sb)
                yield
                dve.wait_ge(cvar_sb.sem, cvar_sb.count(c, 1))
                dve.wait_ge(crstd_sb.sem, crstd_sb.count(c, 1))
                if begun(c - 1):
                    dve.wait_ge(x2T_ps.sem, x2T_ps.count(c - 1))
                if begun(c - 1):
                    dve.wait_ge(scattered.sem, scattered.count(c - 1))
                for i in range(NC_):
                    last = nc.vector.tensor_scalar(x2[:, i:i + 1, 0:D], resid[:, ds(at + i, 1), :],
                                                   mv[:, 3, i, 0:1], rstd[:, 3, i:i + 1],
                                                   ALU.subtract, ALU.mult)
                last.then_inc(x2_sb.sem, 1)

            def tap(b, n):
                half, k = divmod(n, K)
                if k == 0:
                    dve.wait_ge(xT_sb.sem, xT_sb.count(b, 2 * half + 1))
                    if half == 0:
                        if begun(b - 1):
                            dve.wait_ge(pw_ps.sem, pw_ps.count(b - 1))
                    ins = nc.vector.tensor_scalar(conv[:, half], xT[:, half, 0:S_IN], w_dw[:, half, 0:1],
                                                  b_dw[:, half:half + 1], ALU.mult, ALU.add)
                else:
                    dve.wait_ge(tap_done.sem, tap_done.count(b, (K - 1) * half + k - 1))
                    ins = nc.vector.scalar_tensor_tensor(conv[:, half], xT[:, half, k:k + S_IN],
                                                         w_dw[:, half, k:k + 1], conv[:, half], ALU.mult, ALU.add)
                if k < K - 1:
                    ins.then_inc(tap_done.sem, 1)
                else:
                    ins.then_inc(conv_sb.sem, 1)

            def choose(c):
                one, two_ = pick[:, 0], pick[:, 1]
                def bc(x):
                    return x.unsqueeze(2).to_broadcast([CH, NC_, E])
                dve.wait_ge(lg_ps.sem, lg_ps.count(c))
                if begun(c - 1):
                    dve.wait_ge(rank_ps.sem, rank_ps.count(c - 1))
                if begun(c - 1):
                    dve.wait_ge(slots_sb.sem, slots_sb.count(c - 1))
                nc.vector.tensor_tensor(logit[:, :, :], bank("C", "lg")[0:CH, 0:NC_ * E].rearrange(
                    "p (t e) -> p t e", e=E), small[:, 0], ALU.add).then_inc(lg_sb.sem, 1)
                dve.wait_ge(lg_sb.sem, lg_sb.count(c))
                nc.vector.tensor_reduce(top[:, 0], logit[:, :, :], AX.X, ALU.max).then_inc(own_c.sem, 1)
                dve.wait_ge(own_c.sem, own_c.after(1))
                nc.vector.tensor_tensor(hit[:, :, :], logit[:, :, :], bc(top[:, 0]), ALU.is_equal
                                        ).then_inc(own_c.sem, 1)
                dve.wait_ge(own_c.sem, own_c.after(1))
                nc.vector.tensor_tensor(hit[:, :, :], hit[:, :, :], small[:, 1], ALU.mult
                                        ).then_inc(own_c.sem, 1)
                dve.wait_ge(own_c.sem, own_c.after(1))
                nc.vector.tensor_reduce(top[:, 1], hit[:, :, :], AX.X, ALU.max).then_inc(own_c.sem, 1)
                dve.wait_ge(own_c.sem, own_c.after(1))
                nc.vector.tensor_tensor(one, small[:, 1], bc(top[:, 1]), ALU.is_equal).then_inc(own_c.sem, 1)
                dve.wait_ge(own_c.sem, own_c.after(1))
                nc.vector.scalar_tensor_tensor(logit2[:, :, :], one, -3.0e38, logit[:, :, :],
                                                          ALU.mult, ALU.add).then_inc(own_c.sem, 1)
                dve.wait_ge(own_c.sem, own_c.after(1))
                nc.vector.tensor_reduce(top[:, 2], logit2[:, :, :], AX.X, ALU.max).then_inc(own_c.sem, 1)
                dve.wait_ge(own_c.sem, own_c.after(1))
                nc.vector.tensor_tensor(hit[:, :, :], logit2[:, :, :], bc(top[:, 2]), ALU.is_equal
                                        ).then_inc(own_c.sem, 1)
                dve.wait_ge(own_c.sem, own_c.after(1))
                nc.vector.tensor_tensor(hit[:, :, :], hit[:, :, :], small[:, 1], ALU.mult
                                        ).then_inc(own_c.sem, 1)
                dve.wait_ge(own_c.sem, own_c.after(1))
                nc.vector.tensor_reduce(top[:, 3], hit[:, :, :], AX.X, ALU.max).then_inc(own_c.sem, 1)
                dve.wait_ge(own_c.sem, own_c.after(1))
                nc.vector.tensor_tensor(two_, small[:, 1], bc(top[:, 3]), ALU.is_equal).then_inc(own_c.sem, 1)
                dve.wait_ge(own_c.sem, own_c.after(1))
                nc.vector.tensor_tensor(picked[:, :, :], one, two_, ALU.add).then_inc(pick_sb.sem, 1)
                nc.vector.tensor_tensor(gap[:, ds(c * NC_, NC_)], top[:, 2], top[:, 0], ALU.subtract)
                nc.vector.tensor_copy(x2[:, :, D:D + 1], tok2[:, ds(c * NC_, NC_)].unsqueeze(2))
                nc.vector.tensor_scalar(x2[:, :, D + 1:D + 2], top[:, 1].unsqueeze(2), -1.0, float(E),
                                                   ALU.mult, ALU.add).then_inc(own_c.sem, 1)

            def place(c):
                dve.wait_ge(rank_ps.sem, rank_ps.count(c))
                nc.vector.tensor_tensor(row_of[:, :, :], bank("C", "rank")[0:CH, 0:NC_ * E].rearrange(
                    "p (t e) -> p t e", e=E), small[:, 2], ALU.add).then_inc(rank_sb.sem, 1)
                nc.vector.tensor_reduce(tile_sum[:, :], picked[:, :, :].rearrange("p t e -> p e t"),
                                                   AX.X, ALU.add).then_inc(own_c.sem, 1)
                dve.wait_ge(rank_sb.sem, rank_sb.count(c))
                dve.wait_ge(own_c.sem, own_c.after(2))
                nc.vector.tensor_tensor(
                    row_hit[:, :, :, :], pick[:, :, :, :],
                    row_of[:, :, :].unsqueeze(1).to_broadcast([CH, 2, NC_, E]), ALU.mult).then_inc(own_c.sem, 1)
                nc.vector.tensor_tensor(counts[:, :], counts[:, :], tile_sum[:, :], ALU.add
                                        ).then_inc(counts_sb.sem, 1)
                dve.wait_ge(own_c.sem, own_c.after(1))
                nc.vector.tensor_reduce(slots_f[:, :, :], row_hit[:, :, :, :], AX.X, ALU.add
                                        ).then_inc(own_c.sem, 1)
                dve.wait_ge(own_c.sem, own_c.after(1))
                nc.vector.tensor_copy(slots[:, :, :], slots_f[:, :, :]).then_inc(slots_sb.sem, 1)
                own_c.end()

            def apply_decay(b, g):
                i, h0 = g // 4, HG * (g % 4)
                dve.wait_ge(sc_ps.sem, sc_ps.count(b, g))
                if g == 0:
                    if begun(b - 1):
                        dve.wait_ge(av_ps.sem, av_ps.count(b - 1))
                nc.vector.tensor_tensor(
                    scores[:, i, h0:h0 + HG], bank("B", "sc", g)[0:CH, 0:HG * CH].rearrange(
                        "p (h n) -> p h n", n=CH), decay[:, h0:h0 + HG], ALU.mult
                ).then_inc(sc_sb.sem, 1)

            def pool_pairs(a_, u):
                lo = POOL_CUT[0] * u
                dve.wait_ge(pw_sb.sem, pw_sb.count(a_, 2 * u + 1))
                if u == 0:
                    if begun(a_ - 1):
                        dve.wait_ge(chan_ps.sem, chan_ps.count(a_ - 1))
                v = pw[:, :, 2 * lo:2 * (lo + POOL_CUT[u])].rearrange("p h (s t) -> p h s t", t=2)
                nc.vector.tensor_tensor(pooled[:, :, lo:lo + POOL_CUT[u]], v[:, :, :, 0], v[:, :, :, 1],
                                        ALU.max).then_inc(pooled_sb.sem, 1)

            def keep_state(b, i):
                dve.wait_ge(st_ps.sem, st_ps.count(b, i))
                ins = nc.vector.tensor_tensor(
                    state[:, i], bank("B", "st", i)[0:HD, 0:D].rearrange("p (h s) -> p h s", h=2),
                    head_mask[:, :, :].rearrange("p h s -> p (h s)").unsqueeze(1).to_broadcast([HD, 2, HD]),
                    ALU.mult)
                if i == 0:
                    ins.then_inc(st_sb.sem, 1)
                else:
                    own_st.begin(b)
                    ins.then_inc(own_st.sem, 1)
                    dve.wait_ge(own_st.sem, own_st.after(1))
                    own_st.end()
                    dve.wait_ge(st_sb.sem, st_sb.count(b, 0))
                    for half in range(2):
                        ins = nc.vector.scalar_tensor_tensor(
                            state[:, i, half], state[:, i - 1, half], carry[:, half:half + 1],
                            state[:, i, half], ALU.mult, ALU.add)
                    ins.then_inc(st_sb.sem, 1)

            def apply_gate(b, i):
                dve.wait_ge(av_ps.sem, av_ps.count(b, i))
                if i == 0:
                    dve.wait_ge(g_sb.sem, g_sb.count(b))
                    if begun(b - 1):
                        dve.wait_ge(o_ps.sem, o_ps.count(b - 1))
                nc.vector.scalar_tensor_tensor(
                    gated[:, :, CH * i:CH * (i + 1)], gate[:, :, CH * i:CH * (i + 1)], 1.0,
                    bank("C", "av", i)[0:HD, 0:2 * CH].rearrange("p (g n) -> p g n", n=CH),
                    ALU.add, ALU.mult).then_inc(av_sb.sem, 1)

            def spectrum(a_):
                dve.wait_ge(sine_sb.sem, sine_sb.count(a_))
                dve.wait_ge(cosine_ps.sem, cosine_ps.count(a_))
                p_ = bank("A", "cosine")[0:CH, 0:NC_ * NP].rearrange("p (t d) -> p t d", d=NP)
                nc.vector.tensor_copy(y[:, :, 0:NP:NP - 1], p_[:, :, 0:NP:NP - 1])
                nc.vector.tensor_tensor(y[:, :, 1:NP - 1], p_[:, :, 1:NP - 1], sine[:, :, :], ALU.subtract)
                nc.vector.tensor_tensor(y[:, :, NP:D], p_[:, :, 1:NP - 1], sine[:, :, :], ALU.add
                                        ).then_inc(y_sb.sem, 1)
                dve.wait_ge(y_sb.sem, y_sb.count(a_))

            def run(x_, a_, b, c):
                if first(a_):
                    dve.wait_ge(in_a.sem, in_a.count(0))
                if first(b):
                    dve.wait_ge(in_b.sem, in_b.count(0))
                if first(c):
                    dve.wait_ge(in_c.sem, in_c.count(0))
                    dve.wait_ge(zeroed.sem, 3)
                norming = norms_c(c) if c is not None else iter(())
                if a_ is not None:
                    tap(a_, AHEAD)
                next(norming, None)
                if a_ is not None:
                    for n in range(AHEAD + 1, AHEAD + 3):
                        tap(a_, n)
                next(norming, None)
                if a_ is not None:
                    for n in range(AHEAD + 3, AHEAD + 5):
                        tap(a_, n)
                next(norming, None)
                if a_ is not None:
                    for n in range(AHEAD + 5, 2 * K):
                        tap(a_, n)
                if first(a_):
                    causal_decay()
                if a_ is None and b is not None:
                    for g in range(6):
                        apply_decay(b, g)
                if c is not None:
                    choose(c)
                if a_ is None and b is not None:
                    for g in range(6, 9):
                        apply_decay(b, g)
                if first(x_):
                    dve.wait_ge(in_w.sem, in_w.count(0))
                    dve.wait_ge(zeroed.sem, 1)
                if a_ is not None:
                    pool_pairs(a_, 0)
                if x_ is not None:
                    tap(x_, 0)
                if a_ is not None:
                    pool_pairs(a_, 1)
                if c is not None:
                    place(c)
                if a_ is not None and b is not None:
                    for g in range(6):
                        apply_decay(b, g)
                if x_ is not None:
                    tap(x_, 1)
                    tap(x_, 2)
                if b is not None:
                    if a_ is not None:
                        for g in range(6, 9):
                            apply_decay(b, g)
                    keep_state(b, 0)
                    keep_state(b, 1)
                if x_ is not None:
                    for n in range(3, AHEAD):
                        tap(x_, n)
                norming = norms_a(a_) if a_ is not None else iter(())
                if a_ is not None:
                    spectrum(a_)
                next(norming, None)
                if b is not None:
                    for g in range(9, 4 * NC_):
                        apply_decay(b, g)
                next(norming, None)
                if b is not None:
                    for i in range(NC_):
                        apply_gate(b, i)
                next(norming, None)

            pipeline(dve, run)

            own_t.begin(0)
            dve.wait_ge(n_ps.sem, n_ps.count(0))
            nc.vector.tensor_copy(n_f[:, :], ps[0][:, 0:E]).then_inc(own_t.sem, 1)
            dve.wait_ge(own_t.sem, own_t.after(1))
            nc.vector.tensor_tensor(fill_at[0:1, :], n_f[0:1, :], small[0:1, 2, 0], ALU.add
                                    ).then_inc(fill_at_sb.sem, 1)
            nc.vector.tensor_scalar(n_i[:, 0], n_f[:, :], 127.0, None, ALU.add).then_inc(own_t.sem, 1)
            dve.wait_ge(own_t.sem, own_t.after(1))
            nc.vector.tensor_scalar(n_i[:, 1], n_i[:, 0], 7, None, ALU.logical_shift_right
                                    ).then_inc(own_t.sem, 1)
            dve.wait_ge(own_t.sem, own_t.after(1))
            nc.vector.tensor_copy(nt_f[:, :], n_i[:, 1]).then_inc(own_t.sem, 1)
            dve.wait_ge(own_t.sem, own_t.after(1))
            nc.vector.tensor_tensor_scan(end_f[:, :], ones[:, 0:E], nt_f[:, :], 0.0, ALU.mult, ALU.add
                                         ).then_inc(own_t.sem, 1)
            dve.wait_ge(own_t.sem, own_t.after(1))
            j8 = jcol[:, :].unsqueeze(2).to_broadcast([128, MAXTILES, E])
            nc.vector.tensor_tensor(past[:, :, :], j8, end_f[:, :].unsqueeze(1).to_broadcast([128, MAXTILES, E]),
                                    ALU.is_ge).then_inc(own_t.sem, 1)
            dve.wait_ge(own_t.sem, own_t.after(1))
            nc.vector.tensor_tensor(past_n[:, :, :], past[:, :, :],
                                    nt_f[:, :].unsqueeze(1).to_broadcast([128, MAXTILES, E]), ALU.mult
                                    ).then_inc(own_t.sem, 1)
            dve.wait_ge(own_t.sem, own_t.after(1))
            nc.vector.tensor_reduce(e_of[:, :], past[:, :, 0:E - 1], AX.X, ALU.add).then_inc(own_t.sem, 1)
            dve.wait_ge(own_t.sem, own_t.after(1))
            nc.vector.tensor_reduce(tiles_before[:, :], past_n[:, :, 0:E - 1], AX.X, ALU.add
                                    ).then_inc(own_t.sem, 1)
            dve.wait_ge(own_t.sem, own_t.after(1))
            nc.vector.scalar_tensor_tensor(blk[:, 0], e_of[:, :], float(REGION // 128), jcol[:, :],
                                           ALU.mult, ALU.add).then_inc(own_t.sem, 1)
            dve.wait_ge(own_t.sem, own_t.after(1))
            nc.vector.tensor_tensor(blk[:, 0], blk[:, 0], tiles_before[:, :], ALU.subtract
                                    ).then_inc(own_t.sem, 1)
            dve.wait_ge(own_t.sem, own_t.after(1))
            nc.vector.tensor_scalar(blk[:, 1], blk[:, 0], -1.0, float(EMPTY // 128), ALU.mult, ALU.add
                                    ).then_inc(own_t.sem, 1)
            dve.wait_ge(own_t.sem, own_t.after(1))
            nc.vector.tensor_tensor(blk[:, 1], blk[:, 1], past[:, :, E - 1], ALU.mult).then_inc(own_t.sem, 1)
            dve.wait_ge(own_t.sem, own_t.after(1))
            nc.vector.tensor_tensor(blk[:, 2], blk[:, 1], blk[:, 0], ALU.add).then_inc(own_t.sem, 1)
            dve.wait_ge(own_t.sem, own_t.after(1))
            nc.vector.tensor_scalar(table[0:1, 1], blk[0:1, 2], 128.0, None, ALU.mult).then_inc(own_t.sem, 1)
            dve.wait_ge(own_t.sem, own_t.after(1))
            own_t.end()
            nc.vector.tensor_copy(table[0:1, 0], e_of[0:1, :]).then_inc(table_sb.sem, 1)
            dve.wait_ge(table_sb.sem, table_sb.count(0))
            dve.wait_ge(exp_sb.sem, exp_sb.count(0))
            own_g.begin(0)
            nc.vector.tensor_scalar(gates[:, 2], gates[:, 0], 1.0, None, ALU.add).then_inc(own_g.sem, 1)
            dve.wait_ge(own_g.sem, own_g.after(1))
            nc.vector.reciprocal(gates[:, 1], gates[:, 2]).then_inc(own_g.sem, 1)
            dve.wait_ge(own_g.sem, own_g.after(1))
            nc.vector.tensor_tensor(gates[:, 2], gates[:, 0], gates[:, 1], ALU.mult).then_inc(gates_sb.sem, 1)
            dve.wait_ge(gates_sb.sem, gates_sb.count(0))
            own_g.end()
            dve.wait_ge(b2_in.sem, b2_in.count(0))

            def destination(j, p, jj):
                dve.wait_ge(row_in[p].sem, row_in[p].count(jj))
                nc.vector.scalar_tensor_tensor(dest_f[:, ds(j, 1)], xr[p][:, D + 1:D + 2], e_of[:, ds(j, 1)],
                                               xr[p][:, D:D + 1], ALU.not_equal, ALU.add
                                               ).then_inc(dest_sb.sem, 1)

            destination(0, 0, 0)
            destination(1, 1, 0)

            def dve_tile(j, p, jj):
                e = dve.value_load(table[0:1, 0, ds(j, 1)], min_val=0, max_val=E - 1)
                dve.wait_ge(hid_ps.sem, hid_ps.count(j, 1))
                if begun(j - 2):
                    dve.wait_ge(out_ps.sem, out_ps.count(j - 2))
                nc.vector.tensor_scalar(hid[p][:, 4:FC], ps[3 + 2 * p][:, 0:256].rearrange(
                    "p (c t) -> p c t", c=2), 0.0, None, ALU.max).then_inc(hid_b.sem, 1)
                if not (isinstance(j, int) and j >= MAXTILES - 2):
                    destination(j + 2, p, jj + 1)
                if begun(jj - 1):
                    dve.wait_ge(sent[p].sem, sent[p].count(jj - 1))
                dve.wait_ge(dest_sb.sem, dest_sb.count(j))
                nc.vector.tensor_copy(dest[p][:, :], dest_f[:, ds(j, 1)])
                dve.wait_ge(out_ps.sem, out_ps.count(j))
                nc.vector.tensor_tensor(yo[p][:, :], ps[6 + p][:, 0:D], b2_rows[:, ds(e, 1), :].rearrange(
                    "p o d -> p (o d)"), ALU.add).then_inc(out_sb.sem, 1)

            tiles(dve, dve_tile)

            for b in range(B):
                dve.wait_ge(pair_in[b].sem, pair_in[b].count(0))
                own_m.begin(b)
                for i in range(NC_):
                    t = NC_ * b + i
                    last = nc.vector.scalar_tensor_tensor(resid[:, t], pairs[b][:, i, D:2 * D],
                                                          gates[:, 2, t:t + 1], resid[:, t], ALU.mult, ALU.add)
                last.then_inc(own_m.sem, 1)
                dve.wait_ge(own_m.sem, own_m.after(1))
                own_m.end()
                dve.wait_ge(scaled.sem, scaled.count(b))
                nc.vector.tensor_tensor(resid[:, NC_ * b:NC_ * (b + 1), :], pairs[b][:, :, 0:D],
                                        resid[:, NC_ * b:NC_ * (b + 1), :], ALU.add).then_inc(mixed.sem, 1)

        @block.tensor
        def _(pe):
            mm, tr = nc.tensor.matmul, nc.tensor.transpose

            def gate_weights():
                for half in range(2):
                    last = mm(ps[2 + half][0:HD, 0:D], w_g1[:, half, :], w_g2[:, :], start=True, stop=True)
                last.then_inc(wg_ps.sem, 1)
                pe.wait_ge(wg_sb.sem, wg_sb.count(0))

            def keep_clock(products):
                for _ in range(products):
                    mm(ps[7][:, 0:128], ident[:, :], ident[:, :], start=True, stop=True, skip_group_check=True)

            def transpose_x(b, half):
                pe.wait_ge(x_in.sem, x_in.count(b))
                for u in range(2):
                    g = 2 * half + u
                    if shared("A", "xT", g, b):
                        pe.wait_ge(*drained("A", "xT", g, b))
                    for t in range(XT // 2):
                        last = tr(bank("A", "xT", g)[0:HD, CH * t:CH * (t + 1)],
                                  x_rows[:, XT // 2 * u + t, HD * half:HD * (half + 1)], ident[0:CH, 0:CH])
                    last.then_inc(xT_ps.sem, 1)

            def pointwise(b):
                pe.wait_ge(conv_sb.sem, conv_sb.count(b))
                for g in range(4):
                    u, half = divmod(g, 2)
                    lo, n = 2 * POOL_CUT[0] * u, 2 * POOL_CUT[u]
                    if shared("A", "pw", g, b):
                        pe.wait_ge(*drained("A", "pw", g, b))
                    for k in range(2):
                        last = mm(bank("A", "pw", g)[0:HD, 0:n], w_pw[:, k, HD * half:HD * (half + 1)],
                                  conv[:, k, lo:lo + n], start=(k == 0), stop=(k == 1))
                    last.then_inc(pw_ps.sem, 1)

            def dft_channels(b):
                pe.wait_ge(pooled_sb.sem, pooled_sb.count(b))
                for g, ts in enumerate(((0, 1), (2,))):
                    if shared("A", "chan", g, b):
                        pe.wait_ge(*drained("A", "chan", g, b))
                    for i, t in enumerate(ts):
                        for k in range(2):
                            last = mm(bank("A", "chan", g)[0:CH, D * i:D * (i + 1)],
                                      pooled[:, k, CH * t:CH * (t + 1)], dft_c[:, k, :],
                                      start=(k == 0), stop=(k == 1))
                    last.then_inc(chan_ps.sem, 1)

            def dft_positions(b):
                pe.wait_ge(chan_sb.sem, chan_sb.count(b))
                for name, w, lo, n, done in (("sine", sin_s, NP, NQ, sine_ps), ("cosine", cos_s, 0, NP, cosine_ps)):
                    if shared("A", name, 0, b):
                        pe.wait_ge(*drained("A", name, 0, b))
                    for j in range(NC_):
                        for t in range(NC_):
                            last = mm(bank("A", name)[0:CH, n * j:n * (j + 1)],
                                      w[:, t, CH * j:CH * (j + 1)], chan[:, t, lo:lo + n],
                                      start=(t == 0), stop=(t == NC_ - 1))
                    last.then_inc(done.sem, 1)

            def transpose_xn(b):
                pe.wait_ge(xn_sb.sem, xn_sb.count(b))
                for half in range(2):
                    if shared("B", "xnT", half, b):
                        pe.wait_ge(*drained("B", "xnT", half, b))
                    for i in range(NC_):
                        last = tr(bank("B", "xnT", half)[0:HD, CH * i:CH * (i + 1)],
                                  xn[:, i, HD * half:HD * (half + 1)], ident[0:CH, 0:CH])
                    last.then_inc(xnT_ps.sem, 1)

            def project(b):
                rows_of_xnT(b, "q", w_q, q_ps)
                rows_of_xnT(b, "k", w_k, k_ps)
                for i in range(NC_):
                    if shared("B", "v", i, b):
                        pe.wait_ge(*drained("B", "v", i, b))
                    for k in range(2):
                        last = mm(bank("B", "v", i)[0:CH, 0:D], xnT[:, k, CH * i:CH * (i + 1)], w_v[:, k, :],
                                  start=(k == 0), stop=(k == 1))
                    last.then_inc(v_ps.sem, 1)
                rows_of_xnT(b, "g", w_g, g_ps)
                pe.wait_ge(k_sb.sem, k_sb.count(b))
                if shared("B", "kt", 0, b):
                    pe.wait_ge(*drained("B", "kt", 0, b))
                for i in range(NC_ - 1):
                    for half in range(2):
                        lo = D * i + HD * half
                        last = tr(bank("B", "kt")[0:CH, lo:lo + HD], kT[:, half, CH * i:CH * (i + 1)],
                                  ident[0:HD, 0:HD])
                last.then_inc(kt_ps.sem, 1)

            def rows_of_xnT(b, name, w, done):
                for half in range(2):
                    if shared("B", name, half, b):
                        pe.wait_ge(*drained("B", name, half, b))
                    for k in range(2):
                        if name == "q" and half == 0:
                            pe.wait_ge(xnT_sb.sem, xnT_sb.count(b, k))
                        last = mm(bank("B", name, half)[0:HD, 0:S], w[:, k, HD * half:HD * (half + 1)],
                                  xnT[:, k, :], start=(k == 0), stop=(k == 1))
                    last.then_inc(done.sem, 1)

            def score(b, groups):
                if groups[0] == 0:
                    pe.wait_ge(qb_in.sem, qb_in.count(b))
                for g in groups:
                    i, q = divmod(g, 4)
                    half, h0 = divmod(HG * q, HH)
                    if shared("B", "sc", g, b):
                        pe.wait_ge(*drained("B", "sc", g, b))
                    mm(bank("B", "sc", g)[0:CH, 0:HG * CH], kT[:, half, CH * i:CH * (i + 1)],
                       q_block[:, half, h0:h0 + HG, CH * i:CH * (i + 1)], start=True, stop=True
                       ).then_inc(sc_ps.sem, 1)

            def chunk_states(b):
                pe.wait_ge(v_sb.sem, v_sb.count(b))
                pe.wait_ge(k_dec_sb.sem, k_dec_sb.count(b))
                for i in range(NC_ - 1):
                    if shared("B", "st", i, b):
                        pe.wait_ge(*drained("B", "st", i, b))
                    for half in range(2):
                        last = mm(bank("B", "st", i)[0:HD, HD * half:HD * (half + 1)],
                                  k_dec[:, i, HD * half:HD * (half + 1)],
                                  v_pad[:, i, HP * half:HP * (half + 1), :].rearrange(
                                      "p q (j d) -> p q j d", j=2)[:, :, :, 0:DH],
                                  start=True, stop=True)
                    last.then_inc(st_ps.sem, 1)

            def attend(b, i):
                o = bank("C", "av", i)
                pe.wait_ge(sc_sb.sem, sc_sb.count(b, 4 * i + 3))
                if shared("C", "av", i, b):
                    pe.wait_ge(*drained("C", "av", i, b))
                if i:
                    pe.wait_ge(q_dec_sb.sem, q_dec_sb.count(b))
                    pe.wait_ge(st_sb.sem, st_sb.count(b, i - 1))
                for half in range(2):
                    cols = slice(CH * half, CH * (half + 1))
                    if i:
                        mm(o[0:HD, cols], state[:, i - 1, half, :], q_dec[:, half, CH * (i - 1):CH * i],
                           start=True, stop=False, skip_group_check=True)
                    for j in range(2):
                        for q in range(HP):
                            last = mm(o[2 * DH * q:2 * DH * (q + 1), cols],
                                      v_pad[:, i, HP * half + q, 2 * DH * j:2 * DH * (j + 1)],
                                      scores[:, i, HH * half + 2 * q + j, :],
                                      start=(i == 0 and j == 0), stop=(j == 1), skip_group_check=True)
                last.then_inc(av_ps.sem, 1)

            def output(c, g):
                chunks = (0, 1) if g == 0 else (2,)
                pe.wait_ge(av_sb.sem, av_sb.count(c, chunks[-1]))
                if shared("C", "o", g, c):
                    pe.wait_ge(*drained("C", "o", g, c))
                for i, t in enumerate(chunks):
                    for k in range(2):
                        last = mm(bank("C", "o", g)[0:CH, D * i:D * (i + 1)], gated[:, k, CH * t:CH * (t + 1)],
                                  w_o[:, k, :], start=(k == 0), stop=(k == 1))
                last.then_inc(o_ps.sem, 1)

            def transpose_x2(c):
                pe.wait_ge(x2_sb.sem, x2_sb.count(c))
                for half in range(2):
                    if shared("C", "x2T", half, c):
                        pe.wait_ge(*drained("C", "x2T", half, c))
                    for i in range(NC_):
                        last = tr(bank("C", "x2T", half)[0:HD, CH * i:CH * (i + 1)],
                                  x2[:, i, HD * half:HD * (half + 1)], ident[0:CH, 0:CH])
                    last.then_inc(x2T_ps.sem, 1)

            def router(c):
                pe.wait_ge(x2T_sb.sem, x2T_sb.count(c))
                if shared("C", "lg", 0, c):
                    pe.wait_ge(*drained("C", "lg", 0, c))
                for i in range(NC_):
                    for k in range(2):
                        last = mm(bank("C", "lg")[0:CH, E * i:E * (i + 1)], x2T[:, k, CH * i:CH * (i + 1)],
                                  w_r[:, k, :], start=(k == 0), stop=(k == 1))
                last.then_inc(lg_ps.sem, 1)

            def rank(c):
                pe.wait_ge(pick_sb.sem, pick_sb.count(c))
                if begun(c - 1):
                    pe.wait_ge(counts_sb.sem, counts_sb.count(c - 1))
                if shared("C", "rank", 0, c):
                    pe.wait_ge(*drained("C", "rank", 0, c))
                o = bank("C", "rank")
                flat = picked[:, :, :].rearrange("p t e -> p (t e)")
                mm(o[0:CH, 0:NC_ * E], tri[:, :], flat, start=True, stop=False, skip_group_check=True)
                mm(o[0:CH, 0:NC_ * E], ones[0:CH, 0:CH], counts[:, :].unsqueeze(1).to_broadcast([CH, NC_, E]),
                   start=False, stop=False, skip_group_check=True)
                mm(o[0:CH, 2 * E:3 * E], ones[0:CH, 0:CH], flat[:, 0:E], start=False, stop=False,
                   skip_group_check=True)
                mm(o[0:CH, E:3 * E], ones[0:CH, 0:CH], flat[:, 0:2 * E], start=False, stop=True,
                   skip_group_check=True).then_inc(rank_ps.sem, 1)

            def run(x_, a_, b, c):
                if first(x_):
                    pe.wait_ge(ident_in.sem, ident_in.count(0))
                if first(a_):
                    pe.wait_ge(in_a.sem, in_a.count(0))
                if first(b):
                    pe.wait_ge(in_b.sem, in_b.count(0))
                    gate_weights()
                if first(c):
                    pe.wait_ge(in_c.sem, in_c.count(0))
                if c is not None:
                    output(c, 0)
                if first(b):
                    keep_clock(18)
                if b is not None:
                    transpose_xn(b)
                if c is not None:
                    output(c, 1)
                if b is not None:
                    project(b)
                if c is not None:
                    if b is None:
                        keep_clock(33)
                    transpose_x2(c)
                if x_ is not None:
                    transpose_x(x_, 0)
                if a_ is None and b is not None:
                    score(b, range(0, 6))
                if c is not None:
                    router(c)
                if a_ is not None:
                    if first(a_):
                        keep_clock(22)
                    pointwise(a_)
                elif b is not None:
                    score(b, range(6, 9))
                if c is not None:
                    if b is None:
                        keep_clock(12)
                    rank(c)
                if a_ is not None and b is not None:
                    score(b, range(0, 6))
                if a_ is not None:
                    dft_channels(a_)
                if b is not None:
                    if a_ is not None:
                        score(b, range(6, 9))
                    chunk_states(b)
                if a_ is not None:
                    dft_positions(a_)
                if b is not None:
                    attend(b, 0)
                    score(b, range(9, 4 * NC_))
                    attend(b, 1)
                    attend(b, 2)
                if x_ is not None:
                    transpose_x(x_, 1)

            pipeline(pe, run)

            pe.wait_ge(counts_sb.sem, counts_sb.count(B - 1))
            mm(ps[0][:, 0:E], ones[0:CH, :], counts[:, :], start=True, stop=True).then_inc(n_ps.sem, 1)
            keep_clock(54)
            pe.wait_ge(table_sb.sem, table_sb.count(0))
            pe.wait_ge(w2_in.sem, w2_in.count(0))
            pe.wait_ge(zeroed.sem, 4)

            def up(j, p, jj):
                pe.wait_ge(w1_in[p].sem, w1_in[p].count(jj))
                pe.wait_ge(xrT_sb.sem, xrT_sb.count(j))
                if begun(j - 2):
                    pe.wait_ge(hid_a.sem, hid_a.count(j - 2))
                if begun(j - 2):
                    pe.wait_ge(hid_b.sem, hid_b.count(j - 2))
                for m in range(FC):
                    dst = ps[2 + 2 * p][:, 128 * m:128 * (m + 1)] if m < 4 else \
                        ps[3 + 2 * p][:, 128 * (m - 4):128 * (m - 3)]
                    for k in range(2):
                        n = HD + 1 - k
                        last = mm(dst, w1[p][0:n, k, 128 * m:128 * (m + 1)], xrT[p][0:n, k, :],
                                  start=(k == 0), stop=(k == 1))
                    if m in (3, FC - 1):
                        last.then_inc(hid_ps.sem, 1)

            def down(j, p):
                e = pe.value_load(table[0:1, 0, ds(j, 1)], min_val=0, max_val=E - 1)
                pe.wait_ge(hid_a.sem, hid_a.count(j))
                pe.wait_ge(hid_b.sem, hid_b.count(j))
                if begun(j - 2):
                    pe.wait_ge(out_sb.sem, out_sb.count(j - 2))
                for m in range(FC):
                    last = mm(ps[6 + p][:, 0:D], hid[p][:, m, :],
                              w2[:, ds(e, 1), m, :].rearrange("p o d -> p (o d)"),
                              start=(m == 0), stop=(m == FC - 1))
                last.then_inc(out_ps.sem, 1)

            def tile_step(j, p, jj):
                if not (isinstance(j, int) and j + 1 >= MAXTILES):
                    up(j + 1, 1 - p, jj + p)
                if not (isinstance(j, int) and j + 2 >= MAXTILES):
                    pe.wait_ge(row_in[p].sem, row_in[p].count(jj + 1))
                    xrT_in(j + 2, p)
                down(j, p)

            def xrT_in(j, p):
                if begun(j - 2):
                    pe.wait_ge(xrT_sb.sem, xrT_sb.count(j - 2))
                for half in range(2):
                    last = tr(ps[p][0:HD, 128 * half:128 * (half + 1)], xr[p][:, HD * half:HD * (half + 1)],
                              ident[:, :])
                last.then_inc(xrT_ps.sem, 1)

            pe.wait_ge(row_in[0].sem, row_in[0].count(0))
            xrT_in(0, 0)
            pe.wait_ge(row_in[1].sem, row_in[1].count(0))
            xrT_in(1, 1)
            up(0, 0, 0)
            tiles(pe, tile_step)


def tables():
    f = np.float32
    order = channel_order()
    k = np.arange(D)
    turn = 2 * np.pi * ((k[:, None] * k[None, :]) % D) / D
    dft_c = np.concatenate([np.cos(turn)[:, 0:NP], np.sin(turn)[:, 1:NQ + 1]], 1)
    s = np.arange(S)
    turn = 2 * np.pi * ((s[:, None] * s[None, :]) % S) / S
    seq = lambda m: m.reshape(NC_, CH, S).transpose(1, 0, 2).astype(f)
    n = np.arange(CH)
    diff = n[None, :] - n[:, None]
    ch = np.arange(HD)
    tile = np.arange(NT)
    return dict(
        ident=np.eye(128, dtype=f), dft_c=halves(dft_c.astype(f)),
        cos_s=seq(np.cos(turn)), sin_s=seq(np.sin(turn)),
        code=np.tile(E - np.arange(E), (NC_, 1)).astype(f),
        region=np.tile(REGION * np.arange(E), (NC_, 1)).astype(f),
        to_end=(CH - n)[:, None].astype(f), pos=n.astype(f), tri=(n[:, None] < n[None, :]).astype(f),
        head_mask=np.repeat((0.5 * (ch[:, None] // DH == np.arange(HH)[None, :])).astype(f)[:, :, None], DH, 2),
        tok2=(2 * (tile[None, :] * CH + n[:, None])).astype(f), jcol=np.arange(MAXTILES).astype(f),
        diff=np.maximum(diff, 0).astype(f), keep=(0.5 * (diff >= 0)).astype(f)), order


def halves(w):
    return np.ascontiguousarray(w.reshape(2, HD, *w.shape[1:]).swapaxes(0, 1))


def kernel(x, L0_tok_w_dw, L0_tok_b_dw, L0_tok_w_pw, L0_tok_b_pw, L0_tok_gamma, L0_tok_beta, L0_attn_log_slope,
           L0_attn_Wq, L0_attn_Wk, L0_attn_Wv, L0_attn_Wo, L0_attn_Wg1, L0_attn_Wg2, L0_attn_ln_w, L0_attn_ln_b,
           L0_ffn_Wg, L0_ffn_bg, L0_ffn_W1, L0_ffn_b1, L0_ffn_W2, L0_ffn_b2):
    import concourse.bacc as bacc
    from concourse.bass_utils import run_bass_kernel_spmd as run

    arrays, o = tables()
    g = np.asarray
    arrays |= dict(
        x=g(x), w_dw=halves(g(L0_tok_w_dw)[:, 0, :]), b_dw=halves(g(L0_tok_b_dw)),
        w_pw=halves(g(L0_tok_w_pw)[:, :, 0].T), b_pw=halves(g(L0_tok_b_pw)),
        rows=np.stack([g(v)[o] for v in (L0_tok_gamma, L0_tok_beta, L0_attn_ln_w, L0_attn_ln_b)]),
        w_q=halves(g(L0_attn_Wq)[o]), w_k=halves(g(L0_attn_Wk)[o]),
        w_v=halves(g(L0_attn_Wv)[o]),
        w_g1=g(L0_attn_Wg1)[o].T.reshape(G, 2, HD), w_g2=g(L0_attn_Wg2),
        w_o=halves(g(L0_attn_Wo)[:, o]),
        slope=g(L0_attn_log_slope), slope_c=halves(np.repeat(g(L0_attn_log_slope), DH)),
        w_r=halves(g(L0_ffn_Wg)[o]),
        small=np.stack([np.tile(g(L0_ffn_bg), (NC_, 1)), arrays.pop("code"), arrays.pop("region")]),
        w1=g(L0_ffn_W1)[:, o].reshape(E, 2, HD, F).transpose(0, 2, 1, 3), b1=g(L0_ffn_b1),
        w2=g(L0_ffn_W2)[:, :, o].reshape(E, FC, 128, D).transpose(2, 0, 1, 3), b2=g(L0_ffn_b2)[:, o])
    nc = bacc.Bacc("TRN2", target_bir_lowering=False, num_devices=1)
    arrays = {f"in_{k}": np.ascontiguousarray(v) for k, v in arrays.items()}
    aps = {k[3:]: nc.dram_tensor(k, v.shape, mybir.dt.from_np(v.dtype), kind="ExternalInput").ap()
           for k, v in arrays.items()}
    out = nc.dram_tensor("out_rows", (B, S, D), mybir.dt.float32, kind="ExternalOutput").ap()
    build(nc, aps, out)
    got = run(nc, [arrays], core_ids=[0]).results[0]["out_rows"]
    return np.ascontiguousarray(got[:, :, np.argsort(o)])
```
